# Optimizing a Trainium2 kernel written in Bass

```python
import numpy as np
import jax
import jax.numpy as jnp

def _softmax(x, axis=-1):
    return jax.nn.softmax(x, axis=axis)

def _gelu(x):
    return jax.nn.gelu(x, approximate=True)

def _silu(x):
    return jax.nn.silu(x)

def _sigmoid(x):
    return jax.nn.sigmoid(x)

def _layernorm(x, axis=-1, eps=1e-05):
    m = jnp.mean(x, axis=axis, keepdims=True)
    v = jnp.var(x, axis=axis, keepdims=True)
    return (x - m) / jnp.sqrt(v + eps)

def _scatter_add(tgt, idx, src, axis=0):
    return tgt.at[idx].add(src)

def _segment_sum(src, seg, n):
    return jax.ops.segment_sum(src, seg, n)
kernel_name = 'mk_gnn_resnorm_d4_gnn_r16_85355c'

def setup_inputs(seed: int=0):
    np.random.seed(seed)
    _w = jnp.asarray

    def _rec_inputs():
        import jax
        import jax.numpy as jnp
        _gk = jax.random.key(seed)
        x = -0.0005121 + 1.001 * jax.random.normal(jax.random.fold_in(_gk, 1), (3125, 64), jnp.float32)
        _s = jax.random.randint(jax.random.fold_in(_gk, 2), (50000,), 0, 3125, jnp.int32)
        _d = jax.random.randint(jax.random.fold_in(_gk, 3), (50000,), 0, 3125, jnp.int32)
        _loop = jnp.arange(3125, dtype=jnp.int32)
        src = jnp.concatenate([_s, _d, _loop])
        dst = jnp.concatenate([_d, _s, _loop])
        _o = jnp.argsort(dst, stable=True)
        src = src[_o]
        dst = dst[_o]
        edge_attr_16 = 0.000196303 + 1.00016 * jax.random.normal(jax.random.fold_in(_gk, 11), (103125, 16), jnp.float32)
        edge_attr_64 = 1.36993e-05 + 0.999972 * jax.random.normal(jax.random.fold_in(_gk, 12), (103125, 64), jnp.float32)
        edge_attr_9 = 0.000739051 + 0.999958 * jax.random.normal(jax.random.fold_in(_gk, 13), (103125, 9), jnp.float32)
        return (x, src, dst, edge_attr_16, edge_attr_64, edge_attr_9)
    x, src, dst, edge_attr_16, edge_attr_64, edge_attr_9 = _rec_inputs()

    def _L0_gnn_setup():
        import jax, jax.numpy as jnp
        import numpy as np
        N = 3125
        E = 50000
        IN_NF = 64
        HID = 128
        OUT_NF = 64
        L = 4
        EH = HID // 2
        C = 1.0

        def _w(k, shape):
            return jax.random.normal(k, shape, dtype=jnp.float32) / np.sqrt(shape[-2]).astype(np.float32)
        key = jax.random.key(seed)
        ks = jax.random.split(key, 10)
        h = jax.random.normal(ks[0], (N, IN_NF), dtype=jnp.float32)
        edges = jax.random.randint(ks[1], (2, E), 0, N, dtype=jnp.int32)
        return {'h': h, 'edges': edges, 'W_in': _w(ks[2], (IN_NF, HID)), 'b_in': jnp.zeros((HID,), jnp.float32), 'eW1': _w(ks[3], (L, 2 * HID, EH)), 'eb1': jnp.zeros((L, EH), jnp.float32), 'eW2': _w(ks[4], (L, EH, EH)), 'eb2': jnp.zeros((L, EH), jnp.float32), 'nW1': _w(ks[5], (L, HID + EH, HID)), 'nb1': jnp.zeros((L, HID), jnp.float32), 'nW2': _w(ks[6], (L, HID, HID)), 'nb2': jnp.zeros((L, HID), jnp.float32), 'W_out': _w(ks[7], (HID, OUT_NF)), 'b_out': jnp.zeros((OUT_NF,), jnp.float32)}
    _L0_gnn_all = _L0_gnn_setup()
    _L0_gnn_in = {k: v for k, v in _L0_gnn_all.items() if k in ('W_in', 'b_in', 'eW1', 'eb1', 'eW2', 'eb2', 'nW1', 'nb1', 'nW2', 'nb2', 'W_out', 'b_out')}
    del _L0_gnn_all

    def _L1_gnn_setup():
        import jax, jax.numpy as jnp
        import numpy as np
        N, E = (625, 20000)
        D, S, HE = (64, 9, 64)
        H, DQK, DV = (8, 16, 16)
        OK, OV = (H * DQK, H * DV)
        EPS_BN = 1e-05

        def tensor_product(x_e, sh, w, C):
            acc = sh[:, 0:1] * (x_e @ C[:, 0, :])
            for s in range(1, S):
                acc = acc + sh[:, s:s + 1] * (x_e @ C[:, s, :])
            return acc * w

        def mlp2(x, w1, b1, w2, b2):
            return jax.nn.relu(x @ w1 + b1) @ w2 + b2
        key = jax.random.key(seed)
        ks = jax.random.split(key, 20)
        g = lambda k, shape, fan: jax.random.normal(k, shape, jnp.float32) / np.float32(np.sqrt(fan))
        return {'tfn_features': jax.random.normal(ks[0], (N, D), jnp.float32), 'edge_features': jax.random.normal(ks[1], (E, HE), jnp.float32), 'edge_sh': jax.random.normal(ks[2], (E, S), jnp.float32), 'Wq': g(ks[3], (D, OK), D), 'Cqk': g(ks[4], (D, S, OK), D * S), 'Cv': g(ks[5], (D, S, OV), D * S), 'k_w1': g(ks[6], (HE, HE), HE), 'k_b1': jnp.zeros((HE,), jnp.float32), 'k_w2': g(ks[7], (HE, OK), HE), 'k_b2': jnp.zeros((OK,), jnp.float32), 'v_w1': g(ks[8], (HE, HE), HE), 'v_b1': jnp.zeros((HE,), jnp.float32), 'v_w2': g(ks[9], (HE, OV), HE), 'v_b2': jnp.zeros((OV,), jnp.float32), 'W_out': g(ks[10], (OV, D), OV), 'W_self': g(ks[11], (D, D), D), 'gamma': jnp.ones((D,), jnp.float32), 'beta': jnp.zeros((D,), jnp.float32), 'edge_index': jax.random.randint(ks[12], (2, E), 0, N, dtype=jnp.int32)}
    _L1_gnn_all = _L1_gnn_setup()
    _L1_gnn_in = {k: v for k, v in _L1_gnn_all.items() if k in ('Wq', 'Cqk', 'Cv', 'k_w1', 'k_b1', 'k_w2', 'k_b2', 'v_w1', 'v_b1', 'v_w2', 'v_b2', 'W_out', 'W_self', 'gamma', 'beta')}
    del _L1_gnn_all

    def _L2_gnn_setup():
        import jax, jax.numpy as jnp
        import numpy as np
        N_NODES = 6250
        N_EDGES = 100000
        HIDDEN = 64
        EDGE_DIM = 16
        key = jax.random.key(seed)
        ks = jax.random.split(key, 9)
        x = jax.random.normal(ks[0], (N_NODES, HIDDEN), dtype=jnp.float32)
        edge_index = jax.random.randint(ks[1], (2, N_EDGES), 0, N_NODES, dtype=jnp.int32)
        edge_attr = jax.random.normal(ks[2], (N_EDGES, EDGE_DIM), dtype=jnp.float32)
        s1 = 1.0 / np.sqrt(HIDDEN * 2 + EDGE_DIM)
        s2 = 1.0 / np.sqrt(HIDDEN)
        s3 = 1.0 / np.sqrt(HIDDEN * 2)
        W1 = jax.random.uniform(ks[3], (HIDDEN * 2 + EDGE_DIM, HIDDEN), jnp.float32, -s1, s1)
        b1 = jax.random.uniform(ks[4], (HIDDEN,), jnp.float32, -s1, s1)
        W2 = jax.random.uniform(ks[5], (HIDDEN, HIDDEN), jnp.float32, -s2, s2)
        b2 = jax.random.uniform(ks[6], (HIDDEN,), jnp.float32, -s2, s2)
        W3 = jax.random.uniform(ks[7], (HIDDEN * 2, HIDDEN), jnp.float32, -s3, s3)
        b3 = jax.random.uniform(ks[8], (HIDDEN,), jnp.float32, -s3, s3)
        return {'x': x, 'edge_index': edge_index, 'edge_attr': edge_attr, 'W1': W1, 'b1': b1, 'W2': W2, 'b2': b2, 'W3': W3, 'b3': b3}
    _L2_gnn_all = _L2_gnn_setup()
    _L2_gnn_in = {k: v for k, v in _L2_gnn_all.items() if k in ('W1', 'b1', 'W2', 'b2', 'W3', 'b3')}
    del _L2_gnn_all

    def _L3_gnn_setup():
        import jax, jax.numpy as jnp
        import numpy as np
        N_NODES = 6250
        N_EDGES = 100000
        D_FEAT = 64
        key = jax.random.key(seed)
        k1, k2 = jax.random.split(key)
        x = jax.random.normal(k1, (N_NODES, D_FEAT), dtype=jnp.float32)
        edge_index = jax.random.randint(k2, (2, N_EDGES), 0, N_NODES, dtype=jnp.int64)
        return {'x': x, 'edge_index': edge_index}
    _L3_gnn_all = _L3_gnn_setup()
    _L3_gnn_in = {k: v for k, v in _L3_gnn_all.items() if k in ()}
    del _L3_gnn_all
    return {'x': x, 'src': src, 'dst': dst, 'edge_attr_16': edge_attr_16, 'edge_attr_64': edge_attr_64, 'edge_attr_9': edge_attr_9, 'L0_gnn_W_in': _L0_gnn_in['W_in'], 'L0_gnn_b_in': _L0_gnn_in['b_in'], 'L0_gnn_eW1': _L0_gnn_in['eW1'], 'L0_gnn_eb1': _L0_gnn_in['eb1'], 'L0_gnn_eW2': _L0_gnn_in['eW2'], 'L0_gnn_eb2': _L0_gnn_in['eb2'], 'L0_gnn_nW1': _L0_gnn_in['nW1'], 'L0_gnn_nb1': _L0_gnn_in['nb1'], 'L0_gnn_nW2': _L0_gnn_in['nW2'], 'L0_gnn_nb2': _L0_gnn_in['nb2'], 'L0_gnn_W_out': _L0_gnn_in['W_out'], 'L0_gnn_b_out': _L0_gnn_in['b_out'], 'L1_gnn_Wq': _L1_gnn_in['Wq'], 'L1_gnn_Cqk': _L1_gnn_in['Cqk'], 'L1_gnn_Cv': _L1_gnn_in['Cv'], 'L1_gnn_k_w1': _L1_gnn_in['k_w1'], 'L1_gnn_k_b1': _L1_gnn_in['k_b1'], 'L1_gnn_k_w2': _L1_gnn_in['k_w2'], 'L1_gnn_k_b2': _L1_gnn_in['k_b2'], 'L1_gnn_v_w1': _L1_gnn_in['v_w1'], 'L1_gnn_v_b1': _L1_gnn_in['v_b1'], 'L1_gnn_v_w2': _L1_gnn_in['v_w2'], 'L1_gnn_v_b2': _L1_gnn_in['v_b2'], 'L1_gnn_W_out': _L1_gnn_in['W_out'], 'L1_gnn_W_self': _L1_gnn_in['W_self'], 'L1_gnn_gamma': _L1_gnn_in['gamma'], 'L1_gnn_beta': _L1_gnn_in['beta'], 'L2_gnn_W1': _L2_gnn_in['W1'], 'L2_gnn_b1': _L2_gnn_in['b1'], 'L2_gnn_W2': _L2_gnn_in['W2'], 'L2_gnn_b2': _L2_gnn_in['b2'], 'L2_gnn_W3': _L2_gnn_in['W3'], 'L2_gnn_b3': _L2_gnn_in['b3']}

def reference(x, src, dst, edge_attr_16, edge_attr_64, edge_attr_9, L0_gnn_W_in, L0_gnn_b_in, L0_gnn_eW1, L0_gnn_eb1, L0_gnn_eW2, L0_gnn_eb2, L0_gnn_nW1, L0_gnn_nb1, L0_gnn_nW2, L0_gnn_nb2, L0_gnn_W_out, L0_gnn_b_out, L1_gnn_Wq, L1_gnn_Cqk, L1_gnn_Cv, L1_gnn_k_w1, L1_gnn_k_b1, L1_gnn_k_w2, L1_gnn_k_b2, L1_gnn_v_w1, L1_gnn_v_b1, L1_gnn_v_w2, L1_gnn_v_b2, L1_gnn_W_out, L1_gnn_W_self, L1_gnn_gamma, L1_gnn_beta, L2_gnn_W1, L2_gnn_b1, L2_gnn_W2, L2_gnn_b2, L2_gnn_W3, L2_gnn_b3):
    import jax
    import jax.numpy as jnp

    def _L0_gnn_ref(h, edges, W_in, b_in, eW1, eb1, eW2, eb2, nW1, nb1, nW2, nb2, W_out, b_out):
        import jax, jax.numpy as jnp
        import numpy as np
        N = 3125
        E = 50000
        IN_NF = 64
        HID = 128
        OUT_NF = 64
        L = 4
        EH = HID // 2
        C = 1.0

        def _w(k, shape):
            return jax.random.normal(k, shape, dtype=jnp.float32) / np.sqrt(shape[-2]).astype(np.float32)
        row, col = (edges[0], edges[1])
        h = h @ W_in + b_in

        def layer(hc, p):
            w1, b1, w2, b2, m1, c1, m2, c2 = p
            m = jnp.concatenate([hc[row], hc[col]], axis=1)
            m = jax.nn.silu(m @ w1 + b1)
            m = jax.nn.silu(m @ w2 + b2)
            agg = jax.ops.segment_sum(m, row, num_segments=N) * C
            z = jnp.concatenate([hc, agg], axis=1)
            z = jax.nn.silu(z @ m1 + c1)
            z = z @ m2 + c2
            return (hc + z, None)
        h, _ = jax.lax.scan(layer, h, (eW1, eb1, eW2, eb2, nW1, nb1, nW2, nb2))
        return h @ W_out + b_out

    def _L1_gnn_ref(tfn_features, edge_features, edge_sh, Wq, Cqk, Cv, k_w1, k_b1, k_w2, k_b2, v_w1, v_b1, v_w2, v_b2, W_out, W_self, gamma, beta, edge_index):
        import jax, jax.numpy as jnp
        import numpy as np
        N, E = (625, 20000)
        D, S, HE = (64, 9, 64)
        H, DQK, DV = (8, 16, 16)
        OK, OV = (H * DQK, H * DV)
        EPS_BN = 1e-05

        def tensor_product(x_e, sh, w, C):
            acc = sh[:, 0:1] * (x_e @ C[:, 0, :])
            for s in range(1, S):
                acc = acc + sh[:, s:s + 1] * (x_e @ C[:, s, :])
            return acc * w

        def mlp2(x, w1, b1, w2, b2):
            return jax.nn.relu(x @ w1 + b1) @ w2 + b2
        edge_dst, edge_src = (edge_index[0], edge_index[1])
        n = tfn_features.shape[0]
        q = (tfn_features @ Wq).reshape(n, H, DQK)
        x_dst = tfn_features[edge_dst]
        wk = mlp2(edge_features, k_w1, k_b1, k_w2, k_b2)
        wv = mlp2(edge_features, v_w1, v_b1, v_w2, v_b2)
        k = tensor_product(x_dst, edge_sh, wk, Cqk).reshape(-1, H, DQK)
        v = tensor_product(x_dst, edge_sh, wv, Cv).reshape(-1, H, DV)
        attn = jnp.einsum('ehd,ehd->eh', q[edge_src], k)
        amax = jax.ops.segment_max(attn, edge_src, num_segments=n)
        ex = jnp.exp(attn - amax[edge_src])
        denom = jax.ops.segment_sum(ex, edge_src, num_segments=n)
        alpha = ex / (denom[edge_src] + 1e-16)
        upd = jax.ops.segment_sum(v * alpha[..., None], edge_src, num_segments=n)
        upd = upd.reshape(n, OV) @ W_out
        out = tfn_features @ W_self + upd
        mu = out.mean(axis=0)
        var = out.var(axis=0)
        return (out - mu) * jax.lax.rsqrt(var + EPS_BN) * gamma + beta

    def _L2_gnn_ref(x, edge_index, edge_attr, W1, b1, W2, b2, W3, b3):
        import jax, jax.numpy as jnp
        import numpy as np
        N_NODES = 6250
        N_EDGES = 100000
        HIDDEN = 64
        EDGE_DIM = 16
        src, dst = (edge_index[0], edge_index[1])
        m_in = jnp.concatenate([x[src], x[dst], edge_attr], axis=-1)
        h = jax.nn.silu(m_in @ W1 + b1)
        messages = jax.nn.silu(h @ W2 + b2)
        agg = jax.ops.segment_sum(messages, dst, num_segments=x.shape[0])
        node_in = jnp.concatenate([x, agg], axis=-1)
        return jax.nn.silu(node_in @ W3 + b3)

    def _L3_gnn_ref(x, edge_index):
        import jax, jax.numpy as jnp
        import numpy as np
        N_NODES = 6250
        N_EDGES = 100000
        D_FEAT = 64
        from_, to_ = (edge_index[0], edge_index[1])
        n = x.shape[0]
        deg = jax.ops.segment_sum(jnp.ones_like(to_, dtype=x.dtype), to_, num_segments=n)
        deg_inv = jnp.where(deg > 0, 1.0 / jnp.sqrt(deg), 0.0)
        norm = deg_inv[from_] * deg_inv[to_]
        m_j = norm[:, None] * x[from_]
        out = jax.ops.segment_sum(m_j, to_, num_segments=n)
        return out
    edge_index = jnp.stack([src, dst])
    x = _layernorm(x + _L0_gnn_ref(x, edge_index, L0_gnn_W_in, L0_gnn_b_in, L0_gnn_eW1, L0_gnn_eb1, L0_gnn_eW2, L0_gnn_eb2, L0_gnn_nW1, L0_gnn_nb1, L0_gnn_nW2, L0_gnn_nb2, L0_gnn_W_out, L0_gnn_b_out), axis=-1)
    x = _layernorm(x + _L1_gnn_ref(x, edge_attr_64, edge_attr_9, L1_gnn_Wq, L1_gnn_Cqk, L1_gnn_Cv, L1_gnn_k_w1, L1_gnn_k_b1, L1_gnn_k_w2, L1_gnn_k_b2, L1_gnn_v_w1, L1_gnn_v_b1, L1_gnn_v_w2, L1_gnn_v_b2, L1_gnn_W_out, L1_gnn_W_self, L1_gnn_gamma, L1_gnn_beta, edge_index), axis=-1)
    x = _layernorm(x + _L2_gnn_ref(x, edge_index, edge_attr_16, L2_gnn_W1, L2_gnn_b1, L2_gnn_W2, L2_gnn_b2, L2_gnn_W3, L2_gnn_b3), axis=-1)
    x = _layernorm(x + _L3_gnn_ref(x, edge_index), axis=-1)
    return x

_drawn_inputs = setup_inputs


def setup_inputs(seed=0):
    import zlib

    import numpy as np

    out = dict(_drawn_inputs(seed))
    spreads = {'L0_gnn_b_in': (0.0, 0.1),
     'L0_gnn_eb1': (0.0, 0.1),
     'L0_gnn_eb2': (0.0, 0.1),
     'L0_gnn_nb1': (0.0, 0.499),
     'L0_gnn_nb2': (0.0, 0.368),
     'L0_gnn_b_out': (0.0, 0.8),
     'L1_gnn_k_b1': (0.0, 0.1),
     'L1_gnn_k_b2': (0.0, 0.1),
     'L1_gnn_v_b1': (0.0, 0.1),
     'L1_gnn_v_b2': (0.0, 0.1),
     'L1_gnn_gamma': (1.0, 0.2),
     'L1_gnn_beta': (0.0, 0.1)}
    factors = {}
    for name, (base, spread) in spreads.items():
        noise = np.random.default_rng([zlib.crc32(name.encode()), seed]).standard_normal(out[name].shape)
        drawn = base * np.exp(spread * noise) if base else spread * noise
        out[name] = jnp.asarray(drawn.astype(out[name].dtype))
    for name, factor in factors.items():
        out[name] = (out[name] * factor).astype(out[name].dtype)
    return out
```

```python
from contextlib import ExitStack

import concourse.bass as bass
from concourse import mybir

ALU = mybir.AluOpType
ACT = mybir.ActivationFunctionType
AX = mybir.AxisListType
F32 = mybir.dt.float32
BF16 = mybir.dt.bfloat16
I32 = mybir.dt.int32

P = 128
N = 3125
NE = 103125
NB = -(-N // P)
NPAD = NB * P
GT = 4
GE = GT * P
G = (NE + NB * (GE - 1)) // GE
G += G % 2
T = G * GT
SLOTS = T * P
EC = -(-NE // P)
ETAIL = NE - (P - 1) * EC
SC = 13
assert EC % SC == 0
D = 64
HID = 128
LAYERS = 4
CH = 5
CHN = CH * P
HALF = CHN // 2
BIG = 1.0e30
REC = 4
NOKEY = 255


class Engines:

    def __init__(self, nc, ctx):
        self.nc, self.ctx = nc, ctx
        self.eng = {"pe": nc.tensor, "dve": nc.vector, "act": nc.scalar, "pool": nc.gpsimd, "sp": nc.sync}
        self.sem, self.count = {}, {}
        for n in ("pe", "dve", "act", "pool"):
            self.semaphore(n)

    def semaphore(self, name):
        if name not in self.sem:
            self.sem[name] = self.ctx.enter_context(self.nc.semaphore("s_" + name))
            self.count[name] = 0
        return self.sem[name]


class Phase:

    def __init__(self, n, unroll=1, lead=None):
        self.n, self.unroll, self.steps, self.lead = n, unroll, [], lead

    def step(self, eng, name, waits, fn, stage=0, dma=0, apart=False):
        self.steps.append((eng, name, waits.split(), fn, stage, dma, apart))

    def counts(self):
        turns = self.n + max(s[4] for s in self.steps)
        out = {}
        for eng, name, _, _, _, dma, _ in self.steps:
            if dma:
                for j in range(self.unroll):
                    key = f"{name}_{j}" if self.unroll > 1 else name
                    out[key] = out.get(key, 0) + 16 * dma * len(range(j, self.n, self.unroll))
            else:
                out[eng] = out.get(eng, 0) + turns
        return out

    def emit(self, E, base):
        nc, U = E.nc, self.unroll
        depth = max(s[4] for s in self.steps)
        lags = [int(w.split("@")[1]) for s in self.steps for w in s[2] if "@" in w]
        where, per = {}, {}
        for eng, name, _, _, stage, dma, _ in self.steps:
            if not dma:
                per[eng] = per.get(eng, 0) + 1
            where[name] = (eng, per.get(eng), stage, dma)
        for key in self.counts():
            E.semaphore(key)

        def turn(t, j0, static):
            for eng, name, waits, fn, stage, dma, apart in self.steps:
                e = E.eng[eng]
                if static and not 0 <= t - stage < self.n:
                    if not dma:
                        e.nop(nofuse=True)
                        e.drain().then_inc(E.sem[eng], 1)
                    continue
                need = {}
                for w in waits:
                    src, lag = (w.split("@") + ["0"])[:2]
                    weng, k, wstage, wdma = where[src]
                    lag = int(lag)
                    if static and t - stage - lag < 0:
                        continue
                    back = stage + lag
                    if wdma:
                        jj = (j0 - back) % U
                        key = f"{src}_{jj}" if U > 1 else src
                        if static:
                            val = (t - back) // U + 1
                        else:
                            val = t[0] + (j0 - back) // U + 1
                        need[key] = (wdma, val)
                    else:
                        d = k - (back - wstage) * per[weng]
                        if weng not in need or need[weng] < d:
                            need[weng] = d
                for key, v in need.items():
                    if key in per:
                        tt = t if static else (t[0] * U + j0)
                        e.wait_ge(E.sem[key], base[key] + tt * per[key] + v)
                        if eng == "sp":
                            e.nop(nofuse=True)
                    else:
                        e.wait_ge(E.sem[key], base[key] + v[1] * (16 * v[0]))
                        if eng == "sp":
                            e.nop(nofuse=True)
                if apart and need:
                    e.nop(nofuse=True)
                jb = (j0 - stage) % U
                i = (t - stage) if static else (t[0] * U + (j0 - stage))
                if dma:
                    key = f"{name}_{jb}" if U > 1 else name
                    sem = E.sem[key]
                    for ins in fn(i, jb):
                        ins.then_inc(sem, 16)
                else:
                    fn(i, jb).then_inc(E.sem[eng], 1)

        turns = self.n + depth
        lead = max([depth] + [g + depth for g in lags]) if self.lead is None else self.lead
        lead = -(-lead // U) * U
        loops = max(0, (self.n - lead) // U)
        if loops < 2:
            lead, loops = turns, 0
        for t in range(min(lead, turns)):
            turn(t, t % U, True)
        if loops:
            used = [e.engine for e in (E.eng[n] for n in dict.fromkeys(s[0] for s in self.steps))]
            with nc.Fori(lead // U, lead // U + loops, engines=tuple(used)) as r:
                for j in range(U):
                    turn((r,), j, False)
            for t in range(lead + loops * U, turns):
                turn(t, t % U, True)


def finish(E, phase, base):
    for key, n in phase.counts().items():
        base[key] = base[key] + n
    for eng, e in E.eng.items():
        for key in phase.counts():
            e.wait_ge(E.sem[key], base[key])
            if eng == "sp":
                e.nop(nofuse=True)


def run(E, phase):
    for key in phase.counts():
        E.semaphore(key)
    phase.emit(E, E.count)
    finish(E, phase, E.count)


def run_layers(E, phases, n):
    total = {}
    for ph in phases:
        for key, c in ph.counts().items():
            E.semaphore(key)
            total[key] = total.get(key, 0) + c
    with E.nc.Fori(0, n) as layer:
        for ph in phases:
            ph.layer = layer
        base = {k: E.count[k] + layer * total[k] if k in total else v for k, v in E.count.items()}
        for ph in phases:
            ph.emit(E, base)
            finish(E, ph, base)
    for k, c in total.items():
        E.count[k] += n * c



def build(nc, x_in, src_in, dst_in, ea16, ea64, ea9, L0_W_in, L0_b_in, L0_eW1, L0_eb1, L0_eW2, L0_eb2, L0_nW1,
          L0_nb1, L0_nW2, L0_nb2, L0_W_out, L0_b_out, L1_Wq, L1_Cqk, L1_Cv, L1_k_w1, L1_k_b1, L1_k_w2, L1_k_b2,
          L1_v_w1, L1_v_b1, L1_v_w2, L1_v_b2, L1_W_out, L1_W_self, L1_gamma, L1_beta, L2_W1, L2_b1, L2_W2, L2_b2,
          L2_W3, L2_b3, out, dbg=None):
    with ExitStack() as ctx:
        E = Engines(nc, ctx)

        def sb(name, shape, dt=F32):
            return ctx.enter_context(nc.sbuf_tensor(name, shape, dt))

        def dram(name, shape, dt=F32):
            return nc.dram_tensor(name, shape, dt, kind="Internal").ap()

        PS = ctx.enter_context(nc.psum_tensor("psum", [P, 8 * 512], F32))
        bank = [PS[:, b * 512:(b + 1) * 512] for b in range(8)]
        pe, dve, act, pool, sp = nc.tensor, nc.vector, nc.scalar, nc.gpsimd, nc.sync

        def rows(ap):
            return ap.partition_broadcast(P)

        def col(ap):
            return ap.rearrange("(p a) -> p a", a=1)

        ident = sb("ident", [P, P])
        lane = sb("lane", [P, 1])
        node_iota = sb("node_iota", [P, P])
        ones = sb("ones", [P, P])
        before = sb("before", [P, P])
        real = sb("real", [P, 1])
        c = Phase(1)
        c.step("pool", "iota_n", "", lambda i, j: pool.iota(node_iota[:], [[1, P]], base=0, channel_multiplier=0,
                                                            allow_small_or_imprecise_dtypes=True))
        c.step("pool", "iota_p", "", lambda i, j: pool.iota(lane[:], [[0, 1]], base=0, channel_multiplier=1,
                                                            allow_small_or_imprecise_dtypes=True))
        c.step("dve", "ones", "", lambda i, j: dve.memset(ones[:], 1.0))
        c.step("dve", "ident", "iota_n iota_p", lambda i, j: dve.tensor_scalar(ident[:], node_iota[:], lane[:, 0:1], None, ALU.is_equal))
        c.step("dve", "before", "", lambda i, j: dve.tensor_scalar(before[:], node_iota[:], lane[:, 0:1], None, ALU.is_gt))
        c.step("dve", "real", "", lambda i, j: dve.tensor_scalar(real[:], lane[:], float(N - (NB - 1) * P), None, ALU.is_lt))
        run(E, c)

        tables = {}
        for order in "sd":
            tables[order] = dict(
                slots=dram(f"slots_{order}", [SLOTS, REC], I32),
                keyrow=dram(f"keyrow_{order}", [T * P], BF16),
                gidx=sb(f"gidx_{order}", [P, T], I32),
                key=sb(f"key_{order}", [P, T]),
                blk=sb(f"blk_{order}", [1, 2 * P], I32))
        eid = sb("eid", [P, T], I32)

        with ExitStack() as pre:
            def tmp(name, shape, dt=F32):
                return pre.enter_context(nc.sbuf_tensor(name, shape, dt))

            src = tmp("src", [P, EC], I32)
            dst = tmp("dst", [P, EC], I32)
            bucket = tmp("bucket", [P, EC])
            member = tmp("member", [P, EC])
            onesw = tmp("onesw", [P, EC])
            rank = tmp("rank", [P, EC])
            pos = tmp("pos", [P, EC])
            ibuf = tmp("ibuf", [P, EC], I32)
            row = tmp("row", [P, EC], I32)
            rec = tmp("rec", [P, T, REC], I32)
            cnt = tmp("cnt", [P, NB])
            first = tmp("first", [P, NB])
            itot = tmp("itot", [P, NB], I32)
            ngr = tmp("ngr", [P, NB])
            gend = tmp("gend", [P, NB])
            hit = tmp("hit", [P, 2, NB])
            gb = tmp("gb", [P, 2])
            gcol = tmp("gcol", [P, 2])
            sidx = [tmp(f"sidx{j}", [P, SC], I32) for j in range(2)]
            srec = [tmp(f"srec{j}", [P, SC * REC], I32) for j in range(2)]
            keyt = tmp("keyt", [P, P], BF16)

            ld = Phase(1)
            for t_, in_ in ((src, src_in), (dst, dst_in)):
                def load(i, j, t_=t_, in_=in_):
                    yield sp.dma_start(t_[0:P - 1, :], in_[0:(P - 1) * EC].rearrange("(p c) -> p c", c=EC))
                    yield sp.dma_start(t_[P - 1:P, 0:ETAIL], in_[(P - 1) * EC:NE].rearrange("(a c) -> a c", a=1))
                ld.step("dve", f"empty_{t_.name}", "", lambda i, j, t_=t_: dve.memset(t_[:], NB * P))
                ld.step("sp", f"load_{t_.name}", f"empty_{t_.name}", load, dma=2)
            ld.step("dve", "onesw", "", lambda i, j: dve.memset(onesw[:], 1.0))
            run(E, ld)

            for order, key, other in (("s", src, dst), ("d", dst, src)):
                tb = tables[order]
                a = Phase(1)
                a.step("dve", "empty", "", lambda i, j: dve.memset(rec[:], 0))
                a.step("dve", "nokey", "empty", lambda i, j: dve.memset(rec[:, :, 1], NOKEY))
                a.step("sp", "fill", "nokey", lambda i, j: [sp.dma_start(
                    tb["slots"].rearrange("(p t) r -> p (t r)", p=P), rec[:, :, :].rearrange("p t r -> p (t r)"))], dma=1)
                a.step("dve", "shift", "", lambda i, j: dve.tensor_scalar(ibuf[:], key[:], 7, None, ALU.logical_shift_right))
                a.step("dve", "bucket", "shift", lambda i, j: dve.tensor_copy(bucket[:], ibuf[:]))
                a.step("dve", "r_other", "fill", lambda i, j: dve.tensor_copy(rec[:, 0:EC, 0], other[:]))
                a.step("dve", "r_key", "fill", lambda i, j: dve.tensor_scalar(rec[:, 0:EC, 1], key[:], P - 1, None, ALU.bitwise_and))
                a.step("pool", "r_eid", "fill", lambda i, j: pool.iota(rec[:, 0:EC, 2], [[1, EC]], base=0, channel_multiplier=EC))
                a.step("pool", "r_eid2", "", lambda i, j: pool.iota(rec[:, 0:EC, 3], [[1, EC]], base=0, channel_multiplier=EC))
                a.step("dve", "pos0", "", lambda i, j: dve.memset(pos[:], 0.0))
                run(E, a)
                b = Phase(NB)
                b.step("dve", "member", "sum@1", lambda i, j: dve.tensor_scalar(
                    member[:], bucket[:], node_iota[:, bass.ds(i, 1)], None, ALU.is_equal))
                b.step("dve", "sum", "member", lambda i, j: dve.tensor_reduce(
                    cnt[:, bass.ds(i, 1)], member[:], AX.X, ALU.add))
                run(E, b)
                m = Phase(1)
                m.step("pe", "total", "", lambda i, j: pe.matmul(bank[0][:, 0:NB], ones[:], cnt[:], start=True, stop=True))
                m.step("pe", "below", "", lambda i, j: pe.matmul(bank[1][:, 0:NB], before[:], cnt[:], start=True, stop=True))
                m.step("dve", "itot", "total", lambda i, j: dve.tensor_scalar(itot[:], bank[0][:, 0:NB], float(GE - 1), None, ALU.add))
                m.step("dve", "igr", "itot", lambda i, j: dve.tensor_scalar(itot[:], itot[:], 9, None, ALU.logical_shift_right))
                m.step("dve", "ngr", "igr", lambda i, j: dve.tensor_copy(ngr[:], itot[:]))
                m.step("dve", "gend", "ngr", lambda i, j: dve.tensor_tensor_scan(gend[:], ones[:, 0:NB], ngr[:], 0.0, ALU.mult, ALU.add))
                m.step("dve", "gbeg", "gend", lambda i, j: dve.tensor_tensor(first[:], gend[:], ngr[:], ALU.subtract))
                m.step("dve", "gslot", "gbeg", lambda i, j: dve.tensor_scalar(first[:], first[:], float(GE), -1.0, ALU.mult, ALU.add))
                m.step("dve", "first", "gslot below", lambda i, j: dve.tensor_tensor(first[:], first[:], bank[1][:, 0:NB], ALU.add))
                m.step("pool", "gcol", "", lambda i, j: pool.iota(gcol[:], [[P, 2]], base=0, channel_multiplier=1,
                                                                  allow_small_or_imprecise_dtypes=True))
                for h in range(2):
                    m.step("dve", f"hit{h}", "gend gcol", lambda i, j, h=h: dve.tensor_scalar(
                        hit[:, h, :], gend[:], gcol[:, h:h + 1], None, ALU.is_le))
                m.step("dve", "gb", "hit1", lambda i, j: dve.tensor_reduce(gb[:], hit[:, :, 0:NB - 1], AX.X, ALU.add))
                for h in range(2):
                    m.step("pe", f"gbrow{h}", "gb", lambda i, j, h=h: pe.matmul(
                        bank[2][0:1, h * P:(h + 1) * P], gb[:, h:h + 1], ident[:], start=True, stop=True))
                m.step("dve", "blk", "gbrow1", lambda i, j: dve.tensor_copy(tb["blk"][:], bank[2][0:1, 0:2 * P]))
                run(E, m)
                r = Phase(NB)
                r.step("dve", "member", "masked@1", lambda i, j: dve.tensor_scalar(
                    member[:], bucket[:], node_iota[:, bass.ds(i, 1)], None, ALU.is_equal))
                r.step("dve", "scan", "member pos@1", lambda i, j: dve.tensor_tensor_scan(
                    rank[:], onesw[:], member[:], first[:, bass.ds(i, 1)], ALU.mult, ALU.add))
                r.step("dve", "masked", "scan", lambda i, j: dve.tensor_tensor(rank[:], rank[:], member[:], ALU.mult))
                r.step("dve", "pos", "masked", lambda i, j: dve.tensor_tensor(pos[:], pos[:], rank[:], ALU.add))
                run(E, r)
                w = Phase(1)
                w.step("dve", "ipos", "", lambda i, j: dve.tensor_copy(ibuf[:], pos[:]))
                w.step("dve", "ilane", "ipos", lambda i, j: dve.tensor_scalar(row[:], ibuf[:], P - 1, None, ALU.bitwise_and))
                w.step("dve", "itile", "ilane", lambda i, j: dve.tensor_scalar(ibuf[:], ibuf[:], 7, None, ALU.logical_shift_right))
                w.step("dve", "fold", "itile", lambda i, j: dve.scalar_tensor_tensor(
                    rank[:], row[:], float(T), ibuf[:], ALU.mult, ALU.add))
                w.step("dve", "pad", "", lambda i, j: dve.tensor_scalar(
                    member[:], bucket[:], float(NB), float(2 * SLOTS), ALU.is_ge, ALU.mult))
                w.step("dve", "row", "pad fold", lambda i, j: dve.tensor_tensor(row[:], rank[:], member[:], ALU.add))
                run(E, w)

                def scatter(i, j):
                    for c_ in range(SC):
                        yield pool.indirect_dma_start(
                            tb["slots"], bass.IndirectOffsetOnAxis(ap=sidx[j][:, c_:c_ + 1], axis=0),
                            srec[j][:, c_ * REC:(c_ + 1) * REC], None, bounds_check=SLOTS - 1, oob_is_err=False)
                s = Phase(EC // SC, unroll=2)
                s.step("dve", "sidx", "scatter@2", lambda i, j: dve.tensor_copy(sidx[j][:], row[:, bass.ds(i * SC, SC)]))
                s.step("dve", "srec", "scatter@2", lambda i, j: dve.tensor_copy(
                    srec[j][:], rec[:, bass.ds(i * SC, SC), :].rearrange("p t r -> p (t r)")))
                s.step("pool", "ready", "sidx srec", lambda i, j: pool.nop(nofuse=True))
                s.step("pool", "scatter", "", scatter, dma=SC)
                run(E, s)

                g = Phase(1)
                g.step("sp", "table", "", lambda i, j: [sp.dma_start(
                    rec[:, :, :].rearrange("p t r -> p (t r)"), tb["slots"].rearrange("(p t) r -> p (t r)", p=P))], dma=1)
                g.step("dve", "gidx", "table", lambda i, j: dve.tensor_copy(tb["gidx"][:], rec[:, :, 0]))
                g.step("dve", "key", "table", lambda i, j: dve.tensor_copy(tb["key"][:], rec[:, :, 1]))
                if order == "d":
                    g.step("dve", "eid", "table", lambda i, j: dve.tensor_copy(eid[:], rec[:, :, 2]))
                run(E, g)
                k = Phase(-(-T // P), unroll=1)
                for h in range(-(-T // P)):
                    n_ = min(P, T - h * P)
                    q = Phase(1)
                    q.step("pe", "turn", "", lambda i, j: pe.transpose(bank[0][0:n_, 0:P], tb["key"][:, h * P:h * P + n_], ident[:]))
                    q.step("dve", "keyt", "turn", lambda i, j: dve.tensor_copy(keyt[0:n_, :], bank[0][0:n_, 0:P]))
                    q.step("sp", "store", "keyt", lambda i, j: [sp.dma_start(
                        tb["keyrow"][h * P * P:(h * P + n_) * P].rearrange("(t p) -> t p", p=P), keyt[0:n_, :])], dma=1)
                    run(E, q)
        xn = sb("xn", [P, NB, D])
        xT = sb("xT", [D, NPAD])
        aggT = sb("aggT", [D, NPAD])
        xc = sb("xc", [P, CH * D])
        xr = dram("xr", [NPAD, D])
        sq = sb("sq", [P, NB, D])
        stat = sb("stat", [P, NB])
        stat2 = sb("stat2", [P, NB])

        def transpose_nodes(src_t, dst_t):
            t = Phase(NB // CH)
            t.step("dve", "copy", "turn@1", lambda i, j: dve.tensor_copy(
                xc[:], src_t[:, bass.ds(i * CH, CH), :].rearrange("p b f -> p (b f)")))

            def turn(i, j):
                for b in range(CH):
                    ins = pe.transpose(PS[0:D, b * P:(b + 1) * P], xc[:, b * D:(b + 1) * D], ident[:])
                return ins
            t.step("pe", "turn", "copy out@1", turn, apart=True)
            t.step("act", "out", "turn", lambda i, j: act.copy(dst_t[:, bass.ds(i * CHN, CHN)], PS[0:D, 0:CHN]))
            run(E, t)

        def layernorm(t, extra=None):
            mean = stat[:].unsqueeze(2).broadcast_to([P, NB, D])
            inv = stat2[:].unsqueeze(2).broadcast_to([P, NB, D])
            n = Phase(1)
            n.step("dve", "sum", "", lambda i, j: dve.tensor_reduce(stat[:], t[:], AX.X, ALU.add))
            n.step("dve", "mean", "sum", lambda i, j: dve.tensor_scalar(stat[:], stat[:], 1.0 / D, None, ALU.mult))
            n.step("dve", "center", "mean", lambda i, j: dve.tensor_tensor(t[:], t[:], mean, ALU.subtract))
            n.step("dve", "square", "center", lambda i, j: dve.tensor_tensor(sq[:], t[:], t[:], ALU.mult))
            n.step("dve", "sumsq", "square", lambda i, j: dve.tensor_reduce(stat2[:], sq[:], AX.X, ALU.add))
            n.step("dve", "var", "sumsq", lambda i, j: dve.tensor_scalar(stat2[:], stat2[:], 1.0 / D, 1e-5, ALU.mult, ALU.add))
            n.step("act", "sd", "var", lambda i, j: act.activation(stat2[:], stat2[:], ACT.Sqrt))
            n.step("dve", "inv", "sd", lambda i, j: dve.reciprocal(stat2[:], stat2[:]))
            n.step("dve", "scale", "inv", lambda i, j: dve.tensor_tensor(t[:], t[:], inv, ALU.mult))
            n.step("dve", "mask", "scale", lambda i, j: dve.tensor_scalar(
                t[:, NB - 1, :], t[:, NB - 1, :], real[:, 0:1], None, ALU.mult))
            run(E, n)

        def load_nodes(i, j):
            yield sp.dma_start(xn[:, 0:NB - 1, :], x_in[0:(NB - 1) * P, :].rearrange("(b p) f -> p b f", p=P))
            yield sp.dma_start(xn[0:N - (NB - 1) * P, NB - 1, :], x_in[(NB - 1) * P:N, :])
        ld = Phase(1)
        ld.step("dve", "zero", "", lambda i, j: dve.memset(xn[:], 0.0))
        ld.step("sp", "nodes", "zero", load_nodes, dma=2)
        run(E, ld)
        transpose_nodes(xn, xT)

        W = 2 * GT
        kr = [sb(f"kr{j}", [P, W * P], BF16) for j in range(2)]
        gi = [sb(f"gi{j}", [P, W], I32) for j in range(2)]
        gx = [sb(f"gx{j}", [P, W, D]) for j in range(2)]
        oht = sb("oht", [P, W * P])
        oh = sb("oh", [P, W, P])
        msg = sb("msg", [P, W * D])

        def fetch_steps(ph, tb, table, free):
            ph.step("sp", "keys", "oht@2", lambda i, j: [sp.dma_start(
                kr[j][:], tb["keyrow"][bass.ds(i * (W * P), W * P)].partition_broadcast(P))], dma=1)
            ph.step("dve", "gidx", "rows@2", lambda i, j: dve.tensor_copy(gi[j][:], tb["gidx"][:, bass.ds(i * W, W)]))
            ph.step("pool", "go", f"gidx {free}@2", lambda i, j: pool.nop(nofuse=True))
            ph.step("pool", "rows", "", lambda i, j: [pool.indirect_dma_start(
                gx[j][:, c_, :], None, table, bass.IndirectOffsetOnAxis(ap=gi[j][:, c_:c_ + 1], axis=0)) for c_ in range(W)], dma=W)

        def onehot_steps(ph, tb, last_t, last):
            ph.step("dve", "oht", f"keys {last_t}@1", lambda i, j: dve.tensor_scalar(
                oht[:], kr[j][:], lane[:, 0:1], None, ALU.is_equal), stage=1)
            ph.step("dve", "oh", f"{last}@1", lambda i, j: dve.tensor_tensor(
                oh[:], node_iota[:].unsqueeze(1).broadcast_to([P, W, P]),
                tb["key"][:, bass.ds(i * W, W)].unsqueeze(2).broadcast_to([P, W, P]), ALU.is_equal), stage=1)

        def blocks(eng, tb, i):
            return [eng.value_load(tb["blk"][0:1, bass.ds(i * 2 + h, 1)], min_val=0, max_val=NB - 1) for h in range(2)]

        def add_messages(ph, tb, src_bank, waits):
            def add(i, j, h):
                b = dve.value_load(tb["blk"][0:1, bass.ds(i * 2 + h, 1)], min_val=0, max_val=NB - 1)
                a = aggT[:, bass.ds(b * P, P)]
                return dve.tensor_tensor(a, a, bank[src_bank][0:D, h * P:(h + 1) * P], ALU.add)
            ph.step("dve", "add0", waits + " add1@1", lambda i, j: add(i, j, 0), stage=1, apart=True)
            ph.step("dve", "add1", "add0", lambda i, j: add(i, j, 1), stage=1, apart=True)

        tb = tables["s"]
        hT = sb("hT", [HID, NPAD])
        z1T = sb("z1T", [HID, CHN])
        hcur = sb("hcur", [HID, CHN])
        ptab = sb("ptab", [P, NB * D])
        qst = sb("qst", [P, CH, D])
        w_in = sb("w_in", [D, HID])
        b_in = sb("b_in", [HID, 1])
        w_out = sb("w_out", [HID, D])
        b_out = sb("b_out", [P, D])
        w1 = sb("w1", [HID, 2, D])
        b1 = sb("b1", [P, D])
        w2 = sb("w2", [P, P])
        b2 = sb("b2", [1, W * D])
        m1a = sb("m1a", [HID, HID])
        m1b = sb("m1b", [D, HID])
        c1 = sb("c1", [HID, 1])
        m2 = sb("m2", [HID, HID])
        c2 = sb("c2", [HID, 1])
        h1 = sb("h1", [P, W * D])
        pre_s = sb("pre_s", [P, W * D])

        ld = Phase(1)
        ld.step("dve", "zero", "", lambda i, j: dve.memset(w2[:], 0.0))
        ld.step("sp", "win", "", lambda i, j: [sp.dma_start(w_in[:], L0_W_in), sp.dma_start(b_in[:], col(L0_b_in)),
                                               sp.dma_start(w_out[:], L0_W_out), sp.dma_start(b_out[:], rows(L0_b_out))], dma=4)
        run(E, ld)

        def halves(lo):
            return PS[:, lo * 512:(lo + 2) * 512].rearrange("p (k n) -> p k n", k=2)[:, :, 0:HALF]

        ph = Phase(NB // CH)

        def h_in(i, j):
            for k in range(2):
                ins = pe.matmul(bank[k][:, 0:HALF], w_in[:], xT[:, bass.ds(i * CHN + k * HALF, HALF)], start=True, stop=True)
            return ins
        ph.step("pe", "win", "bias@1", h_in)
        ph.step("act", "bias", "win", lambda i, j: act.activation(
            hT[:, bass.ds(i * CHN, CHN)].rearrange("p (k n) -> p k n", k=2), halves(0), ACT.Identity, bias=b_in[:, 0:1]))
        run(E, ph)

        wl = Phase(1)

        def layer_weights(i, j):
            l = wl.layer
            yield sp.dma_start(w1[:], L0_eW1[bass.ds(l, 1), :, :].rearrange("a (k p) f -> p (a k) f", p=P))
            yield sp.dma_start(b1[:], L0_eb1[bass.ds(l, 1), :].rearrange("a f -> (a f)").partition_broadcast(P))
            for k in range(2):
                yield sp.dma_start(w2[k * D:(k + 1) * D, k * D:(k + 1) * D], L0_eW2[bass.ds(l, 1), :, :].rearrange("a p f -> p (a f)"))
            yield sp.dma_start(b2[:].rearrange("a (t f) -> a t f", f=D),
                               L0_eb2[bass.ds(l, 1), :].unsqueeze(1).broadcast_to([1, W, D]))
            yield sp.dma_start(m1a[:], L0_nW1[bass.ds(l, 1), 0:HID, :].rearrange("a p f -> p (a f)"))
            yield sp.dma_start(m1b[:], L0_nW1[bass.ds(l, 1), HID:HID + D, :].rearrange("a p f -> p (a f)"))
            yield sp.dma_start(c1[:], L0_nb1[bass.ds(l, 1), :].rearrange("a (p f) -> p (a f)", f=1))
            yield sp.dma_start(m2[:], L0_nW2[bass.ds(l, 1), :, :].rearrange("a p f -> p (a f)"))
            yield sp.dma_start(c2[:], L0_nb2[bass.ds(l, 1), :].rearrange("a (p f) -> p (a f)", f=1))
        wl.step("sp", "weights", "", layer_weights, dma=10)
        wl.step("dve", "zero", "", lambda i, j: dve.memset(aggT[:], 0.0))

        nt = Phase(NB // CH)
        nt.step("dve", "hcur", "prod@1", lambda i, j: dve.tensor_copy(hcur[:], hT[:, bass.ds(i * CHN, CHN)]))

        def prod(i, j):
            for b in range(CH):
                ins = pe.matmul(PS[:, b * P:(b + 1) * P], hcur[:, b * P:(b + 1) * P], w1[:].rearrange("p k f -> p (k f)"),
                                start=True, stop=True)
            return ins
        nt.step("pe", "prod", "hcur qst@1 ptab@1", prod)
        prod_out = PS[:, 0:CHN].rearrange("p (b k f) -> p b k f", b=CH, k=2)
        nt.step("dve", "ptab", "prod", lambda i, j: dve.tensor_tensor(
            ptab[:, bass.ds(i * CH * D, CH * D)].rearrange("p (b f) -> p b f", f=D), prod_out[:, :, 0, :],
            b1[:].unsqueeze(1).broadcast_to([P, CH, D]), ALU.add))
        nt.step("act", "qst", "ptab store@1", lambda i, j: act.copy(qst[:], prod_out[:, :, 1, :]))
        nt.step("sp", "store", "qst", lambda i, j: [sp.dma_start(
            xr[bass.ds(i * CHN, CHN), :].rearrange("(b p) f -> p b f", p=P), qst[:])], dma=1)

        def gather_local(tb, table, width, dst):
            def f(i, j):
                bl = blocks(pe, tb, i)
                for t in range(W):
                    ins = pe.matmul(dst[:, t * width:(t + 1) * width], oht[:, t * P:(t + 1) * P],
                                    table[:, bass.ds(bl[t // GT] * width, width)], start=True, stop=True)
                return ins
            return f

        def turn_pairs(i, j):
            for q in range(GT):
                ins = pe.transpose(bank[1][:, q * P:(q + 1) * P], pre_s[:, q * P:(q + 1) * P], ident[:])
            return ins

        def second(i, j):
            pe.matmul(bank[2][:, :], ones[0:1, :], b2[:], start=True, stop=True)
            for q in range(GT):
                ins = pe.matmul(bank[2][:, q * P:(q + 1) * P], h1[:, q * P:(q + 1) * P], w2[:], start=False, stop=True,
                                skip_group_check=True)
            return ins

        def sum_messages(i, j):
            for h in range(2):
                for t in range(h * GT, (h + 1) * GT):
                    ins = pe.matmul(bank[3][0:D, h * P:(h + 1) * P], msg[:, t * D:(t + 1) * D], oh[:, t, :],
                                    start=t % GT == 0, stop=t % GT == GT - 1)
            return ins

        eg = Phase(G // 2, unroll=2)
        fetch_steps(eg, tb, xr, "pre")
        onehot_steps(eg, tb, "local", "sum")
        eg.step("pe", "local", "oht pre@1", gather_local(tb, ptab, D, bank[0]), stage=1, apart=True)
        eg.step("dve", "pre", "local rows turn@1", lambda i, j: dve.tensor_tensor(
            pre_s[:], bank[0][:, :], gx[j][:, :, :].rearrange("p t f -> p (t f)"), ALU.add), stage=1)
        eg.step("pe", "turn", "pre silu1@1", turn_pairs, stage=1, apart=True)
        eg.step("act", "silu1", "turn second@1", lambda i, j: act.activation(h1[:], bank[1][:, :], ACT.Silu), stage=1)
        eg.step("pe", "second", "silu1 silu2@1", second, stage=1)
        eg.step("act", "silu2", "second sum@1", lambda i, j: act.activation(msg[:], bank[2][:, :], ACT.Silu), stage=1)
        eg.step("pe", "sum", "silu2 oh add1@1", sum_messages, stage=1)
        add_messages(eg, tb, 3, "sum")

        up = Phase(NB // CH)

        def z1(i, j):
            for k in range(2):
                s_ = bass.ds(i * CHN + k * HALF, HALF)
                pe.matmul(bank[k][:, 0:HALF], m1a[:], hT[:, s_], start=True, stop=False)
                ins = pe.matmul(bank[k][:, 0:HALF], m1b[:], aggT[:, s_], start=False, stop=True)
            return ins

        def z2(i, j):
            for k in range(2):
                ins = pe.matmul(bank[2 + k][:, 0:HALF], m2[:], z1T[:, k * HALF:(k + 1) * HALF], start=True, stop=True)
            return ins
        up.step("pe", "z1", "silu@1", z1)
        up.step("act", "silu", "z1 z2@1", lambda i, j: act.activation(
            z1T[:].rearrange("p (k n) -> p k n", k=2), halves(0), ACT.Silu, bias=c1[:, 0:1]))
        up.step("pe", "z2", "silu h@1", z2)

        def h_new(i, j):
            s_ = hT[:, bass.ds(i * CHN, CHN)].rearrange("p (k n) -> p k n", k=2)
            return dve.scalar_tensor_tensor(s_, halves(2), c2[:, 0:1], s_, ALU.add, ALU.add)
        up.step("dve", "h", "z2", h_new)
        run_layers(E, [wl, nt, eg, up], LAYERS)

        ph = Phase(NB // CH)
        ph.step("dve", "hcur", "prod@1", lambda i, j: dve.tensor_copy(hcur[:], hT[:, bass.ds(i * CHN, CHN)]))

        def h_out(i, j):
            for b in range(CH):
                ins = pe.matmul(bank[0][:, b * D:(b + 1) * D], hcur[:, b * P:(b + 1) * P], w_out[:], start=True, stop=True)
            return ins
        ph.step("pe", "prod", "hcur add@1", h_out)

        def x_add(i, j):
            s_ = xn[:, bass.ds(i * CH, CH), :]
            return dve.tensor_tensor(s_, s_, bank[0][:, 0:CH * D].rearrange("p (b f) -> p b f", f=D), ALU.add)
        ph.step("dve", "add", "prod bias@1", x_add)

        def x_bias(i, j):
            s_ = xn[:, bass.ds(i * CH, CH), :]
            return dve.tensor_tensor(s_, s_, b_out[:].unsqueeze(1).broadcast_to([P, CH, D]), ALU.add)
        ph.step("dve", "bias", "add", x_bias)
        run(E, ph)
        layernorm(xn)
        tb = tables["d"]
        H, HD = 8, 16
        OKV = 2 * H * HD
        S = 9
        KC = 5
        AW = H * (HD + 1) + 1
        deg = sb("deg", [P, NB])
        transpose_nodes(xn, xT)
        ctx1 = ctx.enter_context(ExitStack())

        def t1(name, shape, dt=F32):
            return ctx1.enter_context(nc.sbuf_tensor(name, shape, dt))

        wq = t1("wq", [D, H * HD])
        cw = t1("cw", [P, KC, OKV])
        kvw1 = t1("kvw1", [P, 2 * D])
        kvb1 = t1("kvb1", [P, 1])
        kvw2 = t1("kvw2", [P, OKV])
        kvb2 = t1("kvb2", [1, OKV])
        wo1 = t1("wo1", [P, D])
        wself = t1("wself", [D, D])
        gamma = t1("gamma", [P, D])
        beta = t1("beta", [P, D])
        qtab = hT
        acc = t1("acc", [P, NB * AW])
        mx = t1("mx", [P, NB * H])
        identb = t1("identb", [P, P], BF16)
        rowno = t1("rowno", [P, 1])
        pick = t1("pick", [3 * 4 * H, GT * H * P], BF16)
        xcc = t1("xcc", [D, CHN])

        def weights1(i, j):
            yield sp.dma_start(wq[:], L1_Wq)
            for half, C in enumerate((L1_Cqk, L1_Cv)):
                o = slice(half * 128, (half + 1) * 128)
                for s in range(S):
                    yield sp.dma_start(cw[(s % 2) * D:(s % 2 + 1) * D, s // 2, o], C[:, s, :])
            yield sp.dma_start(kvw1[D:P, 0:D], L1_k_w1)
            yield sp.dma_start(kvw1[D:P, D:2 * D], L1_v_w1)
            yield sp.dma_start(kvb1[0:D, :], col(L1_k_b1))
            yield sp.dma_start(kvb1[D:P, :], col(L1_v_b1))
            yield sp.dma_start(kvw2[0:D, 0:128], L1_k_w2)
            yield sp.dma_start(kvw2[D:P, 128:256], L1_v_w2)
            yield sp.dma_start(kvb2[:, 0:128], L1_k_b2.rearrange("(a f) -> a f", a=1))
            yield sp.dma_start(kvb2[:, 128:256], L1_v_b2.rearrange("(a f) -> a f", a=1))
            yield sp.dma_start(wo1[:], L1_W_out)
            yield sp.dma_start(wself[:], L1_W_self)
            yield sp.dma_start(gamma[:], rows(L1_gamma))
            yield sp.dma_start(beta[:], rows(L1_beta))
            yield sp.dma_start(xr.rearrange("(b p) f -> p b f", p=P), xn[:])
        ld = Phase(1)
        ld.step("dve", "zero", "", lambda i, j: dve.memset(kvw2[:], 0.0))
        ld.step("dve", "zacc", "", lambda i, j: dve.memset(acc[:], 0.0))
        ld.step("dve", "mx", "", lambda i, j: dve.memset(mx[:], -BIG))
        ld.step("dve", "identb", "", lambda i, j: dve.tensor_copy(identb[:], ident[:]))
        ld.step("dve", "row_a", "", lambda i, j: dve.tensor_scalar(rowno[:], lane[:], 32.0, -32.0, ALU.is_ge, ALU.mult))
        ld.step("dve", "row_b", "row_a", lambda i, j: dve.tensor_scalar(stat[:, 0:1], lane[:], 64.0, -32.0, ALU.is_ge, ALU.mult))
        ld.step("dve", "row_c", "row_b", lambda i, j: dve.tensor_tensor(rowno[:], rowno[:], stat[:, 0:1], ALU.add))
        ld.step("dve", "row_d", "row_c", lambda i, j: dve.tensor_tensor(rowno[:], rowno[:], lane[:], ALU.add))
        ld.step("dve", "pick", "row_d", lambda i, j: dve.tensor_scalar(
            pick[:].rearrange("p (r n) -> p r n", n=P), node_iota[0:96, 0:GT * H].unsqueeze(2).broadcast_to([96, GT * H, P]),
            rowno[0:96, 0:1], None, ALU.is_equal))
        ld.step("sp", "weights", "zero", weights1, dma=1 + 2 * S + 8 + 4 + 1)
        run(E, ld)

        ph = Phase(NB // CH)
        ph.step("dve", "xcc", "prod@1", lambda i, j: dve.tensor_copy(xcc[:], xT[:, bass.ds(i * CHN, CHN)]))

        def q_prod(i, j):
            for b in range(CH):
                ins = pe.matmul(PS[:, b * P:(b + 1) * P], xcc[:, b * P:(b + 1) * P], wq[:], start=True, stop=True)
            return ins
        ph.step("pe", "prod", "xcc out@1", q_prod)
        ph.step("act", "out", "prod", lambda i, j: act.copy(qtab[:, bass.ds(i * CHN, CHN)], PS[:, 0:CHN]))
        run(E, ph)

        loop1 = ExitStack()

        def t2(name, shape, dt=F32):
            return loop1.enter_context(nc.sbuf_tensor(name, shape, dt))

        kr1 = [t2(f"kr1{j}", [P, GE], BF16) for j in range(2)]
        gi1 = [t2(f"gi1{j}", [P, GT], I32) for j in range(2)]
        ei1 = [t2(f"ei1{j}", [P, GT], I32) for j in range(2)]
        gx1 = [t2(f"gx1{j}", [P, GT, D]) for j in range(2)]
        gsh = [t2(f"gsh{j}", [P, GT, S]) for j in range(2)]
        xa = [t2(f"xa{j}", [P, GT, KC * P]) for j in range(2)]
        oht1 = [t2(f"oht1{j}", [P, GE]) for j in range(2)]
        oh1 = [t2(f"oh1{j}", [P, GT, P]) for j in range(2)]
        away = [t2(f"away{j}", [P, GE], BF16) for j in range(2)]
        xt = [t2(f"xt{k}", [P, KC * P]) for k in range(2)]
        hid = [t2(f"hid{k}", [P, P]) for k in range(2)]
        wkv = [t2(f"wkv{k}", [P, OKV]) for k in range(2)]
        kv = [t2(f"kv{j}", [P, GT, OKV]) for j in range(2)]
        qk = t2("qk", [P, H * HD])
        att = [t2(f"att{j}", [P, GT * H]) for j in range(2)]
        rest = t2("rest", [P, GT * H])
        parts = t2("parts", [P, 3 * GT * H], BF16)
        attT = t2("attT", [3 * GT * H, P], BF16)
        tmax = t2("tmax", [P, H, GT + 1])
        newm = t2("newm", [P, H])
        drop = t2("drop", [P, H])
        ex = t2("ex", [P, GT * H])
        msg1 = t2("msg1", [P, GT, AW])

        c = Phase(1)
        c.step("dve", "onecol", "", lambda i, j: dve.memset(msg1[:], 1.0))
        run(E, c)

        at = Phase(G, unroll=2)
        at.step("sp", "keys", "oht@2", lambda i, j: [sp.dma_start(
            kr1[j][:], tb["keyrow"][bass.ds(i * GE, GE)].partition_broadcast(P))], dma=1)
        at.step("dve", "gi", "rows@2", lambda i, j: dve.tensor_copy(gi1[j][:], tb["gidx"][:, bass.ds(i * GT, GT)]))
        at.step("dve", "ei", "rows@2", lambda i, j: dve.tensor_copy(ei1[j][:], eid[:, bass.ds(i * GT, GT)]))
        at.step("pool", "go", "gi ei outer3@2 turn3@2", lambda i, j: pool.nop(nofuse=True))

        def fetch1(i, j):
            for t in range(GT):
                by_src = bass.IndirectOffsetOnAxis(ap=gi1[j][:, t:t + 1], axis=0)
                by_edge = bass.IndirectOffsetOnAxis(ap=ei1[j][:, t:t + 1], axis=0)
                yield pool.indirect_dma_start(gx1[j][:, t, :], None, xr, by_src)
                yield pool.indirect_dma_start(xa[j][:, t, S * D:KC * P], None, ea64, by_edge)
                yield pool.indirect_dma_start(gsh[j][:, t, :], None, ea9, by_edge)
        at.step("pool", "rows", "", fetch1, dma=3 * GT)

        at.step("dve", "oht", "keys qloc@2 shift@2", lambda i, j: dve.tensor_scalar(
            oht1[j][:], kr1[j][:], lane[:, 0:1], None, ALU.is_equal), stage=1)
        at.step("dve", "oh", "sum@2", lambda i, j: dve.tensor_tensor(
            oh1[j][:], node_iota[:].unsqueeze(1).broadcast_to([P, GT, P]),
            tb["key"][:, bass.ds(i * GT, GT)].unsqueeze(2).broadcast_to([P, GT, P]), ALU.is_equal), stage=1)
        at.step("dve", "away", "oht", lambda i, j: dve.tensor_scalar(
            away[j][:], oht1[j][:], 1.0, BIG, ALU.subtract, ALU.mult), stage=1)

        def q_local(i, j):
            b = pe.value_load(tb["blk"][0:1, bass.ds(i, 1)], min_val=0, max_val=NB - 1)
            for t in range(GT):
                ins = pe.matmul(bank[5][:, t * P:(t + 1) * P], oht1[j][:, t * P:(t + 1) * P],
                                qtab[:, bass.ds(b * P, P)], start=True, stop=True)
            return ins

        def outer(t):
            return lambda i, j: dve.tensor_tensor(
                xa[j][:, t, 0:S * D].rearrange("p (s d) -> p s d", d=D),
                gx1[j][:, t, :].unsqueeze(1).broadcast_to([P, S, D]),
                gsh[j][:, t, :].unsqueeze(2).broadcast_to([P, S, D]), ALU.mult)

        def turn1(t):
            def f(i, j):
                for k in range(KC):
                    ins = pe.transpose(PS[:, k * P:(k + 1) * P], xa[j][:, t, k * P:(k + 1) * P], ident[:])
                return ins
            return f

        def main1(t):
            def f(i, j):
                for k in range(KC):
                    n_ = P if k < KC - 1 else D
                    ins = pe.matmul(bank[2 + t % 2][:, 0:OKV], xt[t % 2][0:n_, k * P:(k + 1) * P], cw[0:n_, k, :],
                                    start=k == 0, stop=k == KC - 1)
                return ins
            return f

        def second1(t):
            def f(i, j):
                o = bank[2 + t % 2][:, OKV:2 * OKV]
                pe.matmul(o, ones[0:1, :], kvb2[:], start=True, stop=False)
                return pe.matmul(o, hid[t % 2][:], kvw2[:], start=False, stop=True)
            return f

        def front(t, first_wait=""):
            p2 = f"{t - 2}" if t > 1 else f"{t + 2}"
            lag = "" if t > 1 else "@1"
            prev = f"{t - 1}" if t else "3"
            plag = "" if t else "@1"
            at.step("dve", f"outer{t}", f"rows turn{t}@2", outer(t), stage=1)
            at.step("pe", f"turn{t}", f"outer{t} xt{prev}{plag}", turn1(t), stage=1, apart=True)
            at.step("act", f"xt{t}", f"turn{t} main{p2}{lag} hid{p2}{lag}", lambda i, j: act.copy(xt[t % 2][:], PS[:, 0:KC * P]), stage=1)

        def middle(t):
            p2 = f"{t - 2}" if t > 1 else f"{t + 2}"
            lag = "" if t > 1 else "@1"
            prev = f"{t - 1}" if t else "3"
            plag = "" if t else "@1"
            at.step("pe", f"hid{t}", f"xt{t} relu{prev}{plag}", lambda i, j: pe.matmul(
                bank[4][:, 0:P], kvw1[D:P, :], xt[t % 2][D:P, (KC - 1) * P:KC * P], start=True, stop=True), stage=1)
            at.step("act", f"relu{t}", f"hid{t} second{p2}{lag}", lambda i, j: act.activation(
                hid[t % 2][:], bank[4][:, 0:P], ACT.Relu, bias=kvb1[:, 0:1]), stage=1)
            at.step("pe", f"main{t}", f"kv{p2}{lag} wkv{p2}{lag}", main1(t), stage=1)
            at.step("pe", f"second{t}", f"relu{t}", second1(t), stage=1)
            at.step("act", f"wkv{t}", f"second{t} kv{p2}{lag}", lambda i, j: act.copy(
                wkv[t % 2][:], bank[2 + t % 2][:, OKV:2 * OKV]), stage=1)
            at.step("dve", f"kv{t}", f"wkv{t} msg@2", lambda i, j: dve.tensor_tensor(
                kv[j][:, t, :], bank[2 + t % 2][:, 0:OKV], wkv[t % 2][:], ALU.mult), stage=1)
            at.step("dve", f"qk{t}", f"kv{t} qloc {'att' + prev + plag}", lambda i, j: dve.tensor_tensor(
                qk[:], kv[j][:, t, 0:H * HD], bank[5][:, t * P:(t + 1) * P], ALU.mult), stage=1)
            at.step("dve", f"att{t}", f"qk{t} less@2", lambda i, j: dve.tensor_reduce(
                att[j][:, t * H:(t + 1) * H], qk[:].rearrange("p (h d) -> p h d", d=HD), AX.X, ALU.add), stage=1)

        def split_steps():
            n_ = GT * H
            at.step("dve", "hi", "att3 attr@1", lambda i, j: dve.tensor_copy(parts[:, 0:n_], att[j][:]), stage=2)
            at.step("dve", "rest1", "hi", lambda i, j: dve.tensor_tensor(rest[:], att[j][:], parts[:, 0:n_], ALU.subtract), stage=2)
            at.step("dve", "mid", "rest1", lambda i, j: dve.tensor_copy(parts[:, n_:2 * n_], rest[:]), stage=2)
            at.step("dve", "lo", "mid", lambda i, j: dve.tensor_tensor(parts[:, 2 * n_:3 * n_], rest[:], parts[:, n_:2 * n_], ALU.subtract), stage=2)

        def max_tile(t):
            for half in range(2):
                def spread(i, j, half=half):
                    b = bank[6 + half]
                    pe.matmul(b[:, :], identb[:], away[j][:, t * P:(t + 1) * P].unsqueeze(1).broadcast_to([P, H // 2, P]),
                              start=True, stop=True)
                    for h in range(H // 2):
                        r = t * H + half * (H // 2) + h
                        ins = pe.matmul(b[:, h * P:(h + 1) * P], pick[:, r * P:(r + 1) * P], attT[:], start=False, stop=True,
                                        skip_group_check=True)
                    return ins
                before_ = f"tmax{t - 1}{half}" if t else ("attT" if half == 0 else "add@1")
                at.step("pe", f"spread{t}{half}", f"attT away {before_}", spread, stage=2)
                at.step("dve", f"tmax{t}{half}", f"spread{t}{half} newm@1", lambda i, j, half=half: dve.tensor_reduce(
                    tmax[:, half * (H // 2):(half + 1) * (H // 2), t], bank[6 + half][:, :].rearrange("p (h e) -> p h e", e=P),
                    AX.X, ALU.max), stage=2)

        def my_block(eng, i):
            return eng.value_load(tb["blk"][0:1, bass.ds(i, 1)], min_val=0, max_val=NB - 1)

        def old_max(i, j):
            return dve.tensor_copy(tmax[:, :, GT], mx[:, bass.ds(my_block(dve, i) * H, H)])

        def keep_max(i, j):
            return dve.tensor_copy(mx[:, bass.ds(my_block(dve, i) * H, H)], newm[:])

        def shift(i, j):
            for t in range(GT):
                ins = pe.matmul(bank[6][:, t * H:(t + 1) * H], oht1[j][:, t * P:(t + 1) * P], newm[:], start=True, stop=True)
            return ins

        def sum1(i, j):
            for t in range(GT):
                ins = pe.matmul(bank[7][:, 0:AW], oh1[j][:, t, :], msg1[:, t, :], start=t == 0, stop=t == GT - 1)
            return ins

        def rescale(i, j):
            a = acc[:, bass.ds(my_block(dve, i) * AW, AW - 1)].rearrange("p (h d) -> p h d", h=H)
            return dve.tensor_tensor(a, a, drop[:].unsqueeze(2).broadcast_to([P, H, HD + 1]), ALU.mult)

        def add1(i, j):
            a = acc[:, bass.ds(my_block(dve, i) * AW, AW)]
            return dve.tensor_tensor(a, a, bank[7][:, 0:AW], ALU.add)

        split_steps()
        front(0)
        at.step("pe", "attr", "lo attT@1 less@1", lambda i, j: pe.transpose(
            bank[6].bitcast(BF16)[0:3 * GT * H, 0:P], parts[:], identb[:]), stage=2, apart=True)
        at.step("act", "attT", "attr spread31@1", lambda i, j: act.copy(attT[:], bank[6].bitcast(BF16)[0:3 * GT * H, 0:P]), stage=2)
        at.step("pe", "qloc", "oht att3@1", q_local, stage=1, apart=True)
        front(1)
        middle(0)
        max_tile(0)
        front(2)
        middle(1)
        max_tile(1)
        max_tile(2)
        front(3)
        middle(2)
        max_tile(3)
        at.step("dve", "oldm", "newm@1 keepm@1", old_max, stage=2, apart=True)
        at.step("dve", "newm", "oldm tmax30 tmax31 shift@1", lambda i, j: dve.tensor_reduce(newm[:], tmax[:], AX.X, ALU.max), stage=2)
        at.step("dve", "keepm", "newm", keep_max, stage=2, apart=True)
        at.step("dve", "dropd", "newm dropx@1 resc@1", lambda i, j: dve.tensor_tensor(drop[:], tmax[:, :, GT], newm[:], ALU.subtract), stage=2)
        at.step("act", "dropx", "dropd", lambda i, j: act.activation(drop[:], drop[:], ACT.Exp), stage=2)
        at.step("pe", "shift", "newm tmax30", shift, stage=2)
        at.step("dve", "less", "shift exp@1 msg@1", lambda i, j: dve.tensor_tensor(ex[:], att[j][:], bank[6][:, 0:GT * H], ALU.subtract), stage=2)
        at.step("act", "exp", "less", lambda i, j: act.activation(ex[:], ex[:], ACT.Exp), stage=2)
        middle(3)
        ex_b = ex[:].rearrange("p (t h) -> p t h", h=H)

        def messages(i, j, t):
            return dve.tensor_tensor(
                msg1[:, t, 0:H * (HD + 1)].rearrange("p (h d) -> p h d", h=H)[:, :, 0:HD],
                kv[j][:, t, H * HD:OKV].rearrange("p (h d) -> p h d", h=H),
                ex_b[:, t, :].unsqueeze(2).broadcast_to([P, H, HD]), ALU.mult)
        for t in range(GT):
            at.step("dve", "msg" if t == GT - 1 else f"msg_{t}", "exp sum@1", lambda i, j, t=t: messages(i, j, t), stage=2)
        at.step("dve", "exs", "exp sum@1", lambda i, j: dve.tensor_copy(
            msg1[:, :, 0:H * (HD + 1)].rearrange("p t (h d) -> p t h d", h=H)[:, :, :, HD], ex_b), stage=2)
        at.step("pe", "sum", "msg exs tmax31 oh", sum1, stage=2)
        at.step("dve", "resc", "dropx add@1", rescale, stage=2, apart=True)
        at.step("dve", "add", "resc sum", add1, stage=2, apart=True)
        run(E, at)
        loop1.close()

        att_o = t1("att_o", [P, NB, D])
        den = t1("den", [P, CH * H])
        upd, updT = hcur, z1T
        av = acc[:].rearrange("p (b w) -> p b w", w=AW)
        ph = Phase(1)
        ph.step("dve", "deg", "", lambda i, j: dve.tensor_copy(deg[:], av[:, :, AW - 1]))
        run(E, ph)

        def chunk_acc(i):
            return acc[:, bass.ds(i * CH * AW, CH * AW)].rearrange("p (b w) -> p b w", w=AW)[:, :, 0:AW - 1].rearrange(
                "p b (h d) -> p b h d", h=H)
        ph = Phase(NB // CH)
        ph.step("dve", "den", "upd@1", lambda i, j: dve.tensor_scalar(
            den[:].rearrange("p (b h) -> p b h", h=H), chunk_acc(i)[:, :, :, HD], 1e-16, None, ALU.add))
        ph.step("dve", "inv", "den", lambda i, j: dve.reciprocal(den[:], den[:]))
        for b in range(CH):
            ph.step("dve", "upd" if b == CH - 1 else f"upd{b}", "inv turn@1", lambda i, j, b=b: dve.tensor_tensor(
                upd[:, b * P:(b + 1) * P].rearrange("p (h d) -> p h d", h=H), chunk_acc(i)[:, b, :, 0:HD],
                den[:, b * H:(b + 1) * H].unsqueeze(2).broadcast_to([P, H, HD]), ALU.mult))
        ph.step("dve", "xcc", "prod@1", lambda i, j: dve.tensor_copy(xcc[:], xT[:, bass.ds(i * CHN, CHN)]))

        def turn_upd(i, j):
            for b in range(CH):
                ins = pe.transpose(PS[:, b * P:(b + 1) * P], upd[:, b * P:(b + 1) * P], ident[:])
            return ins
        ph.step("pe", "turn", "upd updT@1", turn_upd, apart=True)
        ph.step("act", "updT", "turn prod@1", lambda i, j: act.copy(updT[:], PS[:, 0:CHN]))

        def o_prod(i, j):
            for b in range(CH):
                o = bank[2][:, b * D:(b + 1) * D]
                pe.matmul(o, updT[:, b * P:(b + 1) * P], wo1[:], start=True, stop=False)
                ins = pe.matmul(o, xcc[:, b * P:(b + 1) * P], wself[:], start=False, stop=True)
            return ins
        ph.step("pe", "prod", "updT xcc out@1", o_prod)
        ph.step("dve", "out", "prod", lambda i, j: dve.tensor_copy(
            att_o[:, bass.ds(i * CH, CH), :], bank[2][:, 0:CH * D].rearrange("p (b f) -> p b f", f=D)))
        run(E, ph)

        part = t1("part", [P, D])
        mu = t1("mu", [P, D])
        ph = Phase(1)
        across = [P, NB, D]
        by_f = "p b f -> p f b"
        ph.step("dve", "sum", "", lambda i, j: dve.tensor_reduce(part[:], att_o[:].rearrange(by_f), AX.X, ALU.add))
        ph.step("pe", "all", "sum", lambda i, j: pe.matmul(bank[0][:, 0:D], ones[:], part[:], start=True, stop=True))
        ph.step("dve", "mu", "all", lambda i, j: dve.tensor_scalar(mu[:], bank[0][:, 0:D], 1.0 / N, None, ALU.mult))
        ph.step("dve", "center", "mu", lambda i, j: dve.tensor_tensor(
            att_o[:], att_o[:], mu[:].unsqueeze(1).broadcast_to(across), ALU.subtract))
        ph.step("dve", "mask", "center", lambda i, j: dve.tensor_scalar(
            att_o[:, NB - 1, :], att_o[:, NB - 1, :], real[:, 0:1], None, ALU.mult))
        ph.step("dve", "square", "mask", lambda i, j: dve.tensor_tensor(sq[:], att_o[:], att_o[:], ALU.mult))
        ph.step("dve", "sumsq", "square", lambda i, j: dve.tensor_reduce(part[:], sq[:].rearrange(by_f), AX.X, ALU.add))
        ph.step("pe", "allsq", "sumsq", lambda i, j: pe.matmul(bank[1][:, 0:D], ones[:], part[:], start=True, stop=True))
        ph.step("dve", "var", "allsq", lambda i, j: dve.tensor_scalar(part[:], bank[1][:, 0:D], 1.0 / N, 1e-5, ALU.mult, ALU.add))
        ph.step("act", "sd", "var", lambda i, j: act.activation(part[:], part[:], ACT.Sqrt))
        ph.step("dve", "inv", "sd", lambda i, j: dve.reciprocal(part[:], part[:]))
        ph.step("dve", "gain", "inv", lambda i, j: dve.tensor_tensor(part[:], part[:], gamma[:], ALU.mult))
        ph.step("dve", "scale", "gain", lambda i, j: dve.tensor_tensor(
            att_o[:], att_o[:], part[:].unsqueeze(1).broadcast_to(across), ALU.mult))
        ph.step("dve", "beta", "scale", lambda i, j: dve.tensor_tensor(
            att_o[:], att_o[:], beta[:].unsqueeze(1).broadcast_to(across), ALU.add))
        ph.step("dve", "res", "beta", lambda i, j: dve.tensor_tensor(xn[:], xn[:], att_o[:], ALU.add))
        run(E, ph)
        layernorm(xn)
        ctx1.close()
        transpose_nodes(xn, xT)
        A = 16
        AP = 32
        w1n = sb("w1n", [D, 2, D])
        w1e = sb("w1e", [P, 4 * D])
        w3a = sb("w3a", [D, D])
        w3b = sb("w3b", [D, D])
        b3 = sb("b3", [P, D])
        xcd = sb("xcd", [D, CHN])
        agc = sb("agc", [D, CHN])
        fe = [sb(f"fe{j}", [P, W, AP]) for j in range(2)]
        fi = [sb(f"fi{j}", [P, W], I32) for j in range(2)]
        feT = sb("feT", [P, 2 * P])

        def weights2(i, j):
            yield sp.dma_start(w1n[:, 1, :], L2_W1[0:D, :])
            yield sp.dma_start(w1n[:, 0, :], L2_W1[D:2 * D, :])
            for k in range(4):
                yield sp.dma_start(w1e[k * AP:k * AP + A, k * D:(k + 1) * D], L2_W1[2 * D:2 * D + A, :])
            yield sp.dma_start(b1[:], rows(L2_b1))
            for k in range(2):
                yield sp.dma_start(w2[k * D:(k + 1) * D, k * D:(k + 1) * D], L2_W2)
            yield sp.dma_start(b2[:].rearrange("a (t f) -> a t f", f=D),
                               L2_b2.rearrange("(a f) -> a f", a=1).unsqueeze(1).broadcast_to([1, W, D]))
            yield sp.dma_start(w3a[:], L2_W3[0:D, :])
            yield sp.dma_start(w3b[:], L2_W3[D:2 * D, :])
            yield sp.dma_start(b3[:], rows(L2_b3))
        ld = Phase(1)
        ld.step("dve", "w1e", "", lambda i, j: dve.memset(w1e[:], 0.0))
        ld.step("sp", "weights", "w1e", weights2, dma=13)
        ld.step("dve", "zero", "", lambda i, j: dve.memset(aggT[:], 0.0))
        for j_ in range(2):
            ld.step("dve", f"gap{j_}", "", lambda i, j, j_=j_: dve.memset(fe[j_][:], 0.0))
        run(E, ld)

        nt = Phase(NB // CH)
        nt.step("dve", "xcd", "prod@1", lambda i, j: dve.tensor_copy(xcd[:], xT[:, bass.ds(i * CHN, CHN)]))

        def prod2(i, j):
            for b in range(CH):
                ins = pe.matmul(PS[:, b * P:(b + 1) * P], xcd[:, b * P:(b + 1) * P], w1n[:].rearrange("p k f -> p (k f)"),
                                start=True, stop=True)
            return ins
        nt.step("pe", "prod", "xcd qst@1 ptab@1", prod2)
        nt.step("dve", "ptab", "prod", lambda i, j: dve.tensor_tensor(
            ptab[:, bass.ds(i * CH * D, CH * D)].rearrange("p (b f) -> p b f", f=D), prod_out[:, :, 0, :],
            b1[:].unsqueeze(1).broadcast_to([P, CH, D]), ALU.add))
        nt.step("act", "qst", "ptab store@1", lambda i, j: act.copy(qst[:], prod_out[:, :, 1, :]))
        nt.step("sp", "store", "qst", lambda i, j: [sp.dma_start(
            xr[bass.ds(i * CHN, CHN), :].rearrange("(b p) f -> p b f", p=P), qst[:])], dma=1)
        run(E, nt)

        def turn_edge(i, j):
            for c_ in range(2):
                ins = pe.transpose(bank[4][:, c_ * P:(c_ + 1) * P],
                                   fe[j][:, c_ * 4:(c_ + 1) * 4, :].rearrange("p t f -> p (t f)"), ident[:])
            return ins

        def local2(i, j):
            bl = blocks(pe, tb, i)
            for c_ in range(2):
                pe.matmul(bank[0][:, c_ * 4 * D:(c_ + 1) * 4 * D], feT[:, c_ * P:(c_ + 1) * P], w1e[:],
                          start=c_ == 0, stop=True, skip_group_check=True)
            for t in range(W):
                ins = pe.matmul(bank[0][:, t * D:(t + 1) * D], oht[:, t * P:(t + 1) * P],
                                ptab[:, bass.ds(bl[t // GT] * D, D)], start=False, stop=True, skip_group_check=True)
            return ins

        eg2 = Phase(G // 2, unroll=2)
        fetch_steps(eg2, tb, xr, "pre")
        eg2.step("dve", "fi", "feat@2", lambda i, j: dve.tensor_copy(fi[j][:], eid[:, bass.ds(i * W, W)]))
        eg2.step("pool", "go2", "fi turne@2", lambda i, j: pool.nop(nofuse=True))
        eg2.step("pool", "feat", "", lambda i, j: [pool.indirect_dma_start(
            fe[j][:, c_, 0:A], None, ea16, bass.IndirectOffsetOnAxis(ap=fi[j][:, c_:c_ + 1], axis=0)) for c_ in range(W)], dma=W)
        onehot_steps(eg2, tb, "local", "sum")
        eg2.step("pe", "turne", "feat feT@1", turn_edge, stage=1, apart=True)
        eg2.step("act", "feT", "turne local@1", lambda i, j: act.copy(feT[:], bank[4][:, 0:2 * P]), stage=1)
        eg2.step("pe", "local", "oht feT pre@1", local2, stage=1, apart=True)
        eg2.step("dve", "pre", "local rows turn@1", lambda i, j: dve.tensor_tensor(
            pre_s[:], bank[0][:, :], gx[j][:, :, :].rearrange("p t f -> p (t f)"), ALU.add), stage=1)
        eg2.step("pe", "turn", "pre silu1@1", turn_pairs, stage=1, apart=True)
        eg2.step("act", "silu1", "turn second@1", lambda i, j: act.activation(h1[:], bank[1][:, :], ACT.Silu), stage=1)
        eg2.step("pe", "second", "silu1 silu2@1", second, stage=1)
        eg2.step("act", "silu2", "second sum@1", lambda i, j: act.activation(msg[:], bank[2][:, :], ACT.Silu), stage=1)
        eg2.step("pe", "sum", "silu2 oh add1@1", sum_messages, stage=1)
        add_messages(eg2, tb, 3, "sum")
        run(E, eg2)

        ph = Phase(NB // CH)
        ph.step("dve", "xcd", "prod@1", lambda i, j: dve.tensor_copy(xcd[:], xT[:, bass.ds(i * CHN, CHN)]))
        ph.step("dve", "agc", "prod@1", lambda i, j: dve.tensor_copy(agc[:], aggT[:, bass.ds(i * CHN, CHN)]))

        def prod3(i, j):
            for b in range(CH):
                o = bank[0][:, b * D:(b + 1) * D]
                pe.matmul(o, xcd[:, b * P:(b + 1) * P], w3a[:], start=True, stop=False)
                ins = pe.matmul(o, agc[:, b * P:(b + 1) * P], w3b[:], start=False, stop=True)
            return ins
        ph.step("pe", "prod", "xcd agc bias@1", prod3)
        ph.step("dve", "bias", "prod silu@1 add@1", lambda i, j: dve.tensor_tensor(
            qst[:], bank[0][:, 0:CH * D].rearrange("p (b f) -> p b f", f=D), b3[:].unsqueeze(1).broadcast_to([P, CH, D]), ALU.add))
        ph.step("act", "silu", "bias", lambda i, j: act.activation(qst[:], qst[:], ACT.Silu))

        def x_plus(i, j):
            s_ = xn[:, bass.ds(i * CH, CH), :]
            return dve.tensor_tensor(s_, s_, qst[:], ALU.add)
        ph.step("dve", "add", "silu", x_plus)
        run(E, ph)
        layernorm(xn)

        dinv = sb("dinv", [P, NB])
        some = sb("some", [P, NB])
        conv = sb("conv", [P, NB * D])
        cv3 = conv[:].rearrange("p (b f) -> p b f", f=D)
        dinv_b = dinv[:].unsqueeze(2).broadcast_to([P, NB, D])
        ph = Phase(1)
        ph.step("dve", "some", "", lambda i, j: dve.tensor_scalar(some[:], deg[:], 0.0, None, ALU.is_gt))
        ph.step("dve", "least", "", lambda i, j: dve.tensor_scalar(dinv[:], deg[:], 1.0, None, ALU.max))
        ph.step("act", "root", "least", lambda i, j: act.activation(dinv[:], dinv[:], ACT.Sqrt))
        ph.step("dve", "inv", "root", lambda i, j: dve.reciprocal(dinv[:], dinv[:]))
        ph.step("dve", "dinv", "inv some", lambda i, j: dve.tensor_tensor(dinv[:], dinv[:], some[:], ALU.mult))
        ph.step("dve", "rows", "dinv", lambda i, j: dve.tensor_tensor(sq[:], xn[:], dinv_b, ALU.mult))
        ph.step("sp", "store", "rows", lambda i, j: [sp.dma_start(xr.rearrange("(b p) f -> p b f", p=P), sq[:])], dma=1)
        ph.step("dve", "zero", "", lambda i, j: dve.memset(conv[:], 0.0))
        run(E, ph)

        def sum3(i, j):
            for h in range(2):
                for t in range(h * GT, (h + 1) * GT):
                    ins = pe.matmul(bank[0][:, h * D:(h + 1) * D], oh[:, t, :], gx[j][:, t, :], start=t % GT == 0, stop=t % GT == GT - 1)
            return ins

        def add3(i, j, h):
            b = dve.value_load(tb["blk"][0:1, bass.ds(i * 2 + h, 1)], min_val=0, max_val=NB - 1)
            a = conv[:, bass.ds(b * D, D)]
            return dve.tensor_tensor(a, a, bank[0][:, h * D:(h + 1) * D], ALU.add)
        eg3 = Phase(G // 2, unroll=2)
        eg3.step("dve", "gidx", "rows@2", lambda i, j: dve.tensor_copy(gi[j][:], tb["gidx"][:, bass.ds(i * W, W)]))
        eg3.step("pool", "go", "gidx sum@2", lambda i, j: pool.nop(nofuse=True))
        eg3.step("pool", "rows", "", lambda i, j: [pool.indirect_dma_start(
            gx[j][:, c_, :], None, xr, bass.IndirectOffsetOnAxis(ap=gi[j][:, c_:c_ + 1], axis=0)) for c_ in range(W)], dma=W)
        eg3.step("dve", "oh", "sum@1", lambda i, j: dve.tensor_tensor(
            oh[:], node_iota[:].unsqueeze(1).broadcast_to([P, W, P]),
            tb["key"][:, bass.ds(i * W, W)].unsqueeze(2).broadcast_to([P, W, P]), ALU.is_equal), stage=1)
        eg3.step("pe", "sum", "oh rows add1@1", sum3, stage=1)
        eg3.step("dve", "add0", "sum add1@1", lambda i, j: add3(i, j, 0), stage=1, apart=True)
        eg3.step("dve", "add1", "add0", lambda i, j: add3(i, j, 1), stage=1, apart=True)
        run(E, eg3)

        ph = Phase(1)
        ph.step("dve", "scale", "", lambda i, j: dve.tensor_tensor(cv3, cv3, dinv_b, ALU.mult))
        ph.step("dve", "res", "scale", lambda i, j: dve.tensor_tensor(xn[:], xn[:], cv3, ALU.add))
        run(E, ph)
        layernorm(xn)

        def result(i, j):
            yield sp.dma_start(out[0:(NB - 1) * P, :].rearrange("(b p) f -> p b f", p=P), xn[:, 0:NB - 1, :])
            yield sp.dma_start(out[(NB - 1) * P:N, :], xn[0:N - (NB - 1) * P, NB - 1, :])
        ph = Phase(1)
        ph.step("sp", "result", "", result, dma=2)
        run(E, ph)


IN = ["x", "src", "dst", "edge_attr_16", "edge_attr_64", "edge_attr_9",
      "L0_gnn_W_in", "L0_gnn_b_in", "L0_gnn_eW1", "L0_gnn_eb1", "L0_gnn_eW2", "L0_gnn_eb2", "L0_gnn_nW1",
      "L0_gnn_nb1", "L0_gnn_nW2", "L0_gnn_nb2", "L0_gnn_W_out", "L0_gnn_b_out", "L1_gnn_Wq", "L1_gnn_Cqk",
      "L1_gnn_Cv", "L1_gnn_k_w1", "L1_gnn_k_b1", "L1_gnn_k_w2", "L1_gnn_k_b2", "L1_gnn_v_w1", "L1_gnn_v_b1",
      "L1_gnn_v_w2", "L1_gnn_v_b2", "L1_gnn_W_out", "L1_gnn_W_self", "L1_gnn_gamma", "L1_gnn_beta",
      "L2_gnn_W1", "L2_gnn_b1", "L2_gnn_W2", "L2_gnn_b2", "L2_gnn_W3", "L2_gnn_b3"]


def kernel(**inputs):
    import numpy as np
    import concourse.bacc as bacc
    from concourse.bass_utils import run_bass_kernel_spmd

    nc = bacc.Bacc("TRN2", target_bir_lowering=False, num_devices=1)
    arrays, args = {}, []
    for name in IN:
        a = np.ascontiguousarray(inputs[name])
        arrays["in_" + name] = a
        args.append(nc.dram_tensor("in_" + name, a.shape, mybir.dt.from_np(a.dtype), kind="ExternalInput").ap())
    args.append(nc.dram_tensor("out_0", (N, D), F32, kind="ExternalOutput").ap())
    build(nc, *args)
    r = run_bass_kernel_spmd(nc, [arrays], core_ids=[0])
    return r.results[0]["out_0"]
```

```python
from contextlib import ExitStack

import concourse.bass as bass
from concourse import mybir

ALU = mybir.AluOpType
ACT = mybir.ActivationFunctionType
AX = mybir.AxisListType
F32 = mybir.dt.float32
BF16 = mybir.dt.bfloat16
I32 = mybir.dt.int32

P = 128
N = 3125
NE = 103125
NB = -(-N // P)
NPAD = NB * P
GT = 4
GE = GT * P
G = (NE + NB * (GE - 1)) // GE
G += G % 2
T = G * GT
SLOTS = T * P
EC = -(-NE // P)
ETAIL = NE - (P - 1) * EC
SC = 13
assert EC % SC == 0
D = 64
HID = 128
LAYERS = 4
CH = 5
CHN = CH * P
HALF = CHN // 2
BIG = 1.0e30
REC = 4
NOKEY = 255


class Engines:

    def __init__(self, nc, ctx):
        self.nc, self.ctx = nc, ctx
        self.eng = {"pe": nc.tensor, "dve": nc.vector, "act": nc.scalar, "pool": nc.gpsimd, "sp": nc.sync}
        self.sem, self.count = {}, {}
        for n in ("pe", "dve", "act", "pool"):
            self.semaphore(n)

    def semaphore(self, name):
        if name not in self.sem:
            self.sem[name] = self.ctx.enter_context(self.nc.semaphore("s_" + name))
            self.count[name] = 0
        return self.sem[name]


class Phase:

    def __init__(self, n, unroll=1, lead=None):
        self.n, self.unroll, self.steps, self.lead, self.late = n, unroll, [], lead, ()

    def step(self, eng, name, waits, fn, stage=0, dma=0, apart=False):
        self.steps.append((eng, name, waits.split(), fn, stage, dma, apart))

    def counts(self):
        turns = self.n + max(s[4] for s in self.steps)
        out = {}
        for eng, name, _, _, _, dma, _ in self.steps:
            if dma:
                for j in range(self.unroll):
                    key = f"{name}_{j}" if self.unroll > 1 else name
                    out[key] = out.get(key, 0) + 16 * dma * len(range(j, self.n, self.unroll))
            else:
                out[eng] = out.get(eng, 0) + turns
        return out

    def emit(self, E, base):
        nc, U = E.nc, self.unroll
        depth = max(s[4] for s in self.steps)
        lags = [int(w.split("@")[1]) for s in self.steps for w in s[2] if "@" in w]
        where, per = {}, {}
        for eng, name, _, _, stage, dma, _ in self.steps:
            if not dma:
                per[eng] = per.get(eng, 0) + 1
            where[name] = (eng, per.get(eng), stage, dma)
        for key in self.counts():
            E.semaphore(key)

        def turn(t, j0, static):
            for eng, name, waits, fn, stage, dma, apart in self.steps:
                e = E.eng[eng]
                if static and not 0 <= t - stage < self.n:
                    if not dma:
                        e.nop(nofuse=True)
                        e.drain().then_inc(E.sem[eng], 1)
                    continue
                need = {}
                for w in waits:
                    src, lag = (w.split("@") + ["0"])[:2]
                    weng, k, wstage, wdma = where[src]
                    lag = int(lag)
                    if static and t - stage - lag < 0:
                        continue
                    back = stage + lag
                    if wdma:
                        jj = (j0 - back) % U
                        key = f"{src}_{jj}" if U > 1 else src
                        if static:
                            val = (t - back) // U + 1
                        else:
                            val = t[0] + (j0 - back) // U + 1
                        need[key] = (wdma, val)
                    else:
                        d = k - (back - wstage) * per[weng]
                        if weng not in need or need[weng] < d:
                            need[weng] = d
                for key, v in need.items():
                    if key in per:
                        tt = t if static else (t[0] * U + j0)
                        e.wait_ge(E.sem[key], base[key] + tt * per[key] + v)
                        if eng == "sp":
                            e.nop(nofuse=True)
                    else:
                        e.wait_ge(E.sem[key], base[key] + v[1] * (16 * v[0]))
                        if eng == "sp":
                            e.nop(nofuse=True)
                if apart and need:
                    e.nop(nofuse=True)
                jb = (j0 - stage) % U
                i = (t - stage) if static else (t[0] * U + (j0 - stage))
                if dma:
                    key = f"{name}_{jb}" if U > 1 else name
                    sem = E.sem[key]
                    for ins in fn(i, jb):
                        ins.then_inc(sem, 16)
                else:
                    fn(i, jb).then_inc(E.sem[eng], 1)

        turns = self.n + depth
        lead = max([depth] + [g + depth for g in lags]) if self.lead is None else self.lead
        lead = -(-lead // U) * U
        loops = max(0, (self.n - lead) // U)
        if loops < 2:
            lead, loops = turns, 0
        for t in range(min(lead, turns)):
            turn(t, t % U, True)
        if loops:
            used = [e.engine for e in (E.eng[n] for n in dict.fromkeys(s[0] for s in self.steps))]
            with nc.Fori(lead // U, lead // U + loops, engines=tuple(used)) as r:
                for j in range(U):
                    turn((r,), j, False)
            for t in range(lead + loops * U, turns):
                turn(t, t % U, True)


def finish(E, phase, base):
    for key, n in phase.counts().items():
        base[key] = base[key] + n
    settle(E, [key for key in phase.counts() if key not in phase.late], base)


def settle(E, keys, base):
    for eng, e in E.eng.items():
        for key in keys:
            e.wait_ge(E.sem[key], base[key])
            if eng == "sp":
                e.nop(nofuse=True)


def run(E, phase):
    for key in phase.counts():
        E.semaphore(key)
    phase.emit(E, E.count)
    finish(E, phase, E.count)


def run_layers(E, phases, n):
    total = {}
    for ph in phases:
        for key, c in ph.counts().items():
            E.semaphore(key)
            total[key] = total.get(key, 0) + c
    with E.nc.Fori(0, n) as layer:
        for ph in phases:
            ph.layer = layer
        base = {k: E.count[k] + layer * total[k] if k in total else v for k, v in E.count.items()}
        for ph in phases:
            ph.emit(E, base)
            finish(E, ph, base)
    for k, c in total.items():
        E.count[k] += n * c



def build(nc, x_in, src_in, dst_in, ea16, ea64, ea9, L0_W_in, L0_b_in, L0_eW1, L0_eb1, L0_eW2, L0_eb2, L0_nW1,
          L0_nb1, L0_nW2, L0_nb2, L0_W_out, L0_b_out, L1_Wq, L1_Cqk, L1_Cv, L1_k_w1, L1_k_b1, L1_k_w2, L1_k_b2,
          L1_v_w1, L1_v_b1, L1_v_w2, L1_v_b2, L1_W_out, L1_W_self, L1_gamma, L1_beta, L2_W1, L2_b1, L2_W2, L2_b2,
          L2_W3, L2_b3, out, dbg=None):
    with ExitStack() as ctx:
        E = Engines(nc, ctx)

        def sb(name, shape, dt=F32):
            return ctx.enter_context(nc.sbuf_tensor(name, shape, dt))

        def dram(name, shape, dt=F32):
            return nc.dram_tensor(name, shape, dt, kind="Internal").ap()

        PS = ctx.enter_context(nc.psum_tensor("psum", [P, 8 * 512], F32))
        bank = [PS[:, b * 512:(b + 1) * 512] for b in range(8)]
        pe, dve, act, pool, sp = nc.tensor, nc.vector, nc.scalar, nc.gpsimd, nc.sync

        def rows(ap):
            return ap.partition_broadcast(P)

        def col(ap):
            return ap.rearrange("(p a) -> p a", a=1)

        ident = sb("ident", [P, P])
        lane = sb("lane", [P, 1])
        node_iota = sb("node_iota", [P, P])
        ones = sb("ones", [P, P])
        before = sb("before", [P, P])
        real = sb("real", [P, 1])
        c = Phase(1)
        c.step("pool", "iota_n", "", lambda i, j: pool.iota(node_iota[:], [[1, P]], base=0, channel_multiplier=0,
                                                            allow_small_or_imprecise_dtypes=True))
        c.step("pool", "iota_p", "", lambda i, j: pool.iota(lane[:], [[0, 1]], base=0, channel_multiplier=1,
                                                            allow_small_or_imprecise_dtypes=True))
        c.step("dve", "ones", "", lambda i, j: dve.memset(ones[:], 1.0))
        c.step("dve", "ident", "iota_n iota_p", lambda i, j: dve.tensor_scalar(ident[:], node_iota[:], lane[:, 0:1], None, ALU.is_equal))
        c.step("dve", "before", "", lambda i, j: dve.tensor_scalar(before[:], node_iota[:], lane[:, 0:1], None, ALU.is_gt))
        c.step("dve", "real", "", lambda i, j: dve.tensor_scalar(real[:], lane[:], float(N - (NB - 1) * P), None, ALU.is_lt))
        onesb = sb("onesb", [3, P], BF16)
        c.step("dve", "onesb", "", lambda i, j: dve.memset(onesb[:], 1.0))
        is_part = sb("is_part", [3, 3])
        c.step("dve", "is_part", "ident", lambda i, j: dve.tensor_copy(is_part[:], ident[0:3, 0:3]))
        run(E, c)

        def split_bias(ph, after, row3, parts3, work):
            hi, mid, low, left = work
            ph.step("dve", "b_hi", after, lambda i, j: dve.tensor_copy(hi, row3))
            ph.step("dve", "b_left", "b_hi", lambda i, j: dve.tensor_tensor(left, row3, hi, ALU.subtract))
            ph.step("dve", "b_mid", "b_left", lambda i, j: dve.tensor_copy(mid, left))
            ph.step("dve", "b_low", "b_mid", lambda i, j: dve.tensor_tensor(low, left, mid, ALU.subtract))
            ph.step("dve", "b_1", "b_low", lambda i, j: dve.tensor_scalar(left, hi, is_part[:, 0:1], None, ALU.mult))
            ph.step("dve", "b_2", "b_1", lambda i, j: dve.scalar_tensor_tensor(left, mid, is_part[:, 1:2], left, ALU.mult, ALU.add))
            ph.step("dve", "b_3", "b_2", lambda i, j: dve.scalar_tensor_tensor(parts3, low, is_part[:, 2:3], left, ALU.mult, ALU.add))

        def split_work(name, n_, alloc):
            return (alloc(name + "_hi", [3, n_], BF16)[:], alloc(name + "_mid", [3, n_], BF16)[:],
                    alloc(name + "_low", [3, n_])[:], alloc(name + "_left", [3, n_])[:])

        A, S = 16, 9
        FW = D + A + S
        feat = dram("feat", [NE, FW])
        cat = Phase(1)

        def concat(i, j):
            yield act.dma_start(feat[:, 0:D], ea64)
            yield act.dma_start(feat[:, D:D + A], ea16)
            yield act.dma_start(feat[:, D + A:FW], ea9)
        cat.step("act", "concat", "", concat, dma=3)
        cat.late = ("concat",)
        run(E, cat)

        tables = {}
        for order in "sd":
            tables[order] = dict(
                slots=dram(f"slots_{order}", [SLOTS, REC], I32),
                keyrow=dram(f"keyrow_{order}", [T * P], BF16),
                gidx=sb(f"gidx_{order}", [P, T], I32),
                key=sb(f"key_{order}", [P, T]),
                blk=sb(f"blk_{order}", [1, 2 * P], I32))
        eid = sb("eid", [P, T], I32)

        with ExitStack() as pre:
            def tmp(name, shape, dt=F32):
                return pre.enter_context(nc.sbuf_tensor(name, shape, dt))

            src = tmp("src", [P, EC], I32)
            dst = tmp("dst", [P, EC], I32)
            bucket = tmp("bucket", [P, EC])
            member = tmp("member", [P, EC])
            onesw = tmp("onesw", [P, EC])
            rank = tmp("rank", [P, EC])
            pos = tmp("pos", [P, EC])
            ibuf = tmp("ibuf", [P, EC], I32)
            row = tmp("row", [P, EC], I32)
            rec = tmp("rec", [P, T, REC], I32)
            cnt = tmp("cnt", [P, NB])
            first = tmp("first", [P, NB])
            itot = tmp("itot", [P, NB], I32)
            ngr = tmp("ngr", [P, NB])
            gend = tmp("gend", [P, NB])
            hit = tmp("hit", [P, 2, NB])
            gb = tmp("gb", [P, 2])
            gcol = tmp("gcol", [P, 2])
            sidx = [tmp(f"sidx{j}", [P, SC], I32) for j in range(2)]
            srec = [tmp(f"srec{j}", [P, SC * REC], I32) for j in range(2)]
            keyt = tmp("keyt", [P, P], BF16)

            ld = Phase(1)
            for t_, in_ in ((src, src_in), (dst, dst_in)):
                def load(i, j, t_=t_, in_=in_):
                    yield sp.dma_start(t_[0:P - 1, :], in_[0:(P - 1) * EC].rearrange("(p c) -> p c", c=EC))
                    yield sp.dma_start(t_[P - 1:P, 0:ETAIL], in_[(P - 1) * EC:NE].rearrange("(a c) -> a c", a=1))
                ld.step("dve", f"empty_{t_.name}", "", lambda i, j, t_=t_: dve.memset(t_[:], NB * P))
                ld.step("sp", f"load_{t_.name}", f"empty_{t_.name}", load, dma=2)
            ld.step("dve", "onesw", "", lambda i, j: dve.memset(onesw[:], 1.0))
            run(E, ld)

            for order, key, other in (("s", src, dst), ("d", dst, src)):
                tb = tables[order]
                a = Phase(1)
                a.step("dve", "empty", "", lambda i, j: dve.memset(rec[:], 0))
                a.step("dve", "nokey", "empty", lambda i, j: dve.memset(rec[:, :, 1], NOKEY))
                a.step("sp", "fill", "nokey", lambda i, j: [sp.dma_start(
                    tb["slots"].rearrange("(p t) r -> p (t r)", p=P), rec[:, :, :].rearrange("p t r -> p (t r)"))], dma=1)
                a.step("dve", "shift", "", lambda i, j: dve.tensor_scalar(ibuf[:], key[:], 7, None, ALU.logical_shift_right))
                a.step("dve", "bucket", "shift", lambda i, j: dve.tensor_copy(bucket[:], ibuf[:]))
                a.step("dve", "r_other", "fill", lambda i, j: dve.tensor_copy(rec[:, 0:EC, 0], other[:]))
                a.step("dve", "r_key", "fill", lambda i, j: dve.tensor_scalar(rec[:, 0:EC, 1], key[:], P - 1, None, ALU.bitwise_and))
                a.step("pool", "r_eid", "fill", lambda i, j: pool.iota(rec[:, 0:EC, 2], [[1, EC]], base=0, channel_multiplier=EC))
                a.step("pool", "r_eid2", "", lambda i, j: pool.iota(rec[:, 0:EC, 3], [[1, EC]], base=0, channel_multiplier=EC))
                a.step("dve", "pos0", "", lambda i, j: dve.memset(pos[:], 0.0))
                run(E, a)
                b = Phase(NB)
                b.step("dve", "member", "sum@1", lambda i, j: dve.tensor_scalar(
                    member[:], bucket[:], node_iota[:, bass.ds(i, 1)], None, ALU.is_equal))
                b.step("dve", "sum", "member", lambda i, j: dve.tensor_reduce(
                    cnt[:, bass.ds(i, 1)], member[:], AX.X, ALU.add))
                run(E, b)
                m = Phase(1)
                m.step("pe", "total", "", lambda i, j: pe.matmul(bank[0][:, 0:NB], ones[:], cnt[:], start=True, stop=True))
                m.step("pe", "below", "", lambda i, j: pe.matmul(bank[1][:, 0:NB], before[:], cnt[:], start=True, stop=True))
                m.step("dve", "itot", "total", lambda i, j: dve.tensor_scalar(itot[:], bank[0][:, 0:NB], float(GE - 1), None, ALU.add))
                m.step("dve", "igr", "itot", lambda i, j: dve.tensor_scalar(itot[:], itot[:], 9, None, ALU.logical_shift_right))
                m.step("dve", "ngr", "igr", lambda i, j: dve.tensor_copy(ngr[:], itot[:]))
                m.step("dve", "gend", "ngr", lambda i, j: dve.tensor_tensor_scan(gend[:], ones[:, 0:NB], ngr[:], 0.0, ALU.mult, ALU.add))
                m.step("dve", "gbeg", "gend", lambda i, j: dve.tensor_tensor(first[:], gend[:], ngr[:], ALU.subtract))
                m.step("dve", "gslot", "gbeg", lambda i, j: dve.tensor_scalar(first[:], first[:], float(GE), -1.0, ALU.mult, ALU.add))
                m.step("dve", "first", "gslot below", lambda i, j: dve.tensor_tensor(first[:], first[:], bank[1][:, 0:NB], ALU.add))
                m.step("pool", "gcol", "", lambda i, j: pool.iota(gcol[:], [[P, 2]], base=0, channel_multiplier=1,
                                                                  allow_small_or_imprecise_dtypes=True))
                for h in range(2):
                    m.step("dve", f"hit{h}", "gend gcol", lambda i, j, h=h: dve.tensor_scalar(
                        hit[:, h, :], gend[:], gcol[:, h:h + 1], None, ALU.is_le))
                m.step("dve", "gb", "hit1", lambda i, j: dve.tensor_reduce(gb[:], hit[:, :, 0:NB - 1], AX.X, ALU.add))
                for h in range(2):
                    m.step("pe", f"gbrow{h}", "gb", lambda i, j, h=h: pe.matmul(
                        bank[2][0:1, h * P:(h + 1) * P], gb[:, h:h + 1], ident[:], start=True, stop=True))
                m.step("dve", "blk", "gbrow1", lambda i, j: dve.tensor_copy(tb["blk"][:], bank[2][0:1, 0:2 * P]))
                run(E, m)
                r = Phase(NB)
                r.step("dve", "member", "masked@1", lambda i, j: dve.tensor_scalar(
                    member[:], bucket[:], node_iota[:, bass.ds(i, 1)], None, ALU.is_equal))
                r.step("dve", "scan", "member pos@1", lambda i, j: dve.tensor_tensor_scan(
                    rank[:], onesw[:], member[:], first[:, bass.ds(i, 1)], ALU.mult, ALU.add))
                r.step("dve", "masked", "scan", lambda i, j: dve.tensor_tensor(rank[:], rank[:], member[:], ALU.mult))
                r.step("dve", "pos", "masked", lambda i, j: dve.tensor_tensor(pos[:], pos[:], rank[:], ALU.add))
                run(E, r)
                w = Phase(1)
                w.step("dve", "ipos", "", lambda i, j: dve.tensor_copy(ibuf[:], pos[:]))
                w.step("dve", "ilane", "ipos", lambda i, j: dve.tensor_scalar(row[:], ibuf[:], P - 1, None, ALU.bitwise_and))
                w.step("dve", "itile", "ilane", lambda i, j: dve.tensor_scalar(ibuf[:], ibuf[:], 7, None, ALU.logical_shift_right))
                w.step("dve", "fold", "itile", lambda i, j: dve.scalar_tensor_tensor(
                    rank[:], row[:], float(T), ibuf[:], ALU.mult, ALU.add))
                w.step("dve", "pad", "", lambda i, j: dve.tensor_scalar(
                    member[:], bucket[:], float(NB), float(2 * SLOTS), ALU.is_ge, ALU.mult))
                w.step("dve", "row", "pad fold", lambda i, j: dve.tensor_tensor(row[:], rank[:], member[:], ALU.add))
                run(E, w)

                def scatter(i, j):
                    for c_ in range(SC):
                        yield pool.indirect_dma_start(
                            tb["slots"], bass.IndirectOffsetOnAxis(ap=sidx[j][:, c_:c_ + 1], axis=0),
                            srec[j][:, c_ * REC:(c_ + 1) * REC], None, bounds_check=SLOTS - 1, oob_is_err=False)
                s = Phase(EC // SC, unroll=2)
                s.step("dve", "sidx", "scatter@2", lambda i, j: dve.tensor_copy(sidx[j][:], row[:, bass.ds(i * SC, SC)]))
                s.step("dve", "srec", "scatter@2", lambda i, j: dve.tensor_copy(
                    srec[j][:], rec[:, bass.ds(i * SC, SC), :].rearrange("p t r -> p (t r)")))
                s.step("pool", "ready", "sidx srec", lambda i, j: pool.nop(nofuse=True))
                s.step("pool", "scatter", "", scatter, dma=SC)
                run(E, s)

                g = Phase(1)
                g.step("sp", "table", "", lambda i, j: [sp.dma_start(
                    rec[:, :, :].rearrange("p t r -> p (t r)"), tb["slots"].rearrange("(p t) r -> p (t r)", p=P))], dma=1)
                g.step("dve", "gidx", "table", lambda i, j: dve.tensor_copy(tb["gidx"][:], rec[:, :, 0]))
                g.step("dve", "key", "table", lambda i, j: dve.tensor_copy(tb["key"][:], rec[:, :, 1]))
                if order == "d":
                    g.step("dve", "eid", "table", lambda i, j: dve.tensor_copy(eid[:], rec[:, :, 2]))
                run(E, g)
                k = Phase(-(-T // P), unroll=1)
                for h in range(-(-T // P)):
                    n_ = min(P, T - h * P)
                    q = Phase(1)
                    q.step("pe", "turn", "", lambda i, j: pe.transpose(bank[0][0:n_, 0:P], tb["key"][:, h * P:h * P + n_], ident[:]))
                    q.step("dve", "keyt", "turn", lambda i, j: dve.tensor_copy(keyt[0:n_, :], bank[0][0:n_, 0:P]))
                    q.step("sp", "store", "keyt", lambda i, j: [sp.dma_start(
                        tb["keyrow"][h * P * P:(h * P + n_) * P].rearrange("(t p) -> t p", p=P), keyt[0:n_, :])], dma=1)
                    run(E, q)
        xn = sb("xn", [P, NB, D])
        xT = sb("xT", [D, NPAD])
        aggT = sb("aggT", [D, NPAD])
        xc = sb("xc", [P, CH * D])
        xr = dram("xr", [NPAD, D])
        sq = sb("sq", [P, NB, D])
        stat = sb("stat", [P, NB])
        stat2 = sb("stat2", [P, NB])

        def transpose_nodes(src_t, dst_t):
            t = Phase(NB // CH)
            t.step("dve", "copy", "turn@1", lambda i, j: dve.tensor_copy(
                xc[:], src_t[:, bass.ds(i * CH, CH), :].rearrange("p b f -> p (b f)")))

            def turn(i, j):
                for b in range(CH):
                    ins = pe.transpose(PS[0:D, b * P:(b + 1) * P], xc[:, b * D:(b + 1) * D], ident[:])
                return ins
            t.step("pe", "turn", "copy out@1", turn, apart=True)
            t.step("act", "out", "turn", lambda i, j: act.copy(dst_t[:, bass.ds(i * CHN, CHN)], PS[0:D, 0:CHN]))
            run(E, t)

        def layernorm(t, extra=None):
            mean = stat[:].unsqueeze(2).broadcast_to([P, NB, D])
            inv = stat2[:].unsqueeze(2).broadcast_to([P, NB, D])
            n = Phase(1)
            n.step("dve", "sum", "", lambda i, j: dve.tensor_reduce(stat[:], t[:], AX.X, ALU.add))
            n.step("dve", "mean", "sum", lambda i, j: dve.tensor_scalar(stat[:], stat[:], 1.0 / D, None, ALU.mult))
            n.step("dve", "center", "mean", lambda i, j: dve.tensor_tensor(t[:], t[:], mean, ALU.subtract))
            n.step("dve", "square", "center", lambda i, j: dve.tensor_tensor(sq[:], t[:], t[:], ALU.mult))
            n.step("dve", "sumsq", "square", lambda i, j: dve.tensor_reduce(stat2[:], sq[:], AX.X, ALU.add))
            n.step("dve", "var", "sumsq", lambda i, j: dve.tensor_scalar(stat2[:], stat2[:], 1.0 / D, 1e-5, ALU.mult, ALU.add))
            n.step("act", "sd", "var", lambda i, j: act.activation(stat2[:], stat2[:], ACT.Sqrt))
            n.step("dve", "inv", "sd", lambda i, j: dve.reciprocal(stat2[:], stat2[:]))
            n.step("dve", "scale", "inv", lambda i, j: dve.tensor_tensor(t[:], t[:], inv, ALU.mult))
            n.step("dve", "mask", "scale", lambda i, j: dve.tensor_scalar(
                t[:, NB - 1, :], t[:, NB - 1, :], real[:, 0:1], None, ALU.mult))
            run(E, n)

        def load_nodes(i, j):
            yield sp.dma_start(xn[:, 0:NB - 1, :], x_in[0:(NB - 1) * P, :].rearrange("(b p) f -> p b f", p=P))
            yield sp.dma_start(xn[0:N - (NB - 1) * P, NB - 1, :], x_in[(NB - 1) * P:N, :])
        ld = Phase(1)
        ld.step("dve", "zero", "", lambda i, j: dve.memset(xn[:], 0.0))
        ld.step("sp", "nodes", "zero", load_nodes, dma=2)
        run(E, ld)
        transpose_nodes(xn, xT)

        W = 2 * GT
        kr = [sb(f"kr{j}", [P, W * P], BF16) for j in range(2)]
        gi = [sb(f"gi{j}", [P, W], I32) for j in range(2)]
        gx = [sb(f"gx{j}", [P, W, D]) for j in range(2)]
        oht = sb("oht", [P, W * P])
        oh = sb("oh", [P, W, P])
        msg = [sb(f"msg{j}", [P, W * D]) for j in range(2)]

        def fetch_steps(ph, tb, table, free):
            ph.step("sp", "keys", "oht@2", lambda i, j: [sp.dma_start(
                kr[j][:], tb["keyrow"][bass.ds(i * (W * P), W * P)].partition_broadcast(P))], dma=1)
            ph.step("dve", "gidx", "rows@2", lambda i, j: dve.tensor_copy(gi[j][:], tb["gidx"][:, bass.ds(i * W, W)]))
            ph.step("pool", "go", f"gidx {free}@2", lambda i, j: pool.nop(nofuse=True))
            ph.step("pool", "rows", "", lambda i, j: [pool.indirect_dma_start(
                gx[j][:, c_, :], None, table, bass.IndirectOffsetOnAxis(ap=gi[j][:, c_:c_ + 1], axis=0)) for c_ in range(W)], dma=W)

        def edge_oh(ph, tb, stage):
            ph.step("dve", "oh", "sum@1", lambda i, j: dve.tensor_tensor(
                oh[:], node_iota[:].unsqueeze(1).broadcast_to([P, W, P]),
                tb["key"][:, bass.ds(i * W, W)].unsqueeze(2).broadcast_to([P, W, P]), ALU.is_equal), stage=stage)

        def node_oh(ph):
            ph.step("dve", "oht", "keys local@1", lambda i, j: dve.tensor_scalar(
                oht[:], kr[j][:], lane[:, 0:1], None, ALU.is_equal), stage=1)

        def blocks(eng, tb, i):
            return [eng.value_load(tb["blk"][0:1, bass.ds(i * 2 + h, 1)], min_val=0, max_val=NB - 1) for h in range(2)]

        def add_messages(ph, tb, src_bank, waits):
            def add(i, j, h):
                b = dve.value_load(tb["blk"][0:1, bass.ds(i * 2 + h, 1)], min_val=0, max_val=NB - 1)
                a = aggT[:, bass.ds(b * P, P)]
                return dve.tensor_tensor(a, a, bank[src_bank][0:D, h * P:(h + 1) * P], ALU.add)
            ph.step("dve", "add0", waits + " add1@1", lambda i, j: add(i, j, 0), stage=3, apart=True)
            ph.step("dve", "add1", "add0", lambda i, j: add(i, j, 1), stage=3, apart=True)

        tb = tables["s"]
        hT = sb("hT", [HID, NPAD])
        z1T = sb("z1T", [HID, CHN])
        hcur = sb("hcur", [HID, CHN])
        ptab = sb("ptab", [P, NB * D])
        qst = sb("qst", [P, CH, D])
        w_in = sb("w_in", [D, HID])
        b_in = sb("b_in", [HID, 1])
        w_out = sb("w_out", [HID, D])
        b_out = sb("b_out", [P, D])
        w1 = sb("w1", [HID, 2, D])
        b1 = sb("b1", [P, D])
        w2 = sb("w2", [P, P])
        b2r = sb("b2r", [3, D])
        b2 = sb("b2", [3, D], BF16)
        b2w = split_work("b2w", D, sb)
        m1a = sb("m1a", [HID, HID])
        m1b = sb("m1b", [D, HID])
        c1 = sb("c1", [HID, 1])
        m2 = sb("m2", [HID, HID])
        c2 = sb("c2", [HID, 1])
        h1 = sb("h1", [P, W * D])
        pre_s = [sb(f"pre_s{j}", [P, W * D]) for j in range(2)]

        ld = Phase(1)
        ld.step("dve", "zero", "", lambda i, j: dve.memset(w2[:], 0.0))
        ld.step("sp", "win", "", lambda i, j: [sp.dma_start(w_in[:], L0_W_in), sp.dma_start(b_in[:], col(L0_b_in)),
                                               sp.dma_start(w_out[:], L0_W_out), sp.dma_start(b_out[:], rows(L0_b_out))], dma=4)
        run(E, ld)

        def halves(lo):
            return PS[:, lo * 512:(lo + 2) * 512].rearrange("p (k n) -> p k n", k=2)[:, :, 0:HALF]

        ph = Phase(NB // CH)

        def h_in(i, j):
            for k in range(2):
                ins = pe.matmul(bank[k][:, 0:HALF], w_in[:], xT[:, bass.ds(i * CHN + k * HALF, HALF)], start=True, stop=True)
            return ins
        ph.step("pe", "win", "bias@1", h_in)
        ph.step("act", "bias", "win", lambda i, j: act.activation(
            hT[:, bass.ds(i * CHN, CHN)].rearrange("p (k n) -> p k n", k=2), halves(0), ACT.Identity, bias=b_in[:, 0:1]))
        run(E, ph)

        wl = Phase(1)

        def layer_weights(i, j):
            l = wl.layer
            yield sp.dma_start(w1[:], L0_eW1[bass.ds(l, 1), :, :].rearrange("a (k p) f -> p (a k) f", p=P))
            yield sp.dma_start(b1[:], L0_eb1[bass.ds(l, 1), :].rearrange("a f -> (a f)").partition_broadcast(P))
            for k in range(2):
                yield sp.dma_start(w2[k * D:(k + 1) * D, k * D:(k + 1) * D], L0_eW2[bass.ds(l, 1), :, :].rearrange("a p f -> p (a f)"))
            yield sp.dma_start(b2r[:], L0_eb2[bass.ds(l, 1), :].rearrange("a f -> (a f)").partition_broadcast(3))
            yield sp.dma_start(m1a[:], L0_nW1[bass.ds(l, 1), 0:HID, :].rearrange("a p f -> p (a f)"))
            yield sp.dma_start(m1b[:], L0_nW1[bass.ds(l, 1), HID:HID + D, :].rearrange("a p f -> p (a f)"))
            yield sp.dma_start(c1[:], L0_nb1[bass.ds(l, 1), :].rearrange("a (p f) -> p (a f)", f=1))
            yield sp.dma_start(m2[:], L0_nW2[bass.ds(l, 1), :, :].rearrange("a p f -> p (a f)"))
            yield sp.dma_start(c2[:], L0_nb2[bass.ds(l, 1), :].rearrange("a (p f) -> p (a f)", f=1))
        wl.step("sp", "weights", "", layer_weights, dma=10)
        wl.step("dve", "zero", "", lambda i, j: dve.memset(aggT[:], 0.0))
        split_bias(wl, "weights", b2r[:], b2[:], b2w)

        nt = Phase(NB // CH)
        nt.step("dve", "hcur", "prod@1", lambda i, j: dve.tensor_copy(hcur[:], hT[:, bass.ds(i * CHN, CHN)]))

        def prod(i, j):
            for b in range(CH):
                ins = pe.matmul(PS[:, b * P:(b + 1) * P], hcur[:, b * P:(b + 1) * P], w1[:].rearrange("p k f -> p (k f)"),
                                start=True, stop=True)
            return ins
        nt.step("pe", "prod", "hcur qst@1 ptab@1", prod)
        prod_out = PS[:, 0:CHN].rearrange("p (b k f) -> p b k f", b=CH, k=2)
        nt.step("dve", "ptab", "prod", lambda i, j: dve.tensor_tensor(
            ptab[:, bass.ds(i * CH * D, CH * D)].rearrange("p (b f) -> p b f", f=D), prod_out[:, :, 0, :],
            b1[:].unsqueeze(1).broadcast_to([P, CH, D]), ALU.add))
        nt.step("act", "qst", "ptab store@1", lambda i, j: act.copy(qst[:], prod_out[:, :, 1, :]))
        nt.step("sp", "store", "qst", lambda i, j: [sp.dma_start(
            xr[bass.ds(i * CHN, CHN), :].rearrange("(b p) f -> p b f", p=P), qst[:])], dma=1)

        def gather_local(tb, table, width, dst):
            def f(i, j):
                bl = blocks(pe, tb, i)
                for t in range(W):
                    ins = pe.matmul(dst[:, t * width:(t + 1) * width], oht[:, t * P:(t + 1) * P],
                                    table[:, bass.ds(bl[t // GT] * width, width)], start=True, stop=True)
                return ins
            return f

        def turn_pairs(i, j):
            for q in range(GT):
                ins = pe.transpose(bank[1][:, q * P:(q + 1) * P], pre_s[j][:, q * P:(q + 1) * P], ident[:])
            return ins

        def second(i, j):
            pe.matmul(bank[2][:, :], onesb[:], b2[:].unsqueeze(1).broadcast_to([3, W, D]), start=True, stop=True)
            for q in range(GT):
                ins = pe.matmul(bank[2][:, q * P:(q + 1) * P], h1[:, q * P:(q + 1) * P], w2[:], start=False, stop=True,
                                skip_group_check=True)
            return ins

        def sum_messages(i, j):
            for h in range(2):
                for t in range(h * GT, (h + 1) * GT):
                    ins = pe.matmul(bank[3][0:D, h * P:(h + 1) * P], msg[j][:, t * D:(t + 1) * D], oh[:, t, :],
                                    start=t % GT == 0, stop=t % GT == GT - 1)
            return ins

        def mlp_steps(ph, tb, local_step, feature_steps=None):
            fetch_steps(ph, tb, xr, "pre")
            ph.step("pe", "turn", "pre silu1@1", turn_pairs, stage=2, apart=True)
            ph.step("act", "silu1", "turn second@1", lambda i, j: act.activation(h1[:], bank[1][:, :], ACT.Silu), stage=2)
            edge_oh(ph, tb, 3)
            node_oh(ph)
            if feature_steps:
                feature_steps(ph)
            ph.step("pe", "sum", "silu2 oh add1@1", sum_messages, stage=3)
            local_step(ph)
            ph.step("pe", "second", "silu1 silu2@1", second, stage=2)
            ph.step("act", "silu2", "second sum@2", lambda i, j: act.activation(msg[j][:], bank[2][:, :], ACT.Silu), stage=2)
            add_messages(ph, tb, 3, "sum")
            ph.step("dve", "pre", "local rows turn@2", lambda i, j: dve.tensor_tensor(
                pre_s[j][:], bank[0][:, :], gx[j][:, :, :].rearrange("p t f -> p (t f)"), ALU.add), stage=1)

        eg = Phase(G // 2, unroll=2)
        mlp_steps(eg, tb, lambda ph: ph.step("pe", "local", "oht pre@1", gather_local(tb, ptab, D, bank[0]), stage=1, apart=True))

        up = Phase(NB // CH)

        def z1(i, j):
            for k in range(2):
                s_ = bass.ds(i * CHN + k * HALF, HALF)
                pe.matmul(bank[k][:, 0:HALF], m1a[:], hT[:, s_], start=True, stop=False)
                ins = pe.matmul(bank[k][:, 0:HALF], m1b[:], aggT[:, s_], start=False, stop=True)
            return ins

        def z2(i, j):
            for k in range(2):
                ins = pe.matmul(bank[2 + k][:, 0:HALF], m2[:], z1T[:, k * HALF:(k + 1) * HALF], start=True, stop=True)
            return ins
        up.step("pe", "z1", "silu@1", z1)
        up.step("act", "silu", "z1 z2@1", lambda i, j: act.activation(
            z1T[:].rearrange("p (k n) -> p k n", k=2), halves(0), ACT.Silu, bias=c1[:, 0:1]))
        up.step("pe", "z2", "silu h@1", z2)

        def h_new(i, j):
            s_ = hT[:, bass.ds(i * CHN, CHN)].rearrange("p (k n) -> p k n", k=2)
            return dve.scalar_tensor_tensor(s_, halves(2), c2[:, 0:1], s_, ALU.add, ALU.add)
        up.step("dve", "h", "z2", h_new)
        run_layers(E, [wl, nt, eg, up], LAYERS)

        ph = Phase(NB // CH)
        ph.step("dve", "hcur", "prod@1", lambda i, j: dve.tensor_copy(hcur[:], hT[:, bass.ds(i * CHN, CHN)]))

        def h_out(i, j):
            for b in range(CH):
                ins = pe.matmul(bank[0][:, b * D:(b + 1) * D], hcur[:, b * P:(b + 1) * P], w_out[:], start=True, stop=True)
            return ins
        ph.step("pe", "prod", "hcur add@1", h_out)

        def x_add(i, j):
            s_ = xn[:, bass.ds(i * CH, CH), :]
            return dve.tensor_tensor(s_, s_, bank[0][:, 0:CH * D].rearrange("p (b f) -> p b f", f=D), ALU.add)
        ph.step("dve", "add", "prod bias@1", x_add)

        def x_bias(i, j):
            s_ = xn[:, bass.ds(i * CH, CH), :]
            return dve.tensor_tensor(s_, s_, b_out[:].unsqueeze(1).broadcast_to([P, CH, D]), ALU.add)
        ph.step("dve", "bias", "add", x_bias)
        run(E, ph)
        layernorm(xn)
        tb = tables["d"]
        H, HD = 8, 16
        OKV = 2 * H * HD
        AP = 32
        KC = 5
        AW = H * (HD + 1) + 1
        deg = sb("deg", [P, NB])
        slot_feat = dram("slot_feat", [P, T * AP])
        transpose_nodes(xn, xT)
        ctx1 = ctx.enter_context(ExitStack())

        def t1(name, shape, dt=F32):
            return ctx1.enter_context(nc.sbuf_tensor(name, shape, dt))

        wq = t1("wq", [D, H * HD])
        cw = t1("cw", [P, KC, OKV])
        kvw1 = t1("kvw1", [P, 2 * D])
        kvb1 = t1("kvb1", [P, 1])
        kvw2 = t1("kvw2", [P, OKV])
        kvb2r = t1("kvb2r", [3, OKV])
        kvb2 = t1("kvb2", [3, OKV], BF16)
        kvb2w = split_work("kvb2w", OKV, t1)
        wo1 = t1("wo1", [P, D])
        wself = t1("wself", [D, D])
        gamma = t1("gamma", [P, D])
        beta = t1("beta", [P, D])
        qtab = hT
        acc = t1("acc", [P, NB * AW])
        mx = t1("mx", [P, NB * H])
        identb = t1("identb", [P, P], BF16)
        rowno = t1("rowno", [P, 1])
        pick = t1("pick", [3 * 4 * H, GT * H * P], BF16)
        xcc = t1("xcc", [D, CHN])

        def weights1(i, j):
            yield sp.dma_start(wq[:], L1_Wq)
            for half, C in enumerate((L1_Cqk, L1_Cv)):
                o = slice(half * 128, (half + 1) * 128)
                for s in range(S):
                    yield sp.dma_start(cw[(s % 2) * D:(s % 2 + 1) * D, s // 2, o], C[:, s, :])
            yield sp.dma_start(kvw1[D:P, 0:D], L1_k_w1)
            yield sp.dma_start(kvw1[D:P, D:2 * D], L1_v_w1)
            yield sp.dma_start(kvb1[0:D, :], col(L1_k_b1))
            yield sp.dma_start(kvb1[D:P, :], col(L1_v_b1))
            yield sp.dma_start(kvw2[0:D, 0:128], L1_k_w2)
            yield sp.dma_start(kvw2[D:P, 128:256], L1_v_w2)
            yield sp.dma_start(kvb2r[:, 0:128], L1_k_b2.partition_broadcast(3))
            yield sp.dma_start(kvb2r[:, 128:256], L1_v_b2.partition_broadcast(3))
            yield sp.dma_start(wo1[:], L1_W_out)
            yield sp.dma_start(wself[:], L1_W_self)
            yield sp.dma_start(gamma[:], rows(L1_gamma))
            yield sp.dma_start(beta[:], rows(L1_beta))
            yield sp.dma_start(xr.rearrange("(b p) f -> p b f", p=P), xn[:])
        ld = Phase(1)
        ld.step("dve", "zero", "", lambda i, j: dve.memset(kvw2[:], 0.0))
        ld.step("dve", "zacc", "", lambda i, j: dve.memset(acc[:], 0.0))
        ld.step("dve", "mx", "", lambda i, j: dve.memset(mx[:], -BIG))
        ld.step("dve", "identb", "", lambda i, j: dve.tensor_copy(identb[:], ident[:]))
        ld.step("dve", "row_a", "", lambda i, j: dve.tensor_scalar(rowno[:], lane[:], 32.0, -32.0, ALU.is_ge, ALU.mult))
        ld.step("dve", "row_b", "row_a", lambda i, j: dve.tensor_scalar(stat[:, 0:1], lane[:], 64.0, -32.0, ALU.is_ge, ALU.mult))
        ld.step("dve", "row_c", "row_b", lambda i, j: dve.tensor_tensor(rowno[:], rowno[:], stat[:, 0:1], ALU.add))
        ld.step("dve", "row_d", "row_c", lambda i, j: dve.tensor_tensor(rowno[:], rowno[:], lane[:], ALU.add))
        ld.step("dve", "pick", "row_d", lambda i, j: dve.tensor_scalar(
            pick[:].rearrange("p (r n) -> p r n", n=P), node_iota[0:96, 0:GT * H].unsqueeze(2).broadcast_to([96, GT * H, P]),
            rowno[0:96, 0:1], None, ALU.is_equal))
        ld.step("sp", "weights", "zero", weights1, dma=1 + 2 * S + 8 + 4 + 1)
        split_bias(ld, "weights", kvb2r[:], kvb2[:], kvb2w)
        run(E, ld)

        ph = Phase(NB // CH)
        ph.step("dve", "xcc", "prod@1", lambda i, j: dve.tensor_copy(xcc[:], xT[:, bass.ds(i * CHN, CHN)]))

        def q_prod(i, j):
            for b in range(CH):
                ins = pe.matmul(PS[:, b * P:(b + 1) * P], xcc[:, b * P:(b + 1) * P], wq[:], start=True, stop=True)
            return ins
        ph.step("pe", "prod", "xcc out@1", q_prod)
        ph.step("act", "out", "prod", lambda i, j: act.copy(qtab[:, bass.ds(i * CHN, CHN)], PS[:, 0:CHN]))
        run(E, ph)

        loop1 = ExitStack()

        def t2(name, shape, dt=F32):
            return loop1.enter_context(nc.sbuf_tensor(name, shape, dt))

        gi1 = [t2(f"gi1{j}", [P, GT], I32) for j in range(2)]
        ei1 = [t2(f"ei1{j}", [P, GT], I32) for j in range(2)]
        gf = [t2(f"gf{j}", [P, GT, D + AP]) for j in range(2)]
        xa = [t2(f"xa{j}", [P, GT, KC * P]) for j in range(2)]
        oht1 = [t2(f"oht1{j}", [P, GE]) for j in range(2)]
        away = [t2(f"away{j}", [P, GE], BF16) for j in range(2)]
        xt = [t2(f"xt{k}", [P, KC * P]) for k in range(2)]
        hid = [t2(f"hid{k}", [P, P]) for k in range(2)]
        wkv = [t2(f"wkv{k}", [P, OKV]) for k in range(2)]
        kv = [t2(f"kv{j}", [P, GT, OKV]) for j in range(2)]
        qk = t2("qk", [P, H * HD])
        att = [t2(f"att{j}", [P, GT * H]) for j in range(2)]
        rest = t2("rest", [P, GT * H])
        parts = t2("parts", [P, 3 * GT * H], BF16)
        attT = t2("attT", [3 * GT * H, P], BF16)
        tmax = t2("tmax", [P, H, GT + 1])
        newm = t2("newm", [P, H])
        drop = t2("drop", [P, H])
        ex = t2("ex", [P, GT * H])
        msg1 = t2("amsg", [P, GT, AW])

        settle(E, ["concat"], E.count)
        c = Phase(1)
        c.step("dve", "onecol", "", lambda i, j: dve.memset(msg1[:], 1.0))
        for j_ in range(2):
            c.step("dve", f"gap{j_}", "", lambda i, j, j_=j_: dve.memset(gf[j_][:], 0.0))
        run(E, c)

        at = Phase(G, unroll=2)
        at.step("sp", "keys", "oht@2", lambda i, j: [sp.dma_start(
            kr[j][:, 0:GE], tb["keyrow"][bass.ds(i * GE, GE)].partition_broadcast(P))], dma=1)
        at.step("dve", "gi", "rows@2", lambda i, j: dve.tensor_copy(gi1[j][:], tb["gidx"][:, bass.ds(i * GT, GT)]))
        at.step("dve", "ei", "rows@2", lambda i, j: dve.tensor_copy(ei1[j][:], eid[:, bass.ds(i * GT, GT)]))
        at.step("pool", "go", "gi ei outer3@2 edge@2 keepf@2", lambda i, j: pool.nop(nofuse=True))

        def fetch1(i, j):
            for t in range(GT):
                yield pool.indirect_dma_start(gx[j][:, t, :], None, xr, bass.IndirectOffsetOnAxis(ap=gi1[j][:, t:t + 1], axis=0))
                yield pool.indirect_dma_start(gf[j][:, t, 0:FW], None, feat, bass.IndirectOffsetOnAxis(ap=ei1[j][:, t:t + 1], axis=0))
        at.step("pool", "rows", "", fetch1, dma=2 * GT)

        def q_local(i, j):
            b = pe.value_load(tb["blk"][0:1, bass.ds(i, 1)], min_val=0, max_val=NB - 1)
            for t in range(GT):
                ins = pe.matmul(bank[5][:, t * P:(t + 1) * P], oht1[j][:, t * P:(t + 1) * P],
                                qtab[:, bass.ds(b * P, P)], start=True, stop=True)
            return ins

        def outer(t):
            return lambda i, j: dve.tensor_tensor(
                xa[j][:, t, 0:S * D].rearrange("p (s d) -> p s d", d=D),
                gx[j][:, t, :].unsqueeze(1).broadcast_to([P, S, D]),
                gf[j][:, t, D + A:FW].unsqueeze(2).broadcast_to([P, S, D]), ALU.mult)

        def turn1(t):
            def f(i, j):
                for k in range(KC):
                    ins = pe.transpose(PS[:, k * P:(k + 1) * P], xa[j][:, t, k * P:(k + 1) * P], ident[:])
                return ins
            return f

        def main1(t):
            def f(i, j):
                for k in range(KC):
                    n_ = P if k < KC - 1 else D
                    ins = pe.matmul(bank[2 + t % 2][:, 0:OKV], xt[t % 2][0:n_, k * P:(k + 1) * P], cw[0:n_, k, :],
                                    start=k == 0, stop=k == KC - 1)
                return ins
            return f

        def second1(t):
            def f(i, j):
                o = bank[2 + t % 2][:, OKV:2 * OKV]
                pe.matmul(o, onesb[:], kvb2[:], start=True, stop=False)
                return pe.matmul(o, hid[t % 2][:], kvw2[:], start=False, stop=True)
            return f

        def around(t, name, back):
            return f"{name}{t - back}" if t >= back else f"{name}{t - back + GT}@1"

        def outer_step(t):
            at.step("dve", f"outer{t}", f"rows turn{t}@2", outer(t), stage=1)

        def turn_steps(t):
            at.step("pe", f"turn{t}", f"outer{t} edge {around(t, 'xt', 1)}", turn1(t), stage=2, apart=True)
            at.step("act", f"xt{t}", f"turn{t} {around(t, 'main', 2)} {around(t, 'hid', 2)}",
                    lambda i, j: act.copy(xt[t % 2][:], PS[:, 0:KC * P]), stage=2)

        def main_steps(t):
            at.step("pe", f"hid{t}", f"xt{t} {around(t, 'relu', 1)}", lambda i, j: pe.matmul(
                bank[4][:, 0:P], kvw1[D:P, :], xt[t % 2][D:P, (KC - 1) * P:KC * P], start=True, stop=True), stage=2)
            at.step("act", f"relu{t}", f"hid{t} {around(t, 'second', 2)}", lambda i, j: act.activation(
                hid[t % 2][:], bank[4][:, 0:P], ACT.Relu, bias=kvb1[:, 0:1]), stage=2)
            at.step("pe", f"main{t}", f"{around(t, 'kv', 2)} {around(t, 'wkv', 2)}", main1(t), stage=2)

        def second_steps(t):
            at.step("pe", f"second{t}", f"relu{t}", second1(t), stage=2)
            at.step("act", f"wkv{t}", f"second{t} {around(t, 'kv', 2)}", lambda i, j: act.copy(
                wkv[t % 2][:], bank[2 + t % 2][:, OKV:2 * OKV]), stage=2)

        def kv_steps(t):
            at.step("dve", f"kv{t}", f"wkv{t} msg@2", lambda i, j: dve.tensor_tensor(
                kv[j][:, t, :], bank[2 + t % 2][:, 0:OKV], wkv[t % 2][:], ALU.mult), stage=2)
            at.step("dve", f"qk{t}", f"kv{t} qloc {around(t, 'att', 1)}", lambda i, j: dve.tensor_tensor(
                qk[:], kv[j][:, t, 0:H * HD], bank[5][:, t * P:(t + 1) * P], ALU.mult), stage=2)
            at.step("dve", f"att{t}", f"qk{t} less@2", lambda i, j: dve.tensor_reduce(
                att[j][:, t * H:(t + 1) * H], qk[:].rearrange("p (h d) -> p h d", d=HD), AX.X, ALU.add), stage=2)

        def split_steps():
            n_ = GT * H
            at.step("dve", "hi", "att3 attr@1", lambda i, j: dve.tensor_copy(parts[:, 0:n_], att[j][:]), stage=3)
            at.step("dve", "rest1", "hi", lambda i, j: dve.tensor_tensor(rest[:], att[j][:], parts[:, 0:n_], ALU.subtract), stage=3)
            at.step("dve", "mid", "rest1", lambda i, j: dve.tensor_copy(parts[:, n_:2 * n_], rest[:]), stage=3)
            at.step("dve", "lo", "mid", lambda i, j: dve.tensor_tensor(parts[:, 2 * n_:3 * n_], rest[:], parts[:, n_:2 * n_], ALU.subtract), stage=3)

        def max_tile(t):
            for half in range(2):
                def spread(i, j, half=half):
                    b = bank[6 + half]
                    pe.matmul(b[:, :], identb[:], away[j][:, t * P:(t + 1) * P].unsqueeze(1).broadcast_to([P, H // 2, P]),
                              start=True, stop=True)
                    for h in range(H // 2):
                        r = t * H + half * (H // 2) + h
                        ins = pe.matmul(b[:, h * P:(h + 1) * P], pick[:, r * P:(r + 1) * P], attT[:], start=False, stop=True,
                                        skip_group_check=True)
                    return ins
                before_ = f"tmax{t - 1}{half}" if t else ("attT" if half == 0 else "add@1")
                at.step("pe", f"spread{t}{half}", f"attT away {before_}", spread, stage=3)
                at.step("dve", f"tmax{t}{half}", f"spread{t}{half} newm@1", lambda i, j, half=half: dve.tensor_reduce(
                    tmax[:, half * (H // 2):(half + 1) * (H // 2), t], bank[6 + half][:, :].rearrange("p (h e) -> p h e", e=P),
                    AX.X, ALU.max), stage=3)

        def my_block(eng, i):
            return eng.value_load(tb["blk"][0:1, bass.ds(i, 1)], min_val=0, max_val=NB - 1)

        def old_max(i, j):
            return dve.tensor_copy(tmax[:, :, GT], mx[:, bass.ds(my_block(dve, i) * H, H)])

        def keep_max(i, j):
            return dve.tensor_copy(mx[:, bass.ds(my_block(dve, i) * H, H)], newm[:])

        def shift(i, j):
            for t in range(GT):
                ins = pe.matmul(bank[6][:, t * H:(t + 1) * H], oht1[j][:, t * P:(t + 1) * P], newm[:], start=True, stop=True)
            return ins

        def sum1(i, j):
            for t in range(GT):
                ins = pe.matmul(bank[7][:, 0:AW], oh[:, t, :], msg1[:, t, :], start=t == 0, stop=t == GT - 1)
            return ins

        def rescale(i, j):
            a = acc[:, bass.ds(my_block(dve, i) * AW, AW - 1)].rearrange("p (h d) -> p h d", h=H)
            return dve.tensor_tensor(a, a, drop[:].unsqueeze(2).broadcast_to([P, H, HD + 1]), ALU.mult)

        def add1(i, j):
            a = acc[:, bass.ds(my_block(dve, i) * AW, AW)]
            return dve.tensor_tensor(a, a, bank[7][:, 0:AW], ALU.add)

        split_steps()
        at.step("dve", "oht", "keys qloc@2 shift@2", lambda i, j: dve.tensor_scalar(
            oht1[j][:], kr[j][:, 0:GE], lane[:, 0:1], None, ALU.is_equal), stage=2)
        at.step("dve", "oh", "sum@1", lambda i, j: dve.tensor_tensor(
            oh[:, 0:GT, :], node_iota[:].unsqueeze(1).broadcast_to([P, GT, P]),
            tb["key"][:, bass.ds(i * GT, GT)].unsqueeze(2).broadcast_to([P, GT, P]), ALU.is_equal), stage=4)
        turn_steps(0)
        at.step("pe", "attr", "lo attT@1 less@1", lambda i, j: pe.transpose(
            bank[6].bitcast(BF16)[0:3 * GT * H, 0:P], parts[:], identb[:]), stage=3, apart=True)
        at.step("act", "attT", "attr spread31@1", lambda i, j: act.copy(attT[:], bank[6].bitcast(BF16)[0:3 * GT * H, 0:P]), stage=3)
        at.step("pe", "qloc", "oht att3@1", q_local, stage=2, apart=True)
        at.step("pe", "sum", "msg exs oh", sum1, stage=4)
        at.step("dve", "resc", "dropx add@1", rescale, stage=4, apart=True)
        at.step("dve", "add", "resc sum", add1, stage=4, apart=True)
        at.step("dve", "away", "oht", lambda i, j: dve.tensor_scalar(
            away[j][:], oht1[j][:], 1.0, BIG, ALU.subtract, ALU.mult), stage=2)
        main_steps(0)
        turn_steps(1)
        max_tile(0)
        second_steps(0)
        outer_step(0)
        main_steps(1)
        kv_steps(0)
        turn_steps(2)
        max_tile(1)
        second_steps(1)
        outer_step(1)
        main_steps(2)
        kv_steps(1)
        turn_steps(3)
        max_tile(2)
        second_steps(2)
        outer_step(2)
        max_tile(3)
        main_steps(3)
        at.step("dve", "oldm", "newm@1 keepm@1", old_max, stage=3, apart=True)
        at.step("dve", "newm", "oldm tmax30 tmax31 shift@1", lambda i, j: dve.tensor_reduce(newm[:], tmax[:], AX.X, ALU.max), stage=3)
        at.step("dve", "keepm", "newm", keep_max, stage=3, apart=True)
        at.step("dve", "dropd", "newm dropx@1 resc@1", lambda i, j: dve.tensor_tensor(drop[:], tmax[:, :, GT], newm[:], ALU.subtract), stage=3)
        at.step("act", "dropx", "dropd", lambda i, j: act.activation(drop[:], drop[:], ACT.Exp), stage=3)
        kv_steps(2)
        at.step("pe", "shift", "newm tmax30", shift, stage=3)
        second_steps(3)
        at.step("dve", "less", "shift exp@1 msg@1", lambda i, j: dve.tensor_tensor(ex[:], att[j][:], bank[6][:, 0:GT * H], ALU.subtract), stage=3)
        at.step("act", "exp", "less", lambda i, j: act.activation(ex[:], ex[:], ACT.Exp), stage=3)
        outer_step(3)
        at.step("act", "edge", "rows turn3@2", lambda i, j: act.copy(xa[j][:, :, S * D:KC * P], gf[j][:, :, 0:D]), stage=1)
        at.step("sp", "keepf", "rows", lambda i, j: [sp.dma_start(
            slot_feat[:, bass.ds(i * (GT * AP), GT * AP)].rearrange("p (t f) -> p t f", f=AP), gf[j][:, :, D:D + AP])], dma=1, stage=1)
        ex_b = ex[:].rearrange("p (t h) -> p t h", h=H)

        def messages(i, j, t):
            return dve.tensor_tensor(
                msg1[:, t, 0:H * (HD + 1)].rearrange("p (h d) -> p h d", h=H)[:, :, 0:HD],
                kv[j][:, t, H * HD:OKV].rearrange("p (h d) -> p h d", h=H),
                ex_b[:, t, :].unsqueeze(2).broadcast_to([P, H, HD]), ALU.mult)
        for t in range(GT):
            at.step("dve", "msg" if t == GT - 1 else f"msg_{t}", "exp sum@1", lambda i, j, t=t: messages(i, j, t), stage=3)
        at.step("dve", "exs", "exp sum@1", lambda i, j: dve.tensor_copy(
            msg1[:, :, 0:H * (HD + 1)].rearrange("p t (h d) -> p t h d", h=H)[:, :, :, HD], ex_b), stage=3)
        kv_steps(3)
        run(E, at)
        loop1.close()

        att_o = t1("att_o", [P, NB, D])
        den = t1("den", [P, CH * H])
        upd, updT = hcur, z1T
        av = acc[:].rearrange("p (b w) -> p b w", w=AW)
        ph = Phase(1)
        ph.step("dve", "deg", "", lambda i, j: dve.tensor_copy(deg[:], av[:, :, AW - 1]))
        run(E, ph)

        def chunk_acc(i):
            return acc[:, bass.ds(i * CH * AW, CH * AW)].rearrange("p (b w) -> p b w", w=AW)[:, :, 0:AW - 1].rearrange(
                "p b (h d) -> p b h d", h=H)
        ph = Phase(NB // CH)
        ph.step("dve", "den", "upd@1", lambda i, j: dve.tensor_scalar(
            den[:].rearrange("p (b h) -> p b h", h=H), chunk_acc(i)[:, :, :, HD], 1e-16, None, ALU.add))
        ph.step("dve", "inv", "den", lambda i, j: dve.reciprocal(den[:], den[:]))
        for b in range(CH):
            ph.step("dve", "upd" if b == CH - 1 else f"upd{b}", "inv turn@1", lambda i, j, b=b: dve.tensor_tensor(
                upd[:, b * P:(b + 1) * P].rearrange("p (h d) -> p h d", h=H), chunk_acc(i)[:, b, :, 0:HD],
                den[:, b * H:(b + 1) * H].unsqueeze(2).broadcast_to([P, H, HD]), ALU.mult))
        ph.step("dve", "xcc", "prod@1", lambda i, j: dve.tensor_copy(xcc[:], xT[:, bass.ds(i * CHN, CHN)]))

        def turn_upd(i, j):
            for b in range(CH):
                ins = pe.transpose(PS[:, b * P:(b + 1) * P], upd[:, b * P:(b + 1) * P], ident[:])
            return ins
        ph.step("pe", "turn", "upd updT@1", turn_upd, apart=True)
        ph.step("act", "updT", "turn prod@1", lambda i, j: act.copy(updT[:], PS[:, 0:CHN]))

        def o_prod(i, j):
            for b in range(CH):
                o = bank[2][:, b * D:(b + 1) * D]
                pe.matmul(o, updT[:, b * P:(b + 1) * P], wo1[:], start=True, stop=False)
                ins = pe.matmul(o, xcc[:, b * P:(b + 1) * P], wself[:], start=False, stop=True)
            return ins
        ph.step("pe", "prod", "updT xcc out@1", o_prod)
        ph.step("dve", "out", "prod", lambda i, j: dve.tensor_copy(
            att_o[:, bass.ds(i * CH, CH), :], bank[2][:, 0:CH * D].rearrange("p (b f) -> p b f", f=D)))
        run(E, ph)

        part = t1("part", [P, D])
        mu = t1("mu", [P, D])
        ph = Phase(1)
        across = [P, NB, D]
        by_f = "p b f -> p f b"
        ph.step("dve", "sum", "", lambda i, j: dve.tensor_reduce(part[:], att_o[:].rearrange(by_f), AX.X, ALU.add))
        ph.step("pe", "all", "sum", lambda i, j: pe.matmul(bank[0][:, 0:D], ones[:], part[:], start=True, stop=True))
        ph.step("dve", "mu", "all", lambda i, j: dve.tensor_scalar(mu[:], bank[0][:, 0:D], 1.0 / N, None, ALU.mult))
        ph.step("dve", "center", "mu", lambda i, j: dve.tensor_tensor(
            att_o[:], att_o[:], mu[:].unsqueeze(1).broadcast_to(across), ALU.subtract))
        ph.step("dve", "mask", "center", lambda i, j: dve.tensor_scalar(
            att_o[:, NB - 1, :], att_o[:, NB - 1, :], real[:, 0:1], None, ALU.mult))
        ph.step("dve", "square", "mask", lambda i, j: dve.tensor_tensor(sq[:], att_o[:], att_o[:], ALU.mult))
        ph.step("dve", "sumsq", "square", lambda i, j: dve.tensor_reduce(part[:], sq[:].rearrange(by_f), AX.X, ALU.add))
        ph.step("pe", "allsq", "sumsq", lambda i, j: pe.matmul(bank[1][:, 0:D], ones[:], part[:], start=True, stop=True))
        ph.step("dve", "var", "allsq", lambda i, j: dve.tensor_scalar(part[:], bank[1][:, 0:D], 1.0 / N, 1e-5, ALU.mult, ALU.add))
        ph.step("act", "sd", "var", lambda i, j: act.activation(part[:], part[:], ACT.Sqrt))
        ph.step("dve", "inv", "sd", lambda i, j: dve.reciprocal(part[:], part[:]))
        ph.step("dve", "gain", "inv", lambda i, j: dve.tensor_tensor(part[:], part[:], gamma[:], ALU.mult))
        ph.step("dve", "scale", "gain", lambda i, j: dve.tensor_tensor(
            att_o[:], att_o[:], part[:].unsqueeze(1).broadcast_to(across), ALU.mult))
        ph.step("dve", "beta", "scale", lambda i, j: dve.tensor_tensor(
            att_o[:], att_o[:], beta[:].unsqueeze(1).broadcast_to(across), ALU.add))
        ph.step("dve", "res", "beta", lambda i, j: dve.tensor_tensor(xn[:], xn[:], att_o[:], ALU.add))
        run(E, ph)
        layernorm(xn)
        ctx1.close()
        transpose_nodes(xn, xT)
        w1n = sb("w1n", [D, 2, D])
        w1e = sb("w1e", [P, 4 * D])
        w3a = sb("w3a", [D, D])
        w3b = sb("w3b", [D, D])
        b3 = sb("b3", [P, D])
        xcd = sb("xcd", [D, CHN])
        agc = sb("agc", [D, CHN])
        fe = [sb(f"fe{j}", [P, W, AP]) for j in range(2)]
        feT = sb("feT", [P, 2 * P])

        def weights2(i, j):
            yield sp.dma_start(w1n[:, 1, :], L2_W1[0:D, :])
            yield sp.dma_start(w1n[:, 0, :], L2_W1[D:2 * D, :])
            for k in range(4):
                yield sp.dma_start(w1e[k * AP:k * AP + A, k * D:(k + 1) * D], L2_W1[2 * D:2 * D + A, :])
            yield sp.dma_start(b1[:], rows(L2_b1))
            for k in range(2):
                yield sp.dma_start(w2[k * D:(k + 1) * D, k * D:(k + 1) * D], L2_W2)
            yield sp.dma_start(b2r[:], L2_b2.partition_broadcast(3))
            yield sp.dma_start(w3a[:], L2_W3[0:D, :])
            yield sp.dma_start(w3b[:], L2_W3[D:2 * D, :])
            yield sp.dma_start(b3[:], rows(L2_b3))
        ld = Phase(1)
        ld.step("dve", "w1e", "", lambda i, j: dve.memset(w1e[:], 0.0))
        ld.step("sp", "weights", "w1e", weights2, dma=13)
        split_bias(ld, "weights", b2r[:], b2[:], b2w)
        ld.step("dve", "zero", "", lambda i, j: dve.memset(aggT[:], 0.0))
        run(E, ld)

        nt = Phase(NB // CH)
        nt.step("dve", "xcd", "prod@1", lambda i, j: dve.tensor_copy(xcd[:], xT[:, bass.ds(i * CHN, CHN)]))

        def prod2(i, j):
            for b in range(CH):
                ins = pe.matmul(PS[:, b * P:(b + 1) * P], xcd[:, b * P:(b + 1) * P], w1n[:].rearrange("p k f -> p (k f)"),
                                start=True, stop=True)
            return ins
        nt.step("pe", "prod", "xcd qst@1 ptab@1", prod2)
        nt.step("dve", "ptab", "prod", lambda i, j: dve.tensor_tensor(
            ptab[:, bass.ds(i * CH * D, CH * D)].rearrange("p (b f) -> p b f", f=D), prod_out[:, :, 0, :],
            b1[:].unsqueeze(1).broadcast_to([P, CH, D]), ALU.add))
        nt.step("act", "qst", "ptab store@1", lambda i, j: act.copy(qst[:], prod_out[:, :, 1, :]))
        nt.step("sp", "store", "qst", lambda i, j: [sp.dma_start(
            xr[bass.ds(i * CHN, CHN), :].rearrange("(b p) f -> p b f", p=P), qst[:])], dma=1)
        run(E, nt)

        def turn_edge(i, j):
            for c_ in range(2):
                ins = pe.transpose(bank[4][:, c_ * P:(c_ + 1) * P],
                                   fe[j][:, c_ * 4:(c_ + 1) * 4, :].rearrange("p t f -> p (t f)"), ident[:])
            return ins

        def local2(i, j):
            bl = blocks(pe, tb, i)
            for c_ in range(2):
                pe.matmul(bank[0][:, c_ * 4 * D:(c_ + 1) * 4 * D], feT[:, c_ * P:(c_ + 1) * P], w1e[:],
                          start=c_ == 0, stop=True, skip_group_check=True)
            for t in range(W):
                ins = pe.matmul(bank[0][:, t * D:(t + 1) * D], oht[:, t * P:(t + 1) * P],
                                ptab[:, bass.ds(bl[t // GT] * D, D)], start=False, stop=True, skip_group_check=True)
            return ins

        def feature_steps(ph):
            ph.step("sp", "feat", "turne@2", lambda i, j: [sp.dma_start(
                fe[j][:].rearrange("p t f -> p (t f)"), slot_feat[:, bass.ds(i * (W * AP), W * AP)])], dma=1)
            ph.step("pe", "turne", "feat feT@1", turn_edge, stage=1, apart=True)
            ph.step("act", "feT", "turne local@1", lambda i, j: act.copy(feT[:], bank[4][:, 0:2 * P]), stage=1)

        eg2 = Phase(G // 2, unroll=2)
        mlp_steps(eg2, tb, lambda ph: ph.step("pe", "local", "oht feT pre@1", local2, stage=1, apart=True), feature_steps)
        run(E, eg2)

        ph = Phase(NB // CH)
        ph.step("dve", "xcd", "prod@1", lambda i, j: dve.tensor_copy(xcd[:], xT[:, bass.ds(i * CHN, CHN)]))
        ph.step("dve", "agc", "prod@1", lambda i, j: dve.tensor_copy(agc[:], aggT[:, bass.ds(i * CHN, CHN)]))

        def prod3(i, j):
            for b in range(CH):
                o = bank[0][:, b * D:(b + 1) * D]
                pe.matmul(o, xcd[:, b * P:(b + 1) * P], w3a[:], start=True, stop=False)
                ins = pe.matmul(o, agc[:, b * P:(b + 1) * P], w3b[:], start=False, stop=True)
            return ins
        ph.step("pe", "prod", "xcd agc bias@1", prod3)
        ph.step("dve", "bias", "prod silu@1 add@1", lambda i, j: dve.tensor_tensor(
            qst[:], bank[0][:, 0:CH * D].rearrange("p (b f) -> p b f", f=D), b3[:].unsqueeze(1).broadcast_to([P, CH, D]), ALU.add))
        ph.step("act", "silu", "bias", lambda i, j: act.activation(qst[:], qst[:], ACT.Silu))

        def x_plus(i, j):
            s_ = xn[:, bass.ds(i * CH, CH), :]
            return dve.tensor_tensor(s_, s_, qst[:], ALU.add)
        ph.step("dve", "add", "silu", x_plus)
        run(E, ph)
        layernorm(xn)

        dinv = sb("dinv", [P, NB])
        some = sb("some", [P, NB])
        conv = sb("conv", [P, NB * D])
        cv3 = conv[:].rearrange("p (b f) -> p b f", f=D)
        dinv_b = dinv[:].unsqueeze(2).broadcast_to([P, NB, D])
        ph = Phase(1)
        ph.step("dve", "some", "", lambda i, j: dve.tensor_scalar(some[:], deg[:], 0.0, None, ALU.is_gt))
        ph.step("dve", "least", "", lambda i, j: dve.tensor_scalar(dinv[:], deg[:], 1.0, None, ALU.max))
        ph.step("act", "root", "least", lambda i, j: act.activation(dinv[:], dinv[:], ACT.Sqrt))
        ph.step("dve", "inv", "root", lambda i, j: dve.reciprocal(dinv[:], dinv[:]))
        ph.step("dve", "dinv", "inv some", lambda i, j: dve.tensor_tensor(dinv[:], dinv[:], some[:], ALU.mult))
        ph.step("dve", "rows", "dinv", lambda i, j: dve.tensor_tensor(sq[:], xn[:], dinv_b, ALU.mult))
        ph.step("sp", "store", "rows", lambda i, j: [sp.dma_start(xr.rearrange("(b p) f -> p b f", p=P), sq[:])], dma=1)
        ph.step("dve", "zero", "", lambda i, j: dve.memset(conv[:], 0.0))
        run(E, ph)

        def sum3(i, j):
            for h in range(2):
                for t in range(h * GT, (h + 1) * GT):
                    ins = pe.matmul(bank[0][:, h * D:(h + 1) * D], oh[:, t, :], gx[j][:, t, :], start=t % GT == 0, stop=t % GT == GT - 1)
            return ins

        def add3(i, j, h):
            b = dve.value_load(tb["blk"][0:1, bass.ds(i * 2 + h, 1)], min_val=0, max_val=NB - 1)
            a = conv[:, bass.ds(b * D, D)]
            return dve.tensor_tensor(a, a, bank[0][:, h * D:(h + 1) * D], ALU.add)
        eg3 = Phase(G // 2, unroll=2)
        eg3.step("dve", "gidx", "rows@2", lambda i, j: dve.tensor_copy(gi[j][:], tb["gidx"][:, bass.ds(i * W, W)]))
        eg3.step("pool", "go", "gidx sum@2", lambda i, j: pool.nop(nofuse=True))
        eg3.step("pool", "rows", "", lambda i, j: [pool.indirect_dma_start(
            gx[j][:, c_, :], None, xr, bass.IndirectOffsetOnAxis(ap=gi[j][:, c_:c_ + 1], axis=0)) for c_ in range(W)], dma=W)
        eg3.step("dve", "oh", "sum@1", lambda i, j: dve.tensor_tensor(
            oh[:], node_iota[:].unsqueeze(1).broadcast_to([P, W, P]),
            tb["key"][:, bass.ds(i * W, W)].unsqueeze(2).broadcast_to([P, W, P]), ALU.is_equal), stage=1)
        eg3.step("pe", "sum", "oh rows add1@1", sum3, stage=1)
        eg3.step("dve", "add0", "sum add1@1", lambda i, j: add3(i, j, 0), stage=1, apart=True)
        eg3.step("dve", "add1", "add0", lambda i, j: add3(i, j, 1), stage=1, apart=True)
        run(E, eg3)

        ph = Phase(1)
        ph.step("dve", "scale", "", lambda i, j: dve.tensor_tensor(cv3, cv3, dinv_b, ALU.mult))
        ph.step("dve", "res", "scale", lambda i, j: dve.tensor_tensor(xn[:], xn[:], cv3, ALU.add))
        run(E, ph)
        layernorm(xn)

        def result(i, j):
            yield sp.dma_start(out[0:(NB - 1) * P, :].rearrange("(b p) f -> p b f", p=P), xn[:, 0:NB - 1, :])
            yield sp.dma_start(out[(NB - 1) * P:N, :], xn[0:N - (NB - 1) * P, NB - 1, :])
        ph = Phase(1)
        ph.step("sp", "result", "", result, dma=2)
        run(E, ph)


IN = ["x", "src", "dst", "edge_attr_16", "edge_attr_64", "edge_attr_9",
      "L0_gnn_W_in", "L0_gnn_b_in", "L0_gnn_eW1", "L0_gnn_eb1", "L0_gnn_eW2", "L0_gnn_eb2", "L0_gnn_nW1",
      "L0_gnn_nb1", "L0_gnn_nW2", "L0_gnn_nb2", "L0_gnn_W_out", "L0_gnn_b_out", "L1_gnn_Wq", "L1_gnn_Cqk",
      "L1_gnn_Cv", "L1_gnn_k_w1", "L1_gnn_k_b1", "L1_gnn_k_w2", "L1_gnn_k_b2", "L1_gnn_v_w1", "L1_gnn_v_b1",
      "L1_gnn_v_w2", "L1_gnn_v_b2", "L1_gnn_W_out", "L1_gnn_W_self", "L1_gnn_gamma", "L1_gnn_beta",
      "L2_gnn_W1", "L2_gnn_b1", "L2_gnn_W2", "L2_gnn_b2", "L2_gnn_W3", "L2_gnn_b3"]


def kernel(**inputs):
    import numpy as np
    import concourse.bacc as bacc
    from concourse.bass_utils import run_bass_kernel_spmd

    nc = bacc.Bacc("TRN2", target_bir_lowering=False, num_devices=1)
    arrays, args = {}, []
    for name in IN:
        a = np.ascontiguousarray(inputs[name])
        arrays["in_" + name] = a
        args.append(nc.dram_tensor("in_" + name, a.shape, mybir.dt.from_np(a.dtype), kind="ExternalInput").ap())
    args.append(nc.dram_tensor("out_0", (N, D), F32, kind="ExternalOutput").ap())
    build(nc, *args)
    r = run_bass_kernel_spmd(nc, [arrays], core_ids=[0])
    return r.results[0]["out_0"]
```

```python
from contextlib import ExitStack

import concourse.bass as bass
from concourse import mybir

ALU = mybir.AluOpType
ACT = mybir.ActivationFunctionType
AX = mybir.AxisListType
F32 = mybir.dt.float32
BF16 = mybir.dt.bfloat16
I32 = mybir.dt.int32

P = 128
N = 3125
NE = 103125
NB = -(-N // P)
NPAD = NB * P
GT = 4
GTS = 4
W = 8


def most_groups(gt):
    n = (NE + NB * (gt * P - 1)) // (gt * P)
    return -(-n // (W // gt)) * (W // gt)


GE = GT * P
G = most_groups(GT)
T = G * GT
EC = -(-NE // P)
ETAIL = NE - (P - 1) * EC
SC = 13
assert EC % SC == 0
D = 64
HID = 128
LAYERS = 4
CH = 5
CHN = CH * P
HALF = CHN // 2
BIG = 1.0e30
REC = 4
NOKEY = 255


class Engines:

    def __init__(self, nc, ctx):
        self.nc, self.ctx = nc, ctx
        self.eng = {"pe": nc.tensor, "dve": nc.vector, "act": nc.scalar, "pool": nc.gpsimd, "sp": nc.sync}
        self.sem, self.count = {}, {}
        for n in ("pe", "dve", "act", "pool"):
            self.semaphore(n)

    def semaphore(self, name):
        if name not in self.sem:
            self.sem[name] = self.ctx.enter_context(self.nc.semaphore("s_" + name))
            self.count[name] = 0
        return self.sem[name]


class Phase:

    def __init__(self, n, unroll=1, lead=None):
        self.n, self.unroll, self.steps, self.lead, self.late = n, unroll, [], lead, ()

    def step(self, eng, name, waits, fn, stage=0, dma=0, apart=False):
        self.steps.append((eng, name, waits.split(), fn, stage, dma, apart))

    def counts(self):
        turns = self.n + max(s[4] for s in self.steps)
        out = {}
        for eng, name, _, _, _, dma, _ in self.steps:
            if dma:
                for j in range(self.unroll):
                    key = f"{name}_{j}" if self.unroll > 1 else name
                    out[key] = out.get(key, 0) + 16 * dma * len(range(j, self.n, self.unroll))
            else:
                out[eng] = out.get(eng, 0) + turns
        return out

    def emit(self, E, base):
        nc, U = E.nc, self.unroll
        depth = max(s[4] for s in self.steps)
        lags = [int(w.split("@")[1]) for s in self.steps for w in s[2] if "@" in w]
        where, per = {}, {}
        for eng, name, _, _, stage, dma, _ in self.steps:
            if not dma:
                per[eng] = per.get(eng, 0) + 1
            where[name] = (eng, per.get(eng), stage, dma)
        for key in self.counts():
            E.semaphore(key)

        def turn(t, j0, static):
            for eng, name, waits, fn, stage, dma, apart in self.steps:
                e = E.eng[eng]
                if static and not 0 <= t - stage < self.n:
                    if not dma:
                        e.nop(nofuse=True)
                        e.drain().then_inc(E.sem[eng], 1)
                    continue
                need = {}
                for w in waits:
                    src, lag = (w.split("@") + ["0"])[:2]
                    weng, k, wstage, wdma = where[src]
                    lag = int(lag)
                    if static and t - stage - lag < 0:
                        continue
                    back = stage + lag
                    if wdma:
                        jj = (j0 - back) % U
                        key = f"{src}_{jj}" if U > 1 else src
                        if static:
                            val = (t - back) // U + 1
                        else:
                            val = t[0] + (j0 - back) // U + 1
                        need[key] = (wdma, val)
                    else:
                        d = k - (back - wstage) * per[weng]
                        if weng not in need or need[weng] < d:
                            need[weng] = d
                for key, v in need.items():
                    if key in per:
                        tt = t if static else (t[0] * U + j0)
                        e.wait_ge(E.sem[key], base[key] + tt * per[key] + v)
                        if eng == "sp":
                            e.nop(nofuse=True)
                    else:
                        e.wait_ge(E.sem[key], base[key] + v[1] * (16 * v[0]))
                        if eng == "sp":
                            e.nop(nofuse=True)
                if apart and need:
                    e.nop(nofuse=True)
                jb = (j0 - stage) % U
                i = (t - stage) if static else (t[0] * U + (j0 - stage))
                if dma:
                    key = f"{name}_{jb}" if U > 1 else name
                    sem = E.sem[key]
                    for ins in fn(i, jb):
                        ins.then_inc(sem, 16)
                else:
                    fn(i, jb).then_inc(E.sem[eng], 1)

        turns = self.n + depth
        lead = max([depth] + [g + depth for g in lags]) if self.lead is None else self.lead
        lead = -(-lead // U) * U
        loops = max(0, (self.n - lead) // U)
        if loops < 2:
            lead, loops = turns, 0
        for t in range(min(lead, turns)):
            turn(t, t % U, True)
        if loops:
            used = [e.engine for e in (E.eng[n] for n in dict.fromkeys(s[0] for s in self.steps))]
            with nc.Fori(lead // U, lead // U + loops, engines=tuple(used)) as r:
                for j in range(U):
                    turn((r,), j, False)
            for t in range(lead + loops * U, turns):
                turn(t, t % U, True)


def finish(E, phase, base):
    for key, n in phase.counts().items():
        base[key] = base[key] + n
    settle(E, [key for key in phase.counts() if key not in phase.late], base)


def settle(E, keys, base):
    for eng, e in E.eng.items():
        for key in keys:
            e.wait_ge(E.sem[key], base[key])
            if eng == "sp":
                e.nop(nofuse=True)


def run(E, phase):
    for key in phase.counts():
        E.semaphore(key)
    phase.emit(E, E.count)
    finish(E, phase, E.count)


def run_layers(E, phases, n):
    total = {}
    for ph in phases:
        for key, c in ph.counts().items():
            E.semaphore(key)
            total[key] = total.get(key, 0) + c
    with E.nc.Fori(0, n) as layer:
        for ph in phases:
            ph.layer = layer
        base = {k: E.count[k] + layer * total[k] if k in total else v for k, v in E.count.items()}
        for ph in phases:
            ph.emit(E, base)
            finish(E, ph, base)
    for k, c in total.items():
        E.count[k] += n * c



def build(nc, x_in, src_in, dst_in, ea16, ea64, ea9, L0_W_in, L0_b_in, L0_eW1, L0_eb1, L0_eW2, L0_eb2, L0_nW1,
          L0_nb1, L0_nW2, L0_nb2, L0_W_out, L0_b_out, L1_Wq, L1_Cqk, L1_Cv, L1_k_w1, L1_k_b1, L1_k_w2, L1_k_b2,
          L1_v_w1, L1_v_b1, L1_v_w2, L1_v_b2, L1_W_out, L1_W_self, L1_gamma, L1_beta, L2_W1, L2_b1, L2_W2, L2_b2,
          L2_W3, L2_b3, out, dbg=None):
    with ExitStack() as ctx:
        E = Engines(nc, ctx)

        def sb(name, shape, dt=F32):
            return ctx.enter_context(nc.sbuf_tensor(name, shape, dt))

        def dram(name, shape, dt=F32):
            return nc.dram_tensor(name, shape, dt, kind="Internal").ap()

        PS = ctx.enter_context(nc.psum_tensor("psum", [P, 8 * 512], F32))
        bank = [PS[:, b * 512:(b + 1) * 512] for b in range(8)]
        pe, dve, act, pool, sp = nc.tensor, nc.vector, nc.scalar, nc.gpsimd, nc.sync

        def rows(ap):
            return ap.partition_broadcast(P)

        def col(ap):
            return ap.rearrange("(p a) -> p a", a=1)

        ident = sb("ident", [P, P])
        lane = sb("lane", [P, 1])
        node_iota = sb("node_iota", [P, P])
        ones = sb("ones", [P, P])
        before = sb("before", [P, P])
        real = sb("real", [P, 1])
        c = Phase(1)
        c.step("pool", "iota_n", "", lambda i, j: pool.iota(node_iota[:], [[1, P]], base=0, channel_multiplier=0,
                                                            allow_small_or_imprecise_dtypes=True))
        c.step("pool", "iota_p", "", lambda i, j: pool.iota(lane[:], [[0, 1]], base=0, channel_multiplier=1,
                                                            allow_small_or_imprecise_dtypes=True))
        c.step("dve", "ones", "", lambda i, j: dve.memset(ones[:], 1.0))
        c.step("dve", "ident", "iota_n iota_p", lambda i, j: dve.tensor_scalar(ident[:], node_iota[:], lane[:, 0:1], None, ALU.is_equal))
        c.step("dve", "before", "", lambda i, j: dve.tensor_scalar(before[:], node_iota[:], lane[:, 0:1], None, ALU.is_gt))
        c.step("dve", "real", "", lambda i, j: dve.tensor_scalar(real[:], lane[:], float(N - (NB - 1) * P), None, ALU.is_lt))
        onesb = sb("onesb", [3, P], BF16)
        c.step("dve", "onesb", "", lambda i, j: dve.memset(onesb[:], 1.0))
        is_part = sb("is_part", [3, 3])
        c.step("dve", "is_part", "ident", lambda i, j: dve.tensor_copy(is_part[:], ident[0:3, 0:3]))
        run(E, c)

        def split_bias(ph, after, row3, parts3, work):
            hi, mid, low, left = work
            ph.step("dve", "b_hi", after, lambda i, j: dve.tensor_copy(hi, row3))
            ph.step("dve", "b_left", "b_hi", lambda i, j: dve.tensor_tensor(left, row3, hi, ALU.subtract))
            ph.step("dve", "b_mid", "b_left", lambda i, j: dve.tensor_copy(mid, left))
            ph.step("dve", "b_low", "b_mid", lambda i, j: dve.tensor_tensor(low, left, mid, ALU.subtract))
            ph.step("dve", "b_1", "b_low", lambda i, j: dve.tensor_scalar(left, hi, is_part[:, 0:1], None, ALU.mult))
            ph.step("dve", "b_2", "b_1", lambda i, j: dve.scalar_tensor_tensor(left, mid, is_part[:, 1:2], left, ALU.mult, ALU.add))
            ph.step("dve", "b_3", "b_2", lambda i, j: dve.scalar_tensor_tensor(parts3, low, is_part[:, 2:3], left, ALU.mult, ALU.add))

        def split_work(name, n_, alloc):
            return (alloc(name + "_hi", [3, n_], BF16)[:], alloc(name + "_mid", [3, n_], BF16)[:],
                    alloc(name + "_low", [3, n_])[:], alloc(name + "_left", [3, n_])[:])

        A, S = 16, 9
        H, HD = 8, 16
        OKV = 2 * H * HD
        FW = A + S
        feat = dram("feat", [NE, FW])
        wtab = dram("wtab", [NE, OKV])
        cat = Phase(1)

        def concat(i, j):
            yield act.dma_start(feat[:, 0:A], ea16)
            yield act.dma_start(feat[:, A:FW], ea9)
        cat.step("act", "concat", "", concat, dma=2)
        cat.late = ("concat",)
        run(E, cat)

        tables = {}
        for order in "sd":
            gt_ = GTS if order == "s" else GT
            g_ = most_groups(gt_)
            t_ = g_ * gt_
            tables[order] = dict(
                gt=gt_, per_turn=W // gt_, groups=g_, tiles=t_, gcols=-(-g_ // P),
                slots=dram(f"slots_{order}", [t_ * P, REC], I32),
                keyrow=dram(f"keyrow_{order}", [t_ * P], BF16),
                gidx=sb(f"gidx_{order}", [P, t_], I32),
                key=sb(f"key_{order}", [P, t_]),
                blk=sb(f"blk_{order}", [1, -(-g_ // P) * P], I32))
        eid = sb("eid", [P, T], I32)

        with ExitStack() as pre:
            def tmp(name, shape, dt=F32):
                return pre.enter_context(nc.sbuf_tensor(name, shape, dt))

            src = tmp("src", [P, EC], I32)
            dst = tmp("dst", [P, EC], I32)
            bucket = tmp("bucket", [P, EC])
            member = tmp("member", [P, EC])
            onesw = tmp("onesw", [P, EC])
            rank = tmp("rank", [P, EC])
            pos = tmp("pos", [P, EC])
            ibuf = tmp("ibuf", [P, EC], I32)
            row = tmp("row", [P, EC], I32)
            rec = tmp("rec", [P, T, REC], I32)
            cnt = tmp("cnt", [P, NB])
            first = tmp("first", [P, NB])
            itot = tmp("itot", [P, NB], I32)
            ngr = tmp("ngr", [P, NB])
            gend = tmp("gend", [P, NB])
            hit = tmp("hit", [P, 4, NB])
            gb = tmp("gb", [P, 4])
            gcol = tmp("gcol", [P, 4])
            sidx = [tmp(f"sidx{j}", [P, SC], I32) for j in range(2)]
            srec = [tmp(f"srec{j}", [P, SC * REC], I32) for j in range(2)]
            keyt = tmp("keyt", [P, 8 * P], BF16)

            EW = -(-NE // (2 * (EC // SC) * P))
            kvw1 = tmp("kvw1", [D, 2 * D])
            kvb1 = tmp("kvb1", [P, 1])
            kvw2 = tmp("kvw2", [P, OKV])
            kvb2r = tmp("kvb2r", [3, OKV])
            kvb2 = tmp("kvb2", [3, OKV], BF16)
            kvb2w = split_work("kvb2w", OKV, tmp)
            ein = [tmp(f"ein{j}", [P, EW * D]) for j in range(2)]
            einT = tmp("einT", [D, EW * P])
            ehid = tmp("ehid", [P, EW * P])
            eo = [tmp(f"eo{j}", [P, EW * OKV]) for j in range(2)]
            EH = EW * P // 2

            def factor_weights(i, j):
                yield sp.dma_start(kvw1[:, 0:D], L1_k_w1)
                yield sp.dma_start(kvw1[:, D:2 * D], L1_v_w1)
                yield sp.dma_start(kvb1[0:D, :], col(L1_k_b1))
                yield sp.dma_start(kvb1[D:P, :], col(L1_v_b1))
                yield sp.dma_start(kvw2[0:D, 0:128], L1_k_w2)
                yield sp.dma_start(kvw2[D:P, 128:256], L1_v_w2)
                yield sp.dma_start(kvb2r[:, 0:128], L1_k_b2.partition_broadcast(3))
                yield sp.dma_start(kvb2r[:, 128:256], L1_v_b2.partition_broadcast(3))

            def factor_steps(ph, base):
                def edges(table, i):
                    return table[bass.ds(base + i * (EW * P), EW * P), :].rearrange("(p t) f -> p (t f)", t=EW)

                def second(i, j):
                    for t in range(EW):
                        o = PS[:, 4 * 512 + t * OKV:4 * 512 + (t + 1) * OKV]
                        pe.matmul(o, onesb[:], kvb2[:], start=True, stop=False)
                        ins = pe.matmul(o, ehid[:, t * P:(t + 1) * P], kvw2[:], start=False, stop=True)
                    return ins

                def turn(i, j):
                    for t in range(EW):
                        ins = pe.transpose(PS[0:D, t * P:(t + 1) * P], ein[j][:, t * D:(t + 1) * D], ident[:])
                    return ins

                def first_(i, j):
                    for k in range(2):
                        ins = pe.matmul(bank[2 + k][:, 0:EH], kvw1[:], einT[:, k * EH:(k + 1) * EH], start=True, stop=True)
                    return ins
                ph.step("sp", "e_load", "e_turn@2", lambda i, j: [sp.dma_start(ein[j][:], edges(ea64, i))], dma=1)
                ph.step("pe", "e_second", "e_relu e_out@1", second, stage=2)
                ph.step("act", "e_out", "e_second e_store@2", lambda i, j: act.copy(
                    eo[j][:], PS[:, 4 * 512:4 * 512 + EW * OKV]), stage=2)
                ph.step("pe", "e_turn", "e_load e_turnT@1", turn, stage=1, apart=True)
                ph.step("act", "e_turnT", "e_turn e_first@1", lambda i, j: act.copy(einT[:], PS[0:D, 0:EW * P]), stage=1)
                ph.step("pe", "e_first", "e_turnT e_relu@1", first_, stage=1)
                ph.step("act", "e_relu", "e_first e_second@1", lambda i, j: act.activation(
                    ehid[:].rearrange("p (k n) -> p k n", k=2),
                    PS[:, 2 * 512:4 * 512].rearrange("p (k n) -> p k n", k=2)[:, :, 0:EH], ACT.Relu, bias=kvb1[:, 0:1]), stage=1)
                ph.step("sp", "e_store", "e_out", lambda i, j: [sp.dma_start(edges(wtab, i), eo[j][:])], dma=1, stage=2)

            ld = Phase(1)
            for t_, in_ in ((src, src_in), (dst, dst_in)):
                def load(i, j, t_=t_, in_=in_):
                    yield sp.dma_start(t_[0:P - 1, :], in_[0:(P - 1) * EC].rearrange("(p c) -> p c", c=EC))
                    yield sp.dma_start(t_[P - 1:P, 0:ETAIL], in_[(P - 1) * EC:NE].rearrange("(a c) -> a c", a=1))
                ld.step("dve", f"empty_{t_.name}", "", lambda i, j, t_=t_: dve.memset(t_[:], NB * P))
                ld.step("sp", f"load_{t_.name}", f"empty_{t_.name}", load, dma=2)
            ld.step("dve", "onesw", "", lambda i, j: dve.memset(onesw[:], 1.0))
            ld.step("dve", "zero", "", lambda i, j: dve.memset(kvw2[:], 0.0))
            ld.step("sp", "weights", "zero", factor_weights, dma=8)
            split_bias(ld, "weights", kvb2r[:], kvb2[:], kvb2w)
            run(E, ld)

            for order, key, other in (("s", src, dst), ("d", dst, src)):
                tb = tables[order]
                Q, ge = tb["tiles"], tb["gt"] * P
                a = Phase(1)
                a.step("dve", "empty", "", lambda i, j: dve.memset(rec[:], 0))
                a.step("dve", "nokey", "empty", lambda i, j: dve.memset(rec[:, :, 1], NOKEY))
                a.step("sp", "fill", "nokey", lambda i, j: [sp.dma_start(
                    tb["slots"].rearrange("(p t) r -> p (t r)", p=P), rec[:, 0:Q, :].rearrange("p t r -> p (t r)"))], dma=1)
                a.step("dve", "shift", "", lambda i, j: dve.tensor_scalar(ibuf[:], key[:], 7, None, ALU.logical_shift_right))
                a.step("dve", "bucket", "shift", lambda i, j: dve.tensor_copy(bucket[:], ibuf[:]))
                a.step("dve", "r_other", "fill", lambda i, j: dve.tensor_copy(rec[:, 0:EC, 0], other[:]))
                a.step("dve", "r_key", "fill", lambda i, j: dve.tensor_scalar(rec[:, 0:EC, 1], key[:], P - 1, None, ALU.bitwise_and))
                a.step("pool", "r_eid", "fill", lambda i, j: pool.iota(rec[:, 0:EC, 2], [[1, EC]], base=0, channel_multiplier=EC))
                a.step("pool", "r_eid2", "", lambda i, j: pool.iota(rec[:, 0:EC, 3], [[1, EC]], base=0, channel_multiplier=EC))
                a.step("dve", "pos0", "", lambda i, j: dve.memset(pos[:], 0.0))
                run(E, a)
                b = Phase(NB)
                b.step("dve", "member", "sum@1", lambda i, j: dve.tensor_scalar(
                    member[:], bucket[:], node_iota[:, bass.ds(i, 1)], None, ALU.is_equal))
                b.step("dve", "sum", "member", lambda i, j: dve.tensor_reduce(
                    cnt[:, bass.ds(i, 1)], member[:], AX.X, ALU.add))
                run(E, b)
                m = Phase(1)
                m.step("pe", "total", "", lambda i, j: pe.matmul(bank[0][:, 0:NB], ones[:], cnt[:], start=True, stop=True))
                m.step("pe", "below", "", lambda i, j: pe.matmul(bank[1][:, 0:NB], before[:], cnt[:], start=True, stop=True))
                m.step("dve", "itot", "total", lambda i, j: dve.tensor_scalar(itot[:], bank[0][:, 0:NB], float(ge - 1), None, ALU.add))
                m.step("dve", "igr", "itot", lambda i, j: dve.tensor_scalar(itot[:], itot[:], ge.bit_length() - 1, None, ALU.logical_shift_right))
                m.step("dve", "ngr", "igr", lambda i, j: dve.tensor_copy(ngr[:], itot[:]))
                m.step("dve", "gend", "ngr", lambda i, j: dve.tensor_tensor_scan(gend[:], ones[:, 0:NB], ngr[:], 0.0, ALU.mult, ALU.add))
                m.step("dve", "gbeg", "gend", lambda i, j: dve.tensor_tensor(first[:], gend[:], ngr[:], ALU.subtract))
                m.step("dve", "gslot", "gbeg", lambda i, j: dve.tensor_scalar(first[:], first[:], float(ge), -1.0, ALU.mult, ALU.add))
                m.step("dve", "first", "gslot below", lambda i, j: dve.tensor_tensor(first[:], first[:], bank[1][:, 0:NB], ALU.add))
                m.step("pool", "gcol", "", lambda i, j: pool.iota(gcol[:], [[P, 4]], base=0, channel_multiplier=1,
                                                                  allow_small_or_imprecise_dtypes=True))
                for h in range(tb["gcols"]):
                    m.step("dve", f"hit{h}", "gend gcol", lambda i, j, h=h: dve.tensor_scalar(
                        hit[:, h, :], gend[:], gcol[:, h:h + 1], None, ALU.is_le))
                m.step("dve", "gb", f"hit{tb['gcols'] - 1}", lambda i, j: dve.tensor_reduce(gb[:, 0:tb["gcols"]], hit[:, 0:tb["gcols"], 0:NB - 1], AX.X, ALU.add))
                for h in range(tb["gcols"]):
                    m.step("pe", f"gbrow{h}", "gb", lambda i, j, h=h: pe.matmul(
                        bank[2][0:1, h * P:(h + 1) * P], gb[:, h:h + 1], ident[:], start=True, stop=True))
                m.step("dve", "blk", f"gbrow{tb['gcols'] - 1}", lambda i, j: dve.tensor_copy(tb["blk"][:], bank[2][0:1, 0:tb["gcols"] * P]))
                run(E, m)
                r = Phase(NB)
                r.step("dve", "member", "masked@1", lambda i, j: dve.tensor_scalar(
                    member[:], bucket[:], node_iota[:, bass.ds(i, 1)], None, ALU.is_equal))
                r.step("dve", "scan", "member pos@1", lambda i, j: dve.tensor_tensor_scan(
                    rank[:], onesw[:], member[:], first[:, bass.ds(i, 1)], ALU.mult, ALU.add))
                r.step("dve", "masked", "scan", lambda i, j: dve.tensor_tensor(rank[:], rank[:], member[:], ALU.mult))
                r.step("dve", "pos", "masked", lambda i, j: dve.tensor_tensor(pos[:], pos[:], rank[:], ALU.add))
                run(E, r)
                w = Phase(1)
                w.step("dve", "ipos", "", lambda i, j: dve.tensor_copy(ibuf[:], pos[:]))
                w.step("dve", "ilane", "ipos", lambda i, j: dve.tensor_scalar(row[:], ibuf[:], P - 1, None, ALU.bitwise_and))
                w.step("dve", "itile", "ilane", lambda i, j: dve.tensor_scalar(ibuf[:], ibuf[:], 7, None, ALU.logical_shift_right))
                w.step("dve", "fold", "itile", lambda i, j: dve.scalar_tensor_tensor(
                    rank[:], row[:], float(Q), ibuf[:], ALU.mult, ALU.add))
                w.step("dve", "pad", "", lambda i, j: dve.tensor_scalar(
                    member[:], bucket[:], float(NB), float(2 * Q * P), ALU.is_ge, ALU.mult))
                w.step("dve", "row", "pad fold", lambda i, j: dve.tensor_tensor(row[:], rank[:], member[:], ALU.add))
                run(E, w)

                def scatter(i, j):
                    for c_ in range(SC):
                        yield pool.indirect_dma_start(
                            tb["slots"], bass.IndirectOffsetOnAxis(ap=sidx[j][:, c_:c_ + 1], axis=0),
                            srec[j][:, c_ * REC:(c_ + 1) * REC], None, bounds_check=Q * P - 1, oob_is_err=False)
                s = Phase(EC // SC, unroll=2)
                s.step("dve", "sidx", "scatter@2", lambda i, j: dve.tensor_copy(sidx[j][:], row[:, bass.ds(i * SC, SC)]))
                s.step("dve", "srec", "scatter@2", lambda i, j: dve.tensor_copy(
                    srec[j][:], rec[:, bass.ds(i * SC, SC), :].rearrange("p t r -> p (t r)")))
                s.step("pool", "ready", "sidx srec", lambda i, j: pool.nop(nofuse=True))
                s.step("pool", "scatter", "", scatter, dma=SC)
                factor_steps(s, 0 if order == "s" else NE - (EC // SC) * EW * P)
                run(E, s)

                g = Phase(1)
                g.step("sp", "table", "", lambda i, j: [sp.dma_start(
                    rec[:, 0:Q, :].rearrange("p t r -> p (t r)"), tb["slots"].rearrange("(p t) r -> p (t r)", p=P))], dma=1)
                g.step("dve", "gidx", "table", lambda i, j: dve.tensor_copy(tb["gidx"][:], rec[:, 0:Q, 0]))
                g.step("dve", "key", "table", lambda i, j: dve.tensor_copy(tb["key"][:], rec[:, 0:Q, 1]))
                if order == "d":
                    g.step("dve", "eid", "table", lambda i, j: dve.tensor_copy(eid[:], rec[:, :, 2]))
                run(E, g)
                whole, left = Q // P, Q % P

                def turn_keys(i, j):
                    for h in range(whole):
                        ins = pe.transpose(PS[:, h * P:(h + 1) * P], tb["key"][:, h * P:(h + 1) * P], ident[:])
                    return ins

                def store_keys(i, j):
                    yield sp.dma_start(tb["keyrow"][0:whole * P * P].rearrange("(h t p) -> t h p", t=P, p=P),
                                       keyt[:, 0:whole * P].rearrange("t (h p) -> t h p", p=P))
                    yield sp.dma_start(tb["keyrow"][whole * P * P:Q * P].rearrange("(t p) -> t p", p=P),
                                       keyt[0:left, whole * P:(whole + 1) * P])
                q = Phase(1)
                q.step("pe", "turn", "", turn_keys)
                q.step("pe", "turnl", "", lambda i, j: pe.transpose(
                    bank[2][0:left, 0:P], tb["key"][:, whole * P:Q], ident[:]))
                q.step("dve", "keyt", "turn", lambda i, j: dve.tensor_copy(keyt[:, 0:whole * P], PS[:, 0:whole * P]))
                q.step("dve", "keytl", "turnl", lambda i, j: dve.tensor_copy(keyt[0:left, whole * P:(whole + 1) * P], bank[2][0:left, 0:P]))
                q.step("sp", "store", "keyt keytl", store_keys, dma=2)
                run(E, q)
        xn = sb("xn", [P, NB, D])
        xT = sb("xT", [D, NPAD])
        aggT = sb("aggT", [D, NPAD])
        xc = sb("xc", [P, CH * D])
        xr = dram("xr", [NPAD, D])
        sq = sb("sq", [P, NB, D])
        stat = sb("stat", [P, NB])
        stat2 = sb("stat2", [P, NB])

        def transpose_nodes(src_t, dst_t):
            t = Phase(NB // CH)
            t.step("dve", "copy", "turn@1", lambda i, j: dve.tensor_copy(
                xc[:], src_t[:, bass.ds(i * CH, CH), :].rearrange("p b f -> p (b f)")))

            def turn(i, j):
                for b in range(CH):
                    ins = pe.transpose(PS[0:D, b * P:(b + 1) * P], xc[:, b * D:(b + 1) * D], ident[:])
                return ins
            t.step("pe", "turn", "copy out@1", turn, apart=True)
            t.step("act", "out", "turn", lambda i, j: act.copy(dst_t[:, bass.ds(i * CHN, CHN)], PS[0:D, 0:CHN]))
            run(E, t)

        def layernorm(t, extra=None):
            mean = stat[:].unsqueeze(2).broadcast_to([P, NB, D])
            inv = stat2[:].unsqueeze(2).broadcast_to([P, NB, D])
            n = Phase(1)
            n.step("dve", "sum", "", lambda i, j: dve.tensor_reduce(stat[:], t[:], AX.X, ALU.add))
            n.step("dve", "mean", "sum", lambda i, j: dve.tensor_scalar(stat[:], stat[:], 1.0 / D, None, ALU.mult))
            n.step("dve", "center", "mean", lambda i, j: dve.tensor_tensor(t[:], t[:], mean, ALU.subtract))
            n.step("dve", "square", "center", lambda i, j: dve.tensor_tensor(sq[:], t[:], t[:], ALU.mult))
            n.step("dve", "sumsq", "square", lambda i, j: dve.tensor_reduce(stat2[:], sq[:], AX.X, ALU.add))
            n.step("dve", "var", "sumsq", lambda i, j: dve.tensor_scalar(stat2[:], stat2[:], 1.0 / D, 1e-5, ALU.mult, ALU.add))
            n.step("act", "sd", "var", lambda i, j: act.activation(stat2[:], stat2[:], ACT.Sqrt))
            n.step("dve", "inv", "sd", lambda i, j: dve.reciprocal(stat2[:], stat2[:]))
            n.step("dve", "scale", "inv", lambda i, j: dve.tensor_tensor(t[:], t[:], inv, ALU.mult))
            n.step("dve", "mask", "scale", lambda i, j: dve.tensor_scalar(
                t[:, NB - 1, :], t[:, NB - 1, :], real[:, 0:1], None, ALU.mult))
            run(E, n)

        def load_nodes(i, j):
            yield sp.dma_start(xn[:, 0:NB - 1, :], x_in[0:(NB - 1) * P, :].rearrange("(b p) f -> p b f", p=P))
            yield sp.dma_start(xn[0:N - (NB - 1) * P, NB - 1, :], x_in[(NB - 1) * P:N, :])
        ld = Phase(1)
        ld.step("dve", "zero", "", lambda i, j: dve.memset(xn[:], 0.0))
        ld.step("sp", "nodes", "zero", load_nodes, dma=2)
        run(E, ld)
        transpose_nodes(xn, xT)

        kr = [sb(f"kr{j}", [P, W * P], BF16) for j in range(2)]
        gi = [sb(f"gi{j}", [P, W], I32) for j in range(2)]
        gx = [sb(f"gx{j}", [P, W, D]) for j in range(2)]
        oht = sb("oht", [P, W * P])
        oh = sb("oh", [P, W, P])
        msg = [sb(f"msg{j}", [P, W * D]) for j in range(2)]

        def fetch_steps(ph, tb, table, free):
            ph.step("sp", "keys", "oht@2", lambda i, j: [sp.dma_start(
                kr[j][:], tb["keyrow"][bass.ds(i * (W * P), W * P)].partition_broadcast(P))], dma=1)
            ph.step("dve", "gidx", "rows@2", lambda i, j: dve.tensor_copy(gi[j][:], tb["gidx"][:, bass.ds(i * W, W)]))
            ph.step("pool", "go", f"gidx {free}@2", lambda i, j: pool.nop(nofuse=True))
            ph.step("pool", "rows", "", lambda i, j: [pool.indirect_dma_start(
                gx[j][:, c_, :], None, table, bass.IndirectOffsetOnAxis(ap=gi[j][:, c_:c_ + 1], axis=0)) for c_ in range(W)], dma=W)

        def edge_oh(ph, tb, stage):
            ph.step("dve", "oh", "sum@1", lambda i, j: dve.tensor_tensor(
                oh[:], node_iota[:].unsqueeze(1).broadcast_to([P, W, P]),
                tb["key"][:, bass.ds(i * W, W)].unsqueeze(2).broadcast_to([P, W, P]), ALU.is_equal), stage=stage)

        def node_oh(ph):
            ph.step("dve", "oht", "keys local@1", lambda i, j: dve.tensor_scalar(
                oht[:], kr[j][:], lane[:, 0:1], None, ALU.is_equal), stage=1)

        def blocks(eng, tb, i):
            n = tb["per_turn"]
            b = [eng.value_load(tb["blk"][0:1, bass.ds(i * n + h, 1)], min_val=0, max_val=NB - 1) for h in range(n)]
            return [b[t // tb["gt"]] for t in range(W)]

        def add_messages(ph, tb, src_bank, waits):
            n = tb["per_turn"]

            def add(i, j, h):
                b = dve.value_load(tb["blk"][0:1, bass.ds(i * n + h, 1)], min_val=0, max_val=NB - 1)
                a = aggT[:, bass.ds(b * P, P)]
                return dve.tensor_tensor(a, a, bank[src_bank][0:D, h * P:(h + 1) * P], ALU.add)
            for h in range(n):
                name = "added" if h == n - 1 else f"add{h}"
                ph.step("dve", name, waits + " added@1" if h == 0 else f"add{h - 1}", lambda i, j, h=h: add(i, j, h), stage=3, apart=True)

        tb = tables["s"]
        hT = sb("hT", [HID, NPAD])
        z1T = sb("z1T", [HID, CHN])
        hcur = sb("hcur", [HID, CHN])
        ptab = sb("ptab", [P, NB * D])
        qst = sb("qst", [P, CH, D])
        w_in = sb("w_in", [D, HID])
        b_in = sb("b_in", [HID, 1])
        w_out = sb("w_out", [HID, D])
        b_out = sb("b_out", [P, D])
        w1 = sb("w1", [HID, 2, D])
        b1 = sb("b1", [P, D])
        w2 = sb("w2", [P, P])
        b2r = sb("b2r", [3, D])
        b2 = sb("b2", [3, D], BF16)
        b2w = split_work("b2w", D, sb)
        m1a = sb("m1a", [HID, HID])
        m1b = sb("m1b", [D, HID])
        c1 = sb("c1", [HID, 1])
        m2 = sb("m2", [HID, HID])
        c2 = sb("c2", [HID, 1])
        h1 = sb("h1", [P, W * D])
        pre_s = [sb(f"pre_s{j}", [P, W * D]) for j in range(2)]

        ld = Phase(1)
        ld.step("dve", "zero", "", lambda i, j: dve.memset(w2[:], 0.0))
        ld.step("sp", "win", "", lambda i, j: [sp.dma_start(w_in[:], L0_W_in), sp.dma_start(b_in[:], col(L0_b_in)),
                                               sp.dma_start(w_out[:], L0_W_out), sp.dma_start(b_out[:], rows(L0_b_out))], dma=4)
        run(E, ld)

        def halves(lo):
            return PS[:, lo * 512:(lo + 2) * 512].rearrange("p (k n) -> p k n", k=2)[:, :, 0:HALF]

        ph = Phase(NB // CH)

        def h_in(i, j):
            for k in range(2):
                ins = pe.matmul(bank[k][:, 0:HALF], w_in[:], xT[:, bass.ds(i * CHN + k * HALF, HALF)], start=True, stop=True)
            return ins
        ph.step("pe", "win", "bias@1", h_in)
        ph.step("act", "bias", "win", lambda i, j: act.activation(
            hT[:, bass.ds(i * CHN, CHN)].rearrange("p (k n) -> p k n", k=2), halves(0), ACT.Identity, bias=b_in[:, 0:1]))
        run(E, ph)

        wl = Phase(1)

        def layer_weights(i, j):
            l = wl.layer
            yield sp.dma_start(w1[:], L0_eW1[bass.ds(l, 1), :, :].rearrange("a (k p) f -> p (a k) f", p=P))
            yield sp.dma_start(b1[:], L0_eb1[bass.ds(l, 1), :].rearrange("a f -> (a f)").partition_broadcast(P))
            for k in range(2):
                yield sp.dma_start(w2[k * D:(k + 1) * D, k * D:(k + 1) * D], L0_eW2[bass.ds(l, 1), :, :].rearrange("a p f -> p (a f)"))
            yield sp.dma_start(b2r[:], L0_eb2[bass.ds(l, 1), :].rearrange("a f -> (a f)").partition_broadcast(3))
            yield sp.dma_start(m1a[:], L0_nW1[bass.ds(l, 1), 0:HID, :].rearrange("a p f -> p (a f)"))
            yield sp.dma_start(m1b[:], L0_nW1[bass.ds(l, 1), HID:HID + D, :].rearrange("a p f -> p (a f)"))
            yield sp.dma_start(c1[:], L0_nb1[bass.ds(l, 1), :].rearrange("a (p f) -> p (a f)", f=1))
            yield sp.dma_start(m2[:], L0_nW2[bass.ds(l, 1), :, :].rearrange("a p f -> p (a f)"))
            yield sp.dma_start(c2[:], L0_nb2[bass.ds(l, 1), :].rearrange("a (p f) -> p (a f)", f=1))
        wl.step("sp", "weights", "", layer_weights, dma=10)
        wl.step("dve", "zero", "", lambda i, j: dve.memset(aggT[:], 0.0))
        split_bias(wl, "weights", b2r[:], b2[:], b2w)

        nt = Phase(NB // CH)
        nt.step("dve", "hcur", "prod@1", lambda i, j: dve.tensor_copy(hcur[:], hT[:, bass.ds(i * CHN, CHN)]))

        def prod(i, j):
            for b in range(CH):
                ins = pe.matmul(PS[:, b * P:(b + 1) * P], hcur[:, b * P:(b + 1) * P], w1[:].rearrange("p k f -> p (k f)"),
                                start=True, stop=True)
            return ins
        nt.step("pe", "prod", "hcur qst@1 ptab@1", prod)
        prod_out = PS[:, 0:CHN].rearrange("p (b k f) -> p b k f", b=CH, k=2)
        nt.step("dve", "ptab", "prod", lambda i, j: dve.tensor_tensor(
            ptab[:, bass.ds(i * CH * D, CH * D)].rearrange("p (b f) -> p b f", f=D), prod_out[:, :, 0, :],
            b1[:].unsqueeze(1).broadcast_to([P, CH, D]), ALU.add))
        nt.step("act", "qst", "ptab store@1", lambda i, j: act.copy(qst[:], prod_out[:, :, 1, :]))
        nt.step("sp", "store", "qst", lambda i, j: [sp.dma_start(
            xr[bass.ds(i * CHN, CHN), :].rearrange("(b p) f -> p b f", p=P), qst[:])], dma=1)

        def gather_local(tb, table, width, dst):
            def f(i, j):
                bl = blocks(pe, tb, i)
                for t in range(W):
                    ins = pe.matmul(dst[:, t * width:(t + 1) * width], oht[:, t * P:(t + 1) * P],
                                    table[:, bass.ds(bl[t] * width, width)], start=True, stop=True)
                return ins
            return f

        def turn_pairs(i, j):
            for q in range(GT):
                ins = pe.transpose(bank[1][:, q * P:(q + 1) * P], pre_s[j][:, q * P:(q + 1) * P], ident[:])
            return ins

        def second(i, j):
            pe.matmul(bank[2][:, :], onesb[:], b2[:].unsqueeze(1).broadcast_to([3, W, D]), start=True, stop=True)
            for q in range(GT):
                ins = pe.matmul(bank[2][:, q * P:(q + 1) * P], h1[:, q * P:(q + 1) * P], w2[:], start=False, stop=True,
                                skip_group_check=True)
            return ins

        def sum_messages(tb):
            def f(i, j):
                for t in range(W):
                    h = t // tb["gt"]
                    ins = pe.matmul(bank[3][0:D, h * P:(h + 1) * P], msg[j][:, t * D:(t + 1) * D], oh[:, t, :],
                                    start=t % tb["gt"] == 0, stop=(t + 1) % tb["gt"] == 0)
                return ins
            return f

        def mlp_steps(ph, tb, local_step, feature_steps=None):
            fetch_steps(ph, tb, xr, "pre")
            ph.step("pe", "turn", "pre silu1@1", turn_pairs, stage=2, apart=True)
            ph.step("act", "silu1", "turn second@1", lambda i, j: act.activation(h1[:], bank[1][:, :], ACT.Silu), stage=2)
            edge_oh(ph, tb, 3)
            node_oh(ph)
            if feature_steps:
                feature_steps(ph)
            ph.step("pe", "sum", "silu2 oh added@1", sum_messages(tb), stage=3)
            local_step(ph)
            ph.step("pe", "second", "silu1 silu2@1", second, stage=2)
            ph.step("act", "silu2", "second sum@2", lambda i, j: act.activation(msg[j][:], bank[2][:, :], ACT.Silu), stage=2)
            add_messages(ph, tb, 3, "sum")
            ph.step("dve", "pre", "local rows turn@2", lambda i, j: dve.tensor_tensor(
                pre_s[j][:], bank[0][:, :], gx[j][:, :, :].rearrange("p t f -> p (t f)"), ALU.add), stage=1)

        eg = Phase(tb["tiles"] // W, unroll=2)
        mlp_steps(eg, tb, lambda ph: ph.step("pe", "local", "oht pre@1", gather_local(tb, ptab, D, bank[0]), stage=1, apart=True))

        up = Phase(NB // CH)

        def z1(i, j):
            for k in range(2):
                s_ = bass.ds(i * CHN + k * HALF, HALF)
                pe.matmul(bank[k][:, 0:HALF], m1a[:], hT[:, s_], start=True, stop=False)
                ins = pe.matmul(bank[k][:, 0:HALF], m1b[:], aggT[:, s_], start=False, stop=True)
            return ins

        def z2(i, j):
            for k in range(2):
                ins = pe.matmul(bank[2 + k][:, 0:HALF], m2[:], z1T[:, k * HALF:(k + 1) * HALF], start=True, stop=True)
            return ins
        up.step("pe", "z1", "silu@1", z1)
        up.step("act", "silu", "z1 z2@1", lambda i, j: act.activation(
            z1T[:].rearrange("p (k n) -> p k n", k=2), halves(0), ACT.Silu, bias=c1[:, 0:1]))
        up.step("pe", "z2", "silu h@1", z2)

        def h_new(i, j):
            s_ = hT[:, bass.ds(i * CHN, CHN)].rearrange("p (k n) -> p k n", k=2)
            return dve.scalar_tensor_tensor(s_, halves(2), c2[:, 0:1], s_, ALU.add, ALU.add)
        up.step("dve", "h", "z2", h_new)
        run_layers(E, [wl, nt, eg, up], LAYERS)

        ph = Phase(NB // CH)
        ph.step("dve", "hcur", "prod@1", lambda i, j: dve.tensor_copy(hcur[:], hT[:, bass.ds(i * CHN, CHN)]))

        def h_out(i, j):
            for b in range(CH):
                ins = pe.matmul(bank[0][:, b * D:(b + 1) * D], hcur[:, b * P:(b + 1) * P], w_out[:], start=True, stop=True)
            return ins
        ph.step("pe", "prod", "hcur add@1", h_out)

        def x_add(i, j):
            s_ = xn[:, bass.ds(i * CH, CH), :]
            return dve.tensor_tensor(s_, s_, bank[0][:, 0:CH * D].rearrange("p (b f) -> p b f", f=D), ALU.add)
        ph.step("dve", "add", "prod bias@1", x_add)

        def x_bias(i, j):
            s_ = xn[:, bass.ds(i * CH, CH), :]
            return dve.tensor_tensor(s_, s_, b_out[:].unsqueeze(1).broadcast_to([P, CH, D]), ALU.add)
        ph.step("dve", "bias", "add", x_bias)
        run(E, ph)
        layernorm(xn)
        tb = tables["d"]
        AP = 32
        SD = S * D
        KC = -(-SD // P)
        AW = H * (HD + 1) + 1
        deg = sb("deg", [P, NB])
        slot_feat = dram("slot_feat", [P, T * AP])
        transpose_nodes(xn, xT)
        ctx1 = ctx.enter_context(ExitStack())

        def t1(name, shape, dt=F32):
            return ctx1.enter_context(nc.sbuf_tensor(name, shape, dt))

        wq = t1("wq", [D, H * HD])
        cw = t1("cw", [P, KC, OKV])
        wo1 = t1("wo1", [P, D])
        wself = t1("wself", [D, D])
        gamma = t1("gamma", [P, D])
        beta = t1("beta", [P, D])
        qtab = hT
        acc = t1("acc", [P, NB * AW])
        mx = t1("mx", [P, NB * H])
        identb = t1("identb", [P, P], BF16)
        rowno = t1("rowno", [P, 1])
        PR = 3 * GT * H
        CR = 8 + 16 + 1
        pick = t1("pick", [PR + CR, GT * H * P], BF16)
        code = t1("code", [P, PR + CR], BF16)
        empty1 = t1("empty1", [PR + CR, 1])
        digit = t1("digit", [P, 2], I32)
        digitf = t1("digitf", [P, 2])
        xcc = t1("xcc", [D, CHN])

        def weights1(i, j):
            yield sp.dma_start(wq[:], L1_Wq)
            for half, C in enumerate((L1_Cqk, L1_Cv)):
                o = slice(half * 128, (half + 1) * 128)
                for s in range(S):
                    yield sp.dma_start(cw[(s % 2) * D:(s % 2 + 1) * D, s // 2, o], C[:, s, :])
            yield sp.dma_start(wo1[:], L1_W_out)
            yield sp.dma_start(wself[:], L1_W_self)
            yield sp.dma_start(gamma[:], rows(L1_gamma))
            yield sp.dma_start(beta[:], rows(L1_beta))
            yield sp.dma_start(xr.rearrange("(b p) f -> p b f", p=P), xn[:])
        ld = Phase(1)
        ld.step("dve", "zacc", "", lambda i, j: dve.memset(acc[:], 0.0))
        ld.step("dve", "mx", "", lambda i, j: dve.memset(mx[:], -BIG))
        ld.step("dve", "identb", "", lambda i, j: dve.tensor_copy(identb[:], ident[:]))
        ld.step("dve", "row_a", "", lambda i, j: dve.tensor_scalar(rowno[:], lane[:], 32.0, -32.0, ALU.is_ge, ALU.mult))
        ld.step("dve", "row_b", "row_a", lambda i, j: dve.tensor_scalar(stat[:, 0:1], lane[:], 64.0, -32.0, ALU.is_ge, ALU.mult))
        ld.step("dve", "row_c", "row_b", lambda i, j: dve.tensor_tensor(rowno[:], rowno[:], stat[:, 0:1], ALU.add))
        ld.step("dve", "row_d", "row_c", lambda i, j: dve.tensor_tensor(rowno[:], rowno[:], lane[:], ALU.add))
        ld.step("dve", "pick", "row_d", lambda i, j: dve.tensor_scalar(
            pick[0:PR, :].rearrange("p (r n) -> p r n", n=P), node_iota[0:PR, 0:GT * H].unsqueeze(2).broadcast_to([PR, GT * H, P]),
            rowno[0:PR, 0:1], None, ALU.is_equal))
        ld.step("dve", "digit0", "", lambda i, j: dve.tensor_copy(digit[:, 0:1], lane[:]))
        ld.step("dve", "digit1", "digit0", lambda i, j: dve.tensor_scalar(digit[:, 1:2], digit[:, 0:1], 15, None, ALU.bitwise_and))
        ld.step("dve", "digit2", "digit1", lambda i, j: dve.tensor_scalar(digit[:, 0:1], digit[:, 0:1], 4, None, ALU.logical_shift_right))
        ld.step("dve", "digitf", "digit2", lambda i, j: dve.tensor_copy(digitf[:], digit[:]))
        ld.step("dve", "code0", "", lambda i, j: dve.memset(code[:, 0:PR], 0.0))
        ld.step("dve", "code1", "digitf", lambda i, j: dve.tensor_scalar(
            code[:, PR:PR + 8], node_iota[:, 0:8], digitf[:, 0:1], None, ALU.is_equal))
        ld.step("dve", "code2", "digitf", lambda i, j: dve.tensor_scalar(
            code[:, PR + 8:PR + 24], node_iota[:, 0:16], digitf[:, 1:2], None, ALU.is_equal))
        ld.step("dve", "code3", "", lambda i, j: dve.memset(code[:, PR + 24:PR + CR], -1.0))
        ld.step("dve", "empty1", "", lambda i, j: dve.tensor_scalar(
            empty1[:], lane[0:PR + CR, :], float(PR + CR - 1), None, ALU.is_equal))
        ld.step("pe", "codeT", "code0 code1 code2 code3 identb", lambda i, j: pe.matmul(
            bank[0][0:PR + CR, 0:P], code[:], identb[:], start=True, stop=True))
        ld.step("dve", "other", "codeT", lambda i, j: dve.tensor_scalar(
            pick[PR:PR + CR, :].rearrange("p (r n) -> p r n", n=P),
            bank[0][PR:PR + CR, 0:P].unsqueeze(1).broadcast_to([CR, GT * H, P]), 1.0, BIG, ALU.subtract, ALU.mult))
        ld.step("sp", "weights", "", weights1, dma=1 + 2 * S + 4 + 1)
        run(E, ld)

        ph = Phase(NB // CH)
        ph.step("dve", "xcc", "prod@1", lambda i, j: dve.tensor_copy(xcc[:], xT[:, bass.ds(i * CHN, CHN)]))

        def q_prod(i, j):
            for b in range(CH):
                ins = pe.matmul(PS[:, b * P:(b + 1) * P], xcc[:, b * P:(b + 1) * P], wq[:], start=True, stop=True)
            return ins
        ph.step("pe", "prod", "xcc out@1", q_prod)
        ph.step("act", "out", "prod", lambda i, j: act.copy(qtab[:, bass.ds(i * CHN, CHN)], PS[:, 0:CHN]))
        run(E, ph)

        loop1 = ExitStack()

        def t2(name, shape, dt=F32):
            return loop1.enter_context(nc.sbuf_tensor(name, shape, dt))

        gi1 = [t2(f"gi1{j}", [P, GT], I32) for j in range(2)]
        ei1 = [t2(f"ei1{j}", [P, GT], I32) for j in range(2)]
        gf = [t2(f"gf{j}", [P, GT, AP]) for j in range(2)]
        wkv = [t2(f"wkv{j}", [P, GT, OKV]) for j in range(2)]
        xa = [t2(f"xa{j}", [P, GT, SD]) for j in range(2)]
        oht1 = [t2(f"oht1{j}", [P, GE]) for j in range(2)]
        ohtb = [t2(f"ohtb{j}", [P, GE], BF16) for j in range(2)]
        xt = [t2(f"xt{k}", [P, KC * P]) for k in range(2)]
        kv = [t2(f"kv{j}", [P, GT, OKV]) for j in range(2)]
        qk = t2("qk", [P, H * HD])
        att = [t2(f"att{j}", [P, GT * H]) for j in range(2)]
        rest = t2("rest", [P, GT * H])
        parts = t2("parts", [P, PR + CR], BF16)
        attT = t2("attT", [PR + CR, GE], BF16)
        tmax = t2("tmax", [P, H, GT + 1])
        newm = t2("newm", [P, H])
        drop = t2("drop", [P, H])
        ex = t2("ex", [P, GT * H])
        msg1 = t2("amsg", [P, GT, AW])

        settle(E, ["concat"], E.count)
        c = Phase(1)
        c.step("dve", "parts", "", lambda i, j: dve.memset(parts[:], 0.0))
        c.step("dve", "onecol", "", lambda i, j: dve.memset(msg1[:], 1.0))
        for j_ in range(2):
            c.step("dve", f"gap{j_}", "", lambda i, j, j_=j_: dve.memset(gf[j_][:], 0.0))
        run(E, c)

        at = Phase(G, unroll=2)
        at.step("sp", "keys", "oht@2", lambda i, j: [sp.dma_start(
            kr[j][:, 0:GE], tb["keyrow"][bass.ds(i * GE, GE)].partition_broadcast(P))], dma=1)
        at.step("dve", "gi", "rows@2", lambda i, j: dve.tensor_copy(gi1[j][:], tb["gidx"][:, bass.ds(i * GT, GT)]))
        at.step("dve", "ei", "rows@2 wrows@2", lambda i, j: dve.tensor_copy(ei1[j][:], eid[:, bass.ds(i * GT, GT)]))
        at.step("pool", "go", "gi ei outer3@2 keepf@2", lambda i, j: pool.nop(nofuse=True))

        def fetch1(i, j):
            for t in range(GT):
                yield pool.indirect_dma_start(gx[j][:, t, :], None, xr, bass.IndirectOffsetOnAxis(ap=gi1[j][:, t:t + 1], axis=0))
                yield pool.indirect_dma_start(gf[j][:, t, 0:FW], None, feat, bass.IndirectOffsetOnAxis(ap=ei1[j][:, t:t + 1], axis=0))
        at.step("pool", "rows", "", fetch1, dma=2 * GT)
        at.step("pool", "wgo", "kv3@2", lambda i, j: pool.nop(nofuse=True), stage=1)
        at.step("pool", "wrows", "", lambda i, j: [pool.indirect_dma_start(
            wkv[j][:, t, :], None, wtab, bass.IndirectOffsetOnAxis(ap=ei1[j][:, t:t + 1], axis=0)) for t in range(GT)],
            stage=1, dma=GT)

        def q_local(i, j):
            b = pe.value_load(tb["blk"][0:1, bass.ds(i, 1)], min_val=0, max_val=NB - 1)
            for t in range(GT):
                ins = pe.matmul(bank[5][:, t * P:(t + 1) * P], oht1[j][:, t * P:(t + 1) * P],
                                qtab[:, bass.ds(b * P, P)], start=True, stop=True)
            return ins

        def outer(t):
            return lambda i, j: dve.tensor_tensor(
                xa[j][:, t, :].rearrange("p (s d) -> p s d", d=D),
                gx[j][:, t, :].unsqueeze(1).broadcast_to([P, S, D]),
                gf[j][:, t, A:FW].unsqueeze(2).broadcast_to([P, S, D]), ALU.mult)

        def turn1(t):
            def f(i, j):
                for k in range(KC):
                    n_ = min(P, SD - k * P)
                    ins = pe.transpose(PS[0:n_, k * P:(k + 1) * P], xa[j][:, t, k * P:k * P + n_], ident[:])
                return ins
            return f

        def main1(t):
            def f(i, j):
                for k in range(KC):
                    n_ = min(P, SD - k * P)
                    ins = pe.matmul(bank[2 + t % 2][:, 0:OKV], xt[t % 2][0:n_, k * P:(k + 1) * P], cw[0:n_, k, :],
                                    start=k == 0, stop=k == KC - 1)
                return ins
            return f

        def around(t, name, back):
            return f"{name}{t - back}" if t >= back else f"{name}{t - back + GT}@1"

        def outer_step(t):
            at.step("dve", f"outer{t}", f"rows turn{t}@2", outer(t), stage=1)

        def turn_steps(t, stage=2):
            at.step("pe", f"turn{t}", f"outer{t} {around(t, 'xt', 1)}", turn1(t), stage=stage, apart=True)
            at.step("act", f"xtl{t}", f"turn{t} {around(t, 'main', 2)}", lambda i, j: act.copy(
                xt[t % 2][0:SD % P, (KC - 1) * P:KC * P], PS[0:SD % P, (KC - 1) * P:KC * P]), stage=stage)
            at.step("act", f"xt{t}", f"turn{t} {around(t, 'main', 2)}",
                    lambda i, j: act.copy(xt[t % 2][:, 0:(KC - 1) * P], PS[:, 0:(KC - 1) * P]), stage=stage)

        def main_steps(t):
            at.step("pe", f"main{t}", f"xt{t} {around(t, 'kv', 2)}", main1(t), stage=2)

        def factor_step(t):
            at.step("dve", f"kv{t}", f"main{t} wrows msg@2", lambda i, j: dve.tensor_tensor(
                kv[j][:, t, :], bank[2 + t % 2][:, 0:OKV], wkv[j][:, t, :], ALU.mult), stage=2)

        def logit_steps(t):
            at.step("dve", f"qk{t}", f"kv{t} qloc {around(t, 'att', 1)}", lambda i, j: dve.tensor_tensor(
                qk[:], kv[j][:, t, 0:H * HD], bank[5][:, t * P:(t + 1) * P], ALU.mult), stage=2)
            at.step("dve", f"att{t}", f"qk{t} less@2", lambda i, j: dve.tensor_reduce(
                att[j][:, t * H:(t + 1) * H], qk[:].rearrange("p (h d) -> p h d", d=HD), AX.X, ALU.add), stage=2)

        def kv_steps(t):
            factor_step(t)
            logit_steps(t)

        def split_steps():
            n_ = GT * H
            at.step("dve", "hi", "att3 attr@1", lambda i, j: dve.tensor_copy(parts[:, 0:n_], att[j][:]), stage=3)
            at.step("dve", "rest1", "hi", lambda i, j: dve.tensor_tensor(rest[:], att[j][:], parts[:, 0:n_], ALU.subtract), stage=3)
            at.step("dve", "mid", "rest1", lambda i, j: dve.tensor_copy(parts[:, n_:2 * n_], rest[:]), stage=3)
            at.step("dve", "lo", "mid", lambda i, j: dve.tensor_tensor(parts[:, 2 * n_:3 * n_], rest[:], parts[:, n_:2 * n_], ALU.subtract), stage=3)

        def max_tile(t):
            for half in range(2):
                def spread(i, j, half=half):
                    for h in range(H // 2):
                        r = t * H + half * (H // 2) + h
                        ins = pe.matmul(bank[6 + half][:, h * P:(h + 1) * P], pick[:, r * P:(r + 1) * P],
                                        attT[:, t * P:(t + 1) * P], start=True, stop=True)
                    return ins
                before_ = f"tmax{t - 1}{half}" if t else ("attT" if half == 0 else "add@1")
                at.step("pe", f"spread{t}{half}", f"attT {before_}", spread, stage=3)
                at.step("dve", f"tmax{t}{half}", f"spread{t}{half} newm@1", lambda i, j, half=half: dve.tensor_reduce(
                    tmax[:, half * (H // 2):(half + 1) * (H // 2), t], bank[6 + half][:, :].rearrange("p (h e) -> p h e", e=P),
                    AX.X, ALU.max), stage=3)

        def my_block(eng, i):
            return eng.value_load(tb["blk"][0:1, bass.ds(i, 1)], min_val=0, max_val=NB - 1)

        def old_max(i, j):
            return dve.tensor_copy(tmax[:, :, GT], mx[:, bass.ds(my_block(dve, i) * H, H)])

        def keep_max(i, j):
            return dve.tensor_copy(mx[:, bass.ds(my_block(dve, i) * H, H)], newm[:])

        def shift(i, j):
            for t in range(GT):
                ins = pe.matmul(bank[6][:, t * H:(t + 1) * H], oht1[j][:, t * P:(t + 1) * P], newm[:], start=True, stop=True)
            return ins

        def sum1(i, j):
            for t in range(GT):
                ins = pe.matmul(bank[7][:, 0:AW], oh[:, t, :], msg1[:, t, :], start=t == 0, stop=t == GT - 1)
            return ins

        def rescale(i, j):
            a = acc[:, bass.ds(my_block(dve, i) * AW, AW - 1)].rearrange("p (h d) -> p h d", h=H)
            return dve.tensor_tensor(a, a, drop[:].unsqueeze(2).broadcast_to([P, H, HD + 1]), ALU.mult)

        def add1(i, j):
            a = acc[:, bass.ds(my_block(dve, i) * AW, AW)]
            return dve.tensor_tensor(a, a, bank[7][:, 0:AW], ALU.add)

        split_steps()
        at.step("dve", "ohtb", "keys attr@2", lambda i, j: dve.tensor_scalar(
            ohtb[j][:], kr[j][:, 0:GE], lane[:, 0:1], None, ALU.is_equal), stage=2)
        at.step("dve", "oht", "keys qloc@2 shift@2", lambda i, j: dve.tensor_scalar(
            oht1[j][:], kr[j][:, 0:GE], lane[:, 0:1], None, ALU.is_equal), stage=2)
        at.step("dve", "oh", "sum@1", lambda i, j: dve.tensor_tensor(
            oh[:, 0:GT, :], node_iota[:].unsqueeze(1).broadcast_to([P, GT, P]),
            tb["key"][:, bass.ds(i * GT, GT)].unsqueeze(2).broadcast_to([P, GT, P]), ALU.is_equal), stage=4)
        factor_step(0)
        outer_step(0)
        outer_step(1)
        main_steps(0)
        turn_steps(1)
        main_steps(1)
        def attr(i, j):
            pe.matmul(bank[4][0:PR + CR, :], code[:], ohtb[j][:], start=True, stop=False)
            return pe.matmul(bank[4][0:PR + CR, :], parts[:], identb[:].unsqueeze(1).broadcast_to([P, GT, P]), start=False, stop=True)
        at.step("pe", "attr", "lo ohtb attT@1", attr, stage=3)
        at.step("act", "attT", "attr spread31@1", lambda i, j: act.activation(
            attT[:], bank[4][0:PR + CR, :], ACT.Identity, bias=empty1[:, 0:1]), stage=3)
        at.step("pe", "qloc", "oht att3@1", q_local, stage=2, apart=True)
        logit_steps(0)
        outer_step(2)
        at.step("pe", "sum", "msg exs oh", sum1, stage=4)
        at.step("dve", "resc", "dropx add@1", rescale, stage=4, apart=True)
        at.step("dve", "add", "resc sum", add1, stage=4, apart=True)
        turn_steps(2)
        max_tile(0)
        outer_step(3)
        kv_steps(1)
        main_steps(2)
        max_tile(1)
        turn_steps(3)
        max_tile(2)
        at.step("sp", "keepf", "rows", lambda i, j: [sp.dma_start(
            slot_feat[:, bass.ds(i * (GT * AP), GT * AP)].rearrange("p (t f) -> p t f", f=AP), gf[j][:, :, :])], dma=1, stage=1)
        turn_steps(0, 1)
        max_tile(3)
        at.step("dve", "oldm", "newm@1 keepm@1", old_max, stage=3, apart=True)
        main_steps(3)
        at.step("dve", "newm", "oldm tmax30 tmax31 shift@1", lambda i, j: dve.tensor_reduce(newm[:], tmax[:], AX.X, ALU.max), stage=3)
        at.step("dve", "keepm", "newm", keep_max, stage=3, apart=True)
        at.step("dve", "dropd", "newm dropx@1 resc@1", lambda i, j: dve.tensor_tensor(drop[:], tmax[:, :, GT], newm[:], ALU.subtract), stage=3)
        at.step("act", "dropx", "dropd", lambda i, j: act.activation(drop[:], drop[:], ACT.Exp), stage=3)
        kv_steps(2)
        at.step("pe", "shift", "newm tmax30", shift, stage=3)
        kv_steps(3)
        at.step("dve", "less", "shift exp@1 msg@1", lambda i, j: dve.tensor_tensor(ex[:], att[j][:], bank[6][:, 0:GT * H], ALU.subtract), stage=3)
        at.step("act", "exp", "less", lambda i, j: act.activation(ex[:], ex[:], ACT.Exp), stage=3)
        ex_b = ex[:].rearrange("p (t h) -> p t h", h=H)

        def messages(i, j, t):
            return dve.tensor_tensor(
                msg1[:, t, 0:H * (HD + 1)].rearrange("p (h d) -> p h d", h=H)[:, :, 0:HD],
                kv[j][:, t, H * HD:OKV].rearrange("p (h d) -> p h d", h=H),
                ex_b[:, t, :].unsqueeze(2).broadcast_to([P, H, HD]), ALU.mult)
        for t in range(GT):
            at.step("dve", "msg" if t == GT - 1 else f"msg_{t}", "exp sum@1", lambda i, j, t=t: messages(i, j, t), stage=3)
        at.step("dve", "exs", "exp sum@1", lambda i, j: dve.tensor_copy(
            msg1[:, :, 0:H * (HD + 1)].rearrange("p t (h d) -> p t h d", h=H)[:, :, :, HD], ex_b), stage=3)
        run(E, at)
        loop1.close()

        att_o = t1("att_o", [P, NB, D])
        den = t1("den", [P, CH * H])
        upd, updT = hcur, z1T
        av = acc[:].rearrange("p (b w) -> p b w", w=AW)
        ph = Phase(1)
        ph.step("dve", "deg", "", lambda i, j: dve.tensor_copy(deg[:], av[:, :, AW - 1]))
        run(E, ph)

        def chunk_acc(i):
            return acc[:, bass.ds(i * CH * AW, CH * AW)].rearrange("p (b w) -> p b w", w=AW)[:, :, 0:AW - 1].rearrange(
                "p b (h d) -> p b h d", h=H)
        ph = Phase(NB // CH)
        ph.step("dve", "den", "upd@1", lambda i, j: dve.tensor_scalar(
            den[:].rearrange("p (b h) -> p b h", h=H), chunk_acc(i)[:, :, :, HD], 1e-16, None, ALU.add))
        ph.step("dve", "inv", "den", lambda i, j: dve.reciprocal(den[:], den[:]))
        for b in range(CH):
            ph.step("dve", "upd" if b == CH - 1 else f"upd{b}", "inv turn@1", lambda i, j, b=b: dve.tensor_tensor(
                upd[:, b * P:(b + 1) * P].rearrange("p (h d) -> p h d", h=H), chunk_acc(i)[:, b, :, 0:HD],
                den[:, b * H:(b + 1) * H].unsqueeze(2).broadcast_to([P, H, HD]), ALU.mult))
        ph.step("dve", "xcc", "prod@1", lambda i, j: dve.tensor_copy(xcc[:], xT[:, bass.ds(i * CHN, CHN)]))

        def turn_upd(i, j):
            for b in range(CH):
                ins = pe.transpose(PS[:, b * P:(b + 1) * P], upd[:, b * P:(b + 1) * P], ident[:])
            return ins
        ph.step("pe", "turn", "upd updT@1", turn_upd, apart=True)
        ph.step("act", "updT", "turn prod@1", lambda i, j: act.copy(updT[:], PS[:, 0:CHN]))

        def o_prod(i, j):
            for b in range(CH):
                o = bank[2][:, b * D:(b + 1) * D]
                pe.matmul(o, updT[:, b * P:(b + 1) * P], wo1[:], start=True, stop=False)
                ins = pe.matmul(o, xcc[:, b * P:(b + 1) * P], wself[:], start=False, stop=True)
            return ins
        ph.step("pe", "prod", "updT xcc out@1", o_prod)
        ph.step("dve", "out", "prod", lambda i, j: dve.tensor_copy(
            att_o[:, bass.ds(i * CH, CH), :], bank[2][:, 0:CH * D].rearrange("p (b f) -> p b f", f=D)))
        run(E, ph)

        part = t1("part", [P, D])
        mu = t1("mu", [P, D])
        ph = Phase(1)
        across = [P, NB, D]
        by_f = "p b f -> p f b"
        ph.step("dve", "sum", "", lambda i, j: dve.tensor_reduce(part[:], att_o[:].rearrange(by_f), AX.X, ALU.add))
        ph.step("pe", "all", "sum", lambda i, j: pe.matmul(bank[0][:, 0:D], ones[:], part[:], start=True, stop=True))
        ph.step("dve", "mu", "all", lambda i, j: dve.tensor_scalar(mu[:], bank[0][:, 0:D], 1.0 / N, None, ALU.mult))
        ph.step("dve", "center", "mu", lambda i, j: dve.tensor_tensor(
            att_o[:], att_o[:], mu[:].unsqueeze(1).broadcast_to(across), ALU.subtract))
        ph.step("dve", "mask", "center", lambda i, j: dve.tensor_scalar(
            att_o[:, NB - 1, :], att_o[:, NB - 1, :], real[:, 0:1], None, ALU.mult))
        ph.step("dve", "square", "mask", lambda i, j: dve.tensor_tensor(sq[:], att_o[:], att_o[:], ALU.mult))
        ph.step("dve", "sumsq", "square", lambda i, j: dve.tensor_reduce(part[:], sq[:].rearrange(by_f), AX.X, ALU.add))
        ph.step("pe", "allsq", "sumsq", lambda i, j: pe.matmul(bank[1][:, 0:D], ones[:], part[:], start=True, stop=True))
        ph.step("dve", "var", "allsq", lambda i, j: dve.tensor_scalar(part[:], bank[1][:, 0:D], 1.0 / N, 1e-5, ALU.mult, ALU.add))
        ph.step("act", "sd", "var", lambda i, j: act.activation(part[:], part[:], ACT.Sqrt))
        ph.step("dve", "inv", "sd", lambda i, j: dve.reciprocal(part[:], part[:]))
        ph.step("dve", "gain", "inv", lambda i, j: dve.tensor_tensor(part[:], part[:], gamma[:], ALU.mult))
        ph.step("dve", "scale", "gain", lambda i, j: dve.tensor_tensor(
            att_o[:], att_o[:], part[:].unsqueeze(1).broadcast_to(across), ALU.mult))
        ph.step("dve", "beta", "scale", lambda i, j: dve.tensor_tensor(
            att_o[:], att_o[:], beta[:].unsqueeze(1).broadcast_to(across), ALU.add))
        ph.step("dve", "res", "beta", lambda i, j: dve.tensor_tensor(xn[:], xn[:], att_o[:], ALU.add))
        run(E, ph)
        layernorm(xn)
        ctx1.close()
        transpose_nodes(xn, xT)
        w1n = sb("w1n", [D, 2, D])
        w1e = sb("w1e", [P, 4 * D])
        w3a = sb("w3a", [D, D])
        w3b = sb("w3b", [D, D])
        b3 = sb("b3", [P, D])
        xcd = sb("xcd", [D, CHN])
        agc = sb("agc", [D, CHN])
        fe = [sb(f"fe{j}", [P, W, AP]) for j in range(2)]
        feT = sb("feT", [P, 2 * P])

        def weights2(i, j):
            yield sp.dma_start(w1n[:, 1, :], L2_W1[0:D, :])
            yield sp.dma_start(w1n[:, 0, :], L2_W1[D:2 * D, :])
            for k in range(4):
                yield sp.dma_start(w1e[k * AP:k * AP + A, k * D:(k + 1) * D], L2_W1[2 * D:2 * D + A, :])
            yield sp.dma_start(b1[:], rows(L2_b1))
            for k in range(2):
                yield sp.dma_start(w2[k * D:(k + 1) * D, k * D:(k + 1) * D], L2_W2)
            yield sp.dma_start(b2r[:], L2_b2.partition_broadcast(3))
            yield sp.dma_start(w3a[:], L2_W3[0:D, :])
            yield sp.dma_start(w3b[:], L2_W3[D:2 * D, :])
            yield sp.dma_start(b3[:], rows(L2_b3))
        ld = Phase(1)
        ld.step("dve", "w1e", "", lambda i, j: dve.memset(w1e[:], 0.0))
        ld.step("sp", "weights", "w1e", weights2, dma=13)
        split_bias(ld, "weights", b2r[:], b2[:], b2w)
        ld.step("dve", "zero", "", lambda i, j: dve.memset(aggT[:], 0.0))
        run(E, ld)

        nt = Phase(NB // CH)
        nt.step("dve", "xcd", "prod@1", lambda i, j: dve.tensor_copy(xcd[:], xT[:, bass.ds(i * CHN, CHN)]))

        def prod2(i, j):
            for b in range(CH):
                ins = pe.matmul(PS[:, b * P:(b + 1) * P], xcd[:, b * P:(b + 1) * P], w1n[:].rearrange("p k f -> p (k f)"),
                                start=True, stop=True)
            return ins
        nt.step("pe", "prod", "xcd qst@1 ptab@1", prod2)
        nt.step("dve", "ptab", "prod", lambda i, j: dve.tensor_tensor(
            ptab[:, bass.ds(i * CH * D, CH * D)].rearrange("p (b f) -> p b f", f=D), prod_out[:, :, 0, :],
            b1[:].unsqueeze(1).broadcast_to([P, CH, D]), ALU.add))
        nt.step("act", "qst", "ptab store@1", lambda i, j: act.copy(qst[:], prod_out[:, :, 1, :]))
        nt.step("sp", "store", "qst", lambda i, j: [sp.dma_start(
            xr[bass.ds(i * CHN, CHN), :].rearrange("(b p) f -> p b f", p=P), qst[:])], dma=1)
        run(E, nt)

        def turn_edge(i, j):
            for c_ in range(2):
                ins = pe.transpose(bank[4][:, c_ * P:(c_ + 1) * P],
                                   fe[j][:, c_ * 4:(c_ + 1) * 4, :].rearrange("p t f -> p (t f)"), ident[:])
            return ins

        def local2(i, j):
            bl = blocks(pe, tb, i)
            for c_ in range(2):
                pe.matmul(bank[0][:, c_ * 4 * D:(c_ + 1) * 4 * D], feT[:, c_ * P:(c_ + 1) * P], w1e[:],
                          start=c_ == 0, stop=True, skip_group_check=True)
            for t in range(W):
                ins = pe.matmul(bank[0][:, t * D:(t + 1) * D], oht[:, t * P:(t + 1) * P],
                                ptab[:, bass.ds(bl[t] * D, D)], start=False, stop=True, skip_group_check=True)
            return ins

        def feature_steps(ph):
            ph.step("sp", "feat", "turne@2", lambda i, j: [sp.dma_start(
                fe[j][:].rearrange("p t f -> p (t f)"), slot_feat[:, bass.ds(i * (W * AP), W * AP)])], dma=1)
            ph.step("pe", "turne", "feat feT@1", turn_edge, stage=1, apart=True)
            ph.step("act", "feT", "turne local@1", lambda i, j: act.copy(feT[:], bank[4][:, 0:2 * P]), stage=1)

        eg2 = Phase(tb["tiles"] // W, unroll=2)
        mlp_steps(eg2, tb, lambda ph: ph.step("pe", "local", "oht feT pre@1", local2, stage=1, apart=True), feature_steps)
        run(E, eg2)

        ph = Phase(NB // CH)
        ph.step("dve", "xcd", "prod@1", lambda i, j: dve.tensor_copy(xcd[:], xT[:, bass.ds(i * CHN, CHN)]))
        ph.step("dve", "agc", "prod@1", lambda i, j: dve.tensor_copy(agc[:], aggT[:, bass.ds(i * CHN, CHN)]))

        def prod3(i, j):
            for b in range(CH):
                o = bank[0][:, b * D:(b + 1) * D]
                pe.matmul(o, xcd[:, b * P:(b + 1) * P], w3a[:], start=True, stop=False)
                ins = pe.matmul(o, agc[:, b * P:(b + 1) * P], w3b[:], start=False, stop=True)
            return ins
        ph.step("pe", "prod", "xcd agc bias@1", prod3)
        ph.step("dve", "bias", "prod silu@1 add@1", lambda i, j: dve.tensor_tensor(
            qst[:], bank[0][:, 0:CH * D].rearrange("p (b f) -> p b f", f=D), b3[:].unsqueeze(1).broadcast_to([P, CH, D]), ALU.add))
        ph.step("act", "silu", "bias", lambda i, j: act.activation(qst[:], qst[:], ACT.Silu))

        def x_plus(i, j):
            s_ = xn[:, bass.ds(i * CH, CH), :]
            return dve.tensor_tensor(s_, s_, qst[:], ALU.add)
        ph.step("dve", "add", "silu", x_plus)
        run(E, ph)
        layernorm(xn)

        dinv = sb("dinv", [P, NB])
        some = sb("some", [P, NB])
        conv = sb("conv", [P, NB * D])
        cv3 = conv[:].rearrange("p (b f) -> p b f", f=D)
        dinv_b = dinv[:].unsqueeze(2).broadcast_to([P, NB, D])
        ph = Phase(1)
        ph.step("dve", "some", "", lambda i, j: dve.tensor_scalar(some[:], deg[:], 0.0, None, ALU.is_gt))
        ph.step("dve", "least", "", lambda i, j: dve.tensor_scalar(dinv[:], deg[:], 1.0, None, ALU.max))
        ph.step("act", "root", "least", lambda i, j: act.activation(dinv[:], dinv[:], ACT.Sqrt))
        ph.step("dve", "inv", "root", lambda i, j: dve.reciprocal(dinv[:], dinv[:]))
        ph.step("dve", "dinv", "inv some", lambda i, j: dve.tensor_tensor(dinv[:], dinv[:], some[:], ALU.mult))
        ph.step("dve", "rows", "dinv", lambda i, j: dve.tensor_tensor(sq[:], xn[:], dinv_b, ALU.mult))
        ph.step("sp", "store", "rows", lambda i, j: [sp.dma_start(xr.rearrange("(b p) f -> p b f", p=P), sq[:])], dma=1)
        ph.step("dve", "zero", "", lambda i, j: dve.memset(conv[:], 0.0))
        run(E, ph)

        def sum3(i, j):
            for h in range(2):
                for t in range(h * GT, (h + 1) * GT):
                    ins = pe.matmul(bank[0][:, h * D:(h + 1) * D], oh[:, t, :], gx[j][:, t, :], start=t % GT == 0, stop=t % GT == GT - 1)
            return ins

        def add3(i, j, h):
            b = dve.value_load(tb["blk"][0:1, bass.ds(i * 2 + h, 1)], min_val=0, max_val=NB - 1)
            a = conv[:, bass.ds(b * D, D)]
            return dve.tensor_tensor(a, a, bank[0][:, h * D:(h + 1) * D], ALU.add)
        eg3 = Phase(G // 2, unroll=2)
        eg3.step("dve", "gidx", "rows@2", lambda i, j: dve.tensor_copy(gi[j][:], tb["gidx"][:, bass.ds(i * W, W)]))
        eg3.step("pool", "go", "gidx sum@2", lambda i, j: pool.nop(nofuse=True))
        eg3.step("pool", "rows", "", lambda i, j: [pool.indirect_dma_start(
            gx[j][:, c_, :], None, xr, bass.IndirectOffsetOnAxis(ap=gi[j][:, c_:c_ + 1], axis=0)) for c_ in range(W)], dma=W)
        eg3.step("dve", "oh", "sum@1", lambda i, j: dve.tensor_tensor(
            oh[:], node_iota[:].unsqueeze(1).broadcast_to([P, W, P]),
            tb["key"][:, bass.ds(i * W, W)].unsqueeze(2).broadcast_to([P, W, P]), ALU.is_equal), stage=1)
        eg3.step("pe", "sum", "oh rows add1@1", sum3, stage=1)
        eg3.step("dve", "add0", "sum add1@1", lambda i, j: add3(i, j, 0), stage=1, apart=True)
        eg3.step("dve", "add1", "add0", lambda i, j: add3(i, j, 1), stage=1, apart=True)
        run(E, eg3)

        ph = Phase(1)
        ph.step("dve", "scale", "", lambda i, j: dve.tensor_tensor(cv3, cv3, dinv_b, ALU.mult))
        ph.step("dve", "res", "scale", lambda i, j: dve.tensor_tensor(xn[:], xn[:], cv3, ALU.add))
        run(E, ph)
        layernorm(xn)

        def result(i, j):
            yield sp.dma_start(out[0:(NB - 1) * P, :].rearrange("(b p) f -> p b f", p=P), xn[:, 0:NB - 1, :])
            yield sp.dma_start(out[(NB - 1) * P:N, :], xn[0:N - (NB - 1) * P, NB - 1, :])
        ph = Phase(1)
        ph.step("sp", "result", "", result, dma=2)
        run(E, ph)


IN = ["x", "src", "dst", "edge_attr_16", "edge_attr_64", "edge_attr_9",
      "L0_gnn_W_in", "L0_gnn_b_in", "L0_gnn_eW1", "L0_gnn_eb1", "L0_gnn_eW2", "L0_gnn_eb2", "L0_gnn_nW1",
      "L0_gnn_nb1", "L0_gnn_nW2", "L0_gnn_nb2", "L0_gnn_W_out", "L0_gnn_b_out", "L1_gnn_Wq", "L1_gnn_Cqk",
      "L1_gnn_Cv", "L1_gnn_k_w1", "L1_gnn_k_b1", "L1_gnn_k_w2", "L1_gnn_k_b2", "L1_gnn_v_w1", "L1_gnn_v_b1",
      "L1_gnn_v_w2", "L1_gnn_v_b2", "L1_gnn_W_out", "L1_gnn_W_self", "L1_gnn_gamma", "L1_gnn_beta",
      "L2_gnn_W1", "L2_gnn_b1", "L2_gnn_W2", "L2_gnn_b2", "L2_gnn_W3", "L2_gnn_b3"]


def kernel(**inputs):
    import numpy as np
    import concourse.bacc as bacc
    from concourse.bass_utils import run_bass_kernel_spmd

    nc = bacc.Bacc("TRN2", target_bir_lowering=False, num_devices=1)
    arrays, args = {}, []
    for name in IN:
        a = np.ascontiguousarray(inputs[name])
        arrays["in_" + name] = a
        args.append(nc.dram_tensor("in_" + name, a.shape, mybir.dt.from_np(a.dtype), kind="ExternalInput").ap())
    args.append(nc.dram_tensor("out_0", (N, D), F32, kind="ExternalOutput").ap())
    build(nc, *args)
    r = run_bass_kernel_spmd(nc, [arrays], core_ids=[0])
    return r.results[0]["out_0"]
```
